# Optimizing a Trainium2 kernel written in Bass

```python
import numpy as np
import jax
import jax.numpy as jnp

def _softmax(x, axis=-1):
    return jax.nn.softmax(x, axis=axis)

def _gelu(x):
    return jax.nn.gelu(x, approximate=True)

def _silu(x):
    return jax.nn.silu(x)

def _sigmoid(x):
    return jax.nn.sigmoid(x)

def _layernorm(x, axis=-1, eps=1e-05):
    m = jnp.mean(x, axis=axis, keepdims=True)
    v = jnp.var(x, axis=axis, keepdims=True)
    return (x - m) / jnp.sqrt(v + eps)

def _scatter_add(tgt, idx, src, axis=0):
    return tgt.at[idx].add(src)

def _segment_sum(src, seg, n):
    return jax.ops.segment_sum(src, seg, n)
kernel_name = 'mk_cond_resid_d1_seqx_r4_1c5ae6'

def setup_inputs(seed: int=0):
    np.random.seed(seed)
    _w = jnp.asarray

    def _rec_inputs():
        import jax
        import jax.numpy as jnp
        _rk = jax.random.key(seed)
        x = -5.13e-06 + 0.01765 * jax.random.normal(jax.random.fold_in(_rk, 1), (128, 64, 256), jnp.float32)
        _lenS = 64 - jax.random.randint(jax.random.fold_in(_rk, 7), (128,), 0, max(1, 64 // 4) + 1, jnp.int32)
        _lenS2 = 64 - jax.random.randint(jax.random.fold_in(_rk, 8), (128,), 0, max(1, 64 // 4) + 1, jnp.int32)
        cond_1024 = 0.0061147 + 1.02565 * jax.random.normal(jax.random.fold_in(_rk, 11), (128, 256), jnp.float32)
        return (x, cond_1024)
    x, cond_1024 = _rec_inputs()

    def _L0_cond_setup():
        import math
        import jax, jax.numpy as jnp
        import numpy as np
        EPS = 1e-07
        MAX_TANH_ARG = 1.0 - 1e-05

        def _norm(x):
            return jnp.sqrt(jnp.sum(x * x, axis=-1, keepdims=True)).clip(EPS)

        def logmap0(x):
            n = _norm(x)
            return jnp.arctanh(jnp.clip(n, EPS, MAX_TANH_ARG)) * x / n

        def expmap0(v):
            n = _norm(v)
            return jnp.tanh(n) * v / n

        def mobius_add(x, y):
            x2 = jnp.sum(x * x, -1, keepdims=True)
            y2 = jnp.sum(y * y, -1, keepdims=True)
            xy = jnp.sum(x * y, -1, keepdims=True)
            num = (1 + 2 * xy + y2) * x + (1 - x2) * y
            den = (1 + 2 * xy + x2 * y2).clip(EPS)
            return num / den

        def plin(x, w, b):
            return expmap0(logmap0(x) @ w + b)

        def layer_norm(x, eps=1e-06):
            m = x.mean(-1, keepdims=True)
            v = ((x - m) ** 2).mean(-1, keepdims=True)
            return (x - m) / jnp.sqrt(v + eps)

        def _beta(a, b):
            return math.exp(math.lgamma(a) + math.lgamma(b) - math.lgamma(a + b))
        D, H, FF = (256, 16, 1024)
        HD = D // H
        BETA_N = _beta(D / 2, 0.5)
        BETA_H = _beta(HD / 2, 0.5)

        def _to_heads(p):
            B, S, _ = p.shape
            t = logmap0(p).reshape(B, S, H, HD) * (BETA_H / BETA_N)
            return expmap0(jnp.transpose(t, (0, 2, 1, 3)))

        def _from_heads(ph):
            B, _, S, _ = ph.shape
            t = logmap0(ph) * (BETA_N / BETA_H)
            t = jnp.transpose(t, (0, 2, 1, 3)).reshape(B, S, D)
            return expmap0(t)
        key = jax.random.key(seed)
        ks = jax.random.split(key, 20)
        B, S = (4, 256)
        x = expmap0(0.02 * jax.random.normal(ks[0], (B, S, D), jnp.float32))
        t_emb = jax.random.normal(ks[1], (B, 1, D), jnp.float32)
        g = lambda k, sh: 0.02 * jax.random.normal(k, sh, jnp.float32)
        return {'x': x, 't_emb': t_emb, 'w_q': g(ks[2], (D, D)), 'b_q': jnp.zeros((D,), jnp.float32), 'w_k': g(ks[3], (D, D)), 'b_k': jnp.zeros((D,), jnp.float32), 'w_v': g(ks[4], (D, D)), 'b_v': jnp.zeros((D,), jnp.float32), 'w_o': g(ks[5], (D, D)), 'b_o': jnp.zeros((D,), jnp.float32), 'w_f1': g(ks[6], (D, FF)), 'b_f1': jnp.zeros((FF,), jnp.float32), 'w_f2': g(ks[7], (FF, D)), 'b_f2': jnp.zeros((D,), jnp.float32), 'w_ada': g(ks[8], (D, 6 * D)), 'b_ada': jnp.zeros((6 * D,), jnp.float32)}
    _L0_cond_all = _L0_cond_setup()
    _L0_cond_in = {k: v for k, v in _L0_cond_all.items() if k in ('w_q', 'b_q', 'w_k', 'b_k', 'w_v', 'b_v', 'w_o', 'b_o', 'w_f1', 'b_f1', 'w_f2', 'b_f2', 'w_ada', 'b_ada')}
    del _L0_cond_all
    return {'x': x, 'cond_1024': cond_1024, 'L0_cond_w_q': _L0_cond_in['w_q'], 'L0_cond_b_q': _L0_cond_in['b_q'], 'L0_cond_w_k': _L0_cond_in['w_k'], 'L0_cond_b_k': _L0_cond_in['b_k'], 'L0_cond_w_v': _L0_cond_in['w_v'], 'L0_cond_b_v': _L0_cond_in['b_v'], 'L0_cond_w_o': _L0_cond_in['w_o'], 'L0_cond_b_o': _L0_cond_in['b_o'], 'L0_cond_w_f1': _L0_cond_in['w_f1'], 'L0_cond_b_f1': _L0_cond_in['b_f1'], 'L0_cond_w_f2': _L0_cond_in['w_f2'], 'L0_cond_b_f2': _L0_cond_in['b_f2'], 'L0_cond_w_ada': _L0_cond_in['w_ada'], 'L0_cond_b_ada': _L0_cond_in['b_ada']}

def reference(x, cond_1024, L0_cond_w_q, L0_cond_b_q, L0_cond_w_k, L0_cond_b_k, L0_cond_w_v, L0_cond_b_v, L0_cond_w_o, L0_cond_b_o, L0_cond_w_f1, L0_cond_b_f1, L0_cond_w_f2, L0_cond_b_f2, L0_cond_w_ada, L0_cond_b_ada):
    import jax
    import jax.numpy as jnp

    def _L0_cond_ref(x, t_emb, w_q, b_q, w_k, b_k, w_v, b_v, w_o, b_o, w_f1, b_f1, w_f2, b_f2, w_ada, b_ada):
        import math
        import jax, jax.numpy as jnp
        import numpy as np
        EPS = 1e-07
        MAX_TANH_ARG = 1.0 - 1e-05

        def _norm(x):
            return jnp.sqrt(jnp.sum(x * x, axis=-1, keepdims=True)).clip(EPS)

        def logmap0(x):
            n = _norm(x)
            return jnp.arctanh(jnp.clip(n, EPS, MAX_TANH_ARG)) * x / n

        def expmap0(v):
            n = _norm(v)
            return jnp.tanh(n) * v / n

        def mobius_add(x, y):
            x2 = jnp.sum(x * x, -1, keepdims=True)
            y2 = jnp.sum(y * y, -1, keepdims=True)
            xy = jnp.sum(x * y, -1, keepdims=True)
            num = (1 + 2 * xy + y2) * x + (1 - x2) * y
            den = (1 + 2 * xy + x2 * y2).clip(EPS)
            return num / den

        def plin(x, w, b):
            return expmap0(logmap0(x) @ w + b)

        def layer_norm(x, eps=1e-06):
            m = x.mean(-1, keepdims=True)
            v = ((x - m) ** 2).mean(-1, keepdims=True)
            return (x - m) / jnp.sqrt(v + eps)

        def _beta(a, b):
            return math.exp(math.lgamma(a) + math.lgamma(b) - math.lgamma(a + b))
        D, H, FF = (256, 16, 1024)
        HD = D // H
        BETA_N = _beta(D / 2, 0.5)
        BETA_H = _beta(HD / 2, 0.5)

        def _to_heads(p):
            B, S, _ = p.shape
            t = logmap0(p).reshape(B, S, H, HD) * (BETA_H / BETA_N)
            return expmap0(jnp.transpose(t, (0, 2, 1, 3)))

        def _from_heads(ph):
            B, _, S, _ = ph.shape
            t = logmap0(ph) * (BETA_N / BETA_H)
            t = jnp.transpose(t, (0, 2, 1, 3)).reshape(B, S, D)
            return expmap0(t)
        ada = t_emb @ w_ada + b_ada
        sh_msa, sc_msa, g_msa, sh_mlp, sc_mlp, g_mlp = jnp.split(ada, 6, axis=-1)
        residual = x
        xn = layer_norm(logmap0(x))
        xm = expmap0(xn * (1 + sc_msa) + sh_msa)
        q = _to_heads(plin(xm, w_q, b_q))
        k = _to_heads(plin(xm, w_k, b_k))
        v = _to_heads(plin(xm, w_v, b_v))
        qt, kt, vt = (logmap0(q), logmap0(k), logmap0(v))
        scores = jnp.einsum('bhqd,bhkd->bhqk', qt, kt) / math.sqrt(HD)
        attn = jax.nn.softmax(scores, axis=-1)
        out_h = expmap0(jnp.einsum('bhqk,bhkd->bhqd', attn, vt))
        attn_out = plin(_from_heads(out_h), w_o, b_o)
        attn_t = g_msa * logmap0(attn_out)
        x = mobius_add(residual, expmap0(attn_t))
        residual = x
        xn = layer_norm(logmap0(x))
        xm = expmap0(xn * (1 + sc_mlp) + sh_mlp)
        ff = plin(plin(xm, w_f1, b_f1), w_f2, b_f2)
        ff_t = g_mlp * logmap0(ff)
        return mobius_add(residual, expmap0(ff_t))
    x = x + _L0_cond_ref(x, cond_1024[:, None, :], L0_cond_w_q, L0_cond_b_q, L0_cond_w_k, L0_cond_b_k, L0_cond_w_v, L0_cond_b_v, L0_cond_w_o, L0_cond_b_o, L0_cond_w_f1, L0_cond_b_f1, L0_cond_w_f2, L0_cond_b_f2, L0_cond_w_ada, L0_cond_b_ada)
    return x

_drawn_inputs = setup_inputs


def setup_inputs(seed=0):
    import zlib

    import numpy as np

    out = dict(_drawn_inputs(seed))
    spreads = {'L0_cond_b_q': (0.0, 0.8),
     'L0_cond_b_k': (0.0, 0.8),
     'L0_cond_b_v': (0.0, 0.1),
     'L0_cond_b_o': (0.0, 0.1),
     'L0_cond_b_f1': (0.0, 0.1),
     'L0_cond_b_f2': (0.0, 0.1),
     'L0_cond_b_ada': (0.0, 0.1)}
    factors = {'L0_cond_w_q': 7.81, 'L0_cond_w_k': 6.267}
    for name, (base, spread) in spreads.items():
        noise = np.random.default_rng([zlib.crc32(name.encode()), seed]).standard_normal(out[name].shape)
        drawn = base * np.exp(spread * noise) if base else spread * noise
        out[name] = jnp.asarray(drawn.astype(out[name].dtype))
    for name, factor in factors.items():
        out[name] = (out[name] * factor).astype(out[name].dtype)
    return out
```

```python
import math
from contextlib import ExitStack

import numpy as np

import concourse.bass as bass
from concourse import mybir

F32 = mybir.dt.float32
BF16 = mybir.dt.bfloat16
ALU = mybir.AluOpType
ACT = mybir.ActivationFunctionType
AX = mybir.AxisListType

P = 128
EPS = 1e-7
EPS2 = 1e-14
LN_TINY = 1e-18
LN_EPS = 1e-6
MAX_ARG = float(np.float32(1.0 - 1e-5))
AM = 0.5 * math.log((1 + MAX_ARG) / (1 - MAX_ARG))
SERIES_BELOW = 0.25


def _beta(a, b):
    return math.exp(math.lgamma(a) + math.lgamma(b) - math.lgamma(a + b))


def after(eng, sem, count):
    if isinstance(count, int) and count <= 0:
        return
    eng.wait_ge(sem, count)


def build(nc, x, cond, w_q, b_q, w_k, b_k, w_v, b_v, w_o, b_o, w_f1, b_f1, w_f2, b_f2, w_ada, b_ada, out):
    B, S, D = x.shape
    FF = w_f1.shape[1]
    H = 16
    HD = D // H
    C = D // P
    FC = FF // P
    TB = P // S
    T = B // TB
    HALF = T // 2
    RATIO = _beta(HD / 2, 0.5) / _beta(D / 2, 0.5)
    VW = HD + 1
    NF = 3 * H + 3
    SCALE = 1.0 / math.sqrt(HD)
    assert TB == 2 and C == 2 and H == 16 and HD == 16

    def head_of(o):
        j, c, p = o // 4, o // 2 % 2, o % 2
        return 8 * c + 2 * j + p

    with ExitStack() as ctx:
        def sb(name, shape, dt=F32):
            return ctx.enter_context(nc.sbuf_tensor(name, shape, dt))

        def ps(name, shape):
            return ctx.enter_context(nc.psum_tensor(name, shape, F32))

        def sem(name):
            return ctx.enter_context(nc.semaphore(name))

        mod_dram = nc.dram_tensor("mod_rows", (B, 6 * D), F32).ap()

        x_all = sb("x_all", [P, T, D])
        g_all = sb("g_all", [P, T, D])
        flat = g_all[:, :, :].rearrange("p t d -> p (t d)")
        at = [0]

        def scratch(n):
            at[0] += n
            return flat[:, at[0] - n:at[0]]

        w1 = scratch(C * FF).rearrange("p (c n) -> p c n", c=C)
        w1T = scratch(FC * D).rearrange("p (c n) -> p c n", c=FC)
        w2 = scratch(FC * D).rearrange("p (c n) -> p c n", c=FC)
        b1rep = scratch(FC * P).rearrange("p (c n) -> p c n", c=FC)
        wada = scratch(C * 6 * D).rearrange("p (c n) -> p c n", c=C)
        bada = scratch(6 * D)
        ada = scratch(6 * D)
        condr = scratch(D)
        condT = scratch(D).rearrange("p (c n) -> p c n", c=C)
        b1col = scratch(FC)
        b1row = scratch(P)[0:FC, :]

        wqkv = sb("wqkv", [P, C, 3 * D])
        wo = sb("wo", [P, C, D])
        wff = sb("wff", [P, C, 2 * D])
        w1b = sb("w1b", [P, C])
        bqkv = sb("bqkv", [P, 3 * D])
        bo = sb("bo", [P, D])
        b2 = sb("b2", [P, D])
        b12 = sb("b12", [P, D])
        bb = sb("bb", [P, 1])
        ident = sb("ident", [P, P])

        bn = sb("bn", [P, T, 6])
        arrays = sb("arrays", [P, 26, T])
        stats = sb("stats", [P, T, 4])

        mod = sb("mod", [P, 2, 2 * D])
        gate = sb("gate", [P, 2, D])
        lnx = sb("lnx", [P, D])
        t = sb("t", [P, D])
        tT = sb("tT", [P, 2, C, P])
        u = sb("u", [P, 3 * D])
        usq = sb("usq", [P, 3 * D])
        ss_t = sb("ss_t", [P, 2])
        rt = sb("rt", [P, 2])
        ct = sb("ct", [P, 2])
        hs = sb("hs", [P, NF])
        lnh = sb("lnh", [P, NF])
        y0 = sb("y0", [P, NF])
        nw = sb("nw", [P, 4, NF])
        roots = sb("roots", [P, NF])
        rlim = sb("rlim", [P, 3])
        fac = sb("fac", [P, 3 * H])
        qz = sb("qz", [P, 2, D])
        kk = sb("kk", [P, D])
        v = sb("v", [P, 2, H, VW])
        qkT = sb("qkT", [P, 6, P])
        pT = sb("pT", [P, H, P])
        rden = sb("rden", [P, H])
        o = sb("o", [P, D])
        oT = sb("oT", [P, C, P])
        z = sb("z", [P, D])
        st = sb("st", [P, 4])
        junk = sb("junk", [P, 4, D], BF16)

        c_fac = sb("c_fac", [P, NF])
        c_lim = sb("c_lim", [P, 3])
        c_three = sb("c_three", [P, NF])
        c_mhalf = sb("c_mhalf", [P, 2])
        c_half = sb("c_half", [P, 2])
        c_one = sb("c_one", [P, 2])
        c_two = sb("c_two", [P, 2])
        c_eps2 = sb("c_eps2", [P, 2])
        c_tiny = sb("c_tiny", [P, 1])

        pT_flat = pT[:, :, :].rearrange("p h n -> p (h n)")
        f1, ff, fg, xo = (pT_flat[:, 2 * D * n:2 * D * n + 2 * D].rearrange("p (j d) -> p j d", j=2) for n in range(4))
        yo = usq[:, 0:2 * D].rearrange("p (j d) -> p j d", j=2)
        xa = sb("xa", [P, 2, D])
        t2 = sb("t2", [P, 2, 2, D])
        t2T = sb("t2T", [P, 2, 2, C, P])
        ss2 = sb("ss2", [P, 2])
        rt2 = sb("rt2", [P, 2])
        ct2 = sb("ct2", [P, 2, 2])
        rh = sb("rh", [P, 2])
        rf = sb("rf", [P, 2])
        cf = sb("cf", [P, 2])
        parts = sb("parts", [P, 3, 2])
        den = sb("den", [P, 3, 2])
        qf = sb("qf", [P, 2])
        hh = sb("hh", [P, 3, 2])
        ch = sb("ch", [P, 2])
        ca = sb("ca", [P, 2])
        fst = sb("fst", [P, 3, 2])
        fin = sb("fin", [P, 11, 2])
        na = sb("na", [P, 2])
        th = sb("th", [P, 2])
        al2 = sb("al2", [P, 2])
        be2 = sb("be2", [P, 2])
        junk2 = wqkv[:, :, :].rearrange("p c n -> p (c n)")[:, 0:4 * D].bitcast(BF16).rearrange(
            "p (a j d) -> p a j d", a=4, j=2)

        p_to = ps("p_to", [P, 512])
        p_oz = ps("p_oz", [P, 512])
        p_qkv = ps("p_qkv", [P, 1024])
        p_s = ps("p_s", [P, 2048])
        s_bank = [p_s[:, 512 * n:512 * n + 512] for n in range(4)]

        cond_in = sem("cond_in"); wada_in = sem("wada_in"); bada_in = sem("bada_in")
        w1_in = sem("w1_in"); w2_in = sem("w2_in"); b1_in = sem("b1_in")
        wqkv_in = sem("wqkv_in"); rows_in = sem("rows_in")
        x_in = [sem(f"x_in{k}") for k in range(8)]
        ident_made = sem("ident_made"); consts_made = sem("consts_made")
        condT_psum = sem("condT_psum"); condT_made = sem("condT_made")
        ada_psum = sem("ada_psum"); ada_made = sem("ada_made"); ada_plus = sem("ada_plus")
        ada_stored = sem("ada_stored")
        w1T_psum = sem("w1T_psum"); w1T_made = sem("w1T_made"); b1rep_made = sem("b1rep_made")
        ffw_psum = sem("ffw_psum"); ffw_made = sem("ffw_made")
        zeros_set = sem("zeros_set")
        bn_done = sem("bn_done")
        vec_step = sem("vec_step"); vec_asks = sem("vec_asks"); act_answers = sem("act_answers")
        mod_in = [sem(f"mod_in{k}") for k in range(2)]
        gate_in = [sem(f"gate_in{k}") for k in range(2)]
        ln_half = sem("ln_half"); t_ready = sem("t_ready"); t_squared = sem("t_squared")
        rt_ready = sem("rt_ready"); ln_rows = sem("ln_rows"); ct_ready = sem("ct_ready")
        tT_psum = sem("tT_psum"); tT_ready = sem("tT_ready")
        qkv_psum = sem("qkv_psum"); u_ready = sem("u_ready"); u_squared = sem("u_squared")
        heads_summed = sem("heads_summed"); rows_summed = sem("rows_summed"); roots_ready = sem("roots_ready"); rlim_ready = sem("rlim_ready")
        ln_taken = sem("ln_taken"); y0_ready = sem("y0_ready"); newton = sem("newton"); fac_ready = sem("fac_ready")
        qk_ready = sem("qk_ready"); v_ready = sem("v_ready")
        qkT_psum = sem("qkT_psum"); qkT_ready = sem("qkT_ready")
        s_psum = sem("s_psum"); p_ready = sem("p_ready")
        o_psum = sem("o_psum"); rden_ready = sem("rden_ready"); o_ready = sem("o_ready")
        oT_psum = sem("oT_psum"); oT_ready = sem("oT_ready")
        z_psum = sem("z_psum"); z_ready = sem("z_ready"); zg_ready = sem("zg_ready")
        xg_summed = sem("xg_summed"); z_squared = sem("z_squared"); zg_squared = sem("zg_squared")
        stats_kept = sem("stats_kept")
        factors_made = sem("factors_made")
        mod2_in = [sem(f"mod2_in{k}") for k in range(2)]
        gate2_in = [sem(f"gate2_in{k}") for k in range(2)]
        xa_ready = sem("xa_ready"); x1_ready = sem("x1_ready"); ln2_half = sem("ln2_half")
        t2_ready = sem("t2_ready"); t2_squared = sem("t2_squared"); rt2_ready = sem("rt2_ready"); rh_ready = sem("rh_ready"); rf_ready = sem("rf_ready"); cf_ready = sem("cf_ready"); parts_ready = sem("parts_ready"); den_step = sem("den_step")
        ct2_ready = sem("ct2_ready"); t2T_psum = sem("t2T_psum"); t2T_ready = sem("t2T_ready")
        ff_psum = sem("ff_psum"); qf_ready = sem("qf_ready"); hh_half = sem("hh_half"); hh_scaled = sem("hh_scaled"); hh_ready = sem("hh_ready")
        ch_ready = sem("ch_ready"); ca_ready = sem("ca_ready")
        f1_ready = sem("f1_ready"); ff_ready = sem("ff_ready"); fg_ready = sem("fg_ready")
        ff_squared = sem("ff_squared"); fg_squared = sem("fg_squared"); xf_summed = sem("xf_summed")
        fin_step = sem("fin_step"); na_ready = sem("na_ready"); th_ready = sem("th_ready")
        al2_ready = sem("al2_ready"); be2_ready = sem("be2_ready"); xo_ready = sem("xo_ready"); yo_ready = sem("yo_ready")
        out_ready = sem("out_ready"); out_stored = sem("out_stored")

        (MEAN, VAR, XX, R1, OMX, ALPHA, BETA, MEAN1, R2, XX1, OMX1, W0, W1_, W2_, W3, W4, W5, W6, W7, W8,
         W9, W10, W11, W12, W13, W14) = range(26)

        def row(k):
            return arrays[:, k, :]

        x_t = x.rearrange("(t b) s d -> (b s) t d", b=TB)
        out_t = out.rearrange("(t b) s d -> (b s) t d", b=TB)

        def bcast(vec, n):
            return vec.rearrange("(a n) -> a n", a=1).broadcast_to([P, n])

        def mod_rows(i, lo, hi, b):
            return mod_dram[bass.ds(TB * i + b, 1), lo:hi].broadcast_to([S, hi - lo])

        L_A, L_B, L_C, L_D, L_H, L_L = 0, 1, 2, 3, 4, 5
        FIRST = 8
        M_A, M_B, M_C = 0, 1, 2
        FIRST2 = 4
        FIN_STEPS = 11

        def run_slots(eng, slot, first, items, slots):
            for s in range(first):
                slot(s // 2, s % 2)
            with eng.Fori(first // 2, items // 2) as h:
                slot(h, 0)
                slot(h, 1)
            for s in range(items, slots):
                slot(s // 2, s % 2)

        def count(n):
            return min(n, T) if isinstance(n, int) else n

        def run_tiles(eng, slot):
            run_slots(eng, slot, FIRST, T, T + L_L)

        def run_pairs(eng, slot):
            run_slots(eng, slot, FIRST2, HALF, HALF + M_C)

        def on(h, off, lag, items=T):
            return not isinstance(h, int) or 0 <= 2 * h + off - lag < items

        def on2(h, off, lag):
            return on(h, off, lag, HALF)

        block = ctx.enter_context(nc.Block())

        @block.sync
        def _(sp):
            sp.dma_start(condr, cond[:, :]).then_inc(cond_in, 16)
            sp.dma_start(wada, w_ada.rearrange("(c p) n -> p c n", p=P)).then_inc(wada_in, 16)
            sp.dma_start(bada, bcast(b_ada, 6 * D)).then_inc(bada_in, 16)
            for k in range(8):
                n = T // 8
                sp.dma_start(x_all[:, n * k:n * k + n, :], x_t[:, n * k:n * k + n, :]).then_inc(x_in[k], 16)
            sp.wait_ge(ada_plus, 2)
            sp.dma_start(mod_dram[:, :], ada).then_inc(ada_stored, 16)
            sp.wait_ge(ada_stored, 16)

            def slot(h, off):
                if on(h, off, L_A):
                    i, k = 2 * h + off, off % 2
                    after(sp, t_ready, i - 1)
                    for b in range(TB):
                        sp.dma_start(mod[S * b:S * b + S, k, 0:2 * D], mod_rows(i, 0, 2 * D, b)).then_inc(mod_in[k], 16)
                if on(h, off, L_H):
                    i, k = 2 * h + off - L_H, (off - L_H) % 2
                    after(sp, zg_ready, i - 1)
                    for b in range(TB):
                        sp.dma_start(gate[S * b:S * b + S, k, :], mod_rows(i, 2 * D, 3 * D, b)).then_inc(gate_in[k], 16)

            run_tiles(sp, slot)

            def slot2(h, off):
                if on2(h, off, M_A):
                    i = 2 * h + off - M_A
                    after(sp, t2_ready, 2 * i)
                    for j in range(2):
                        for b in range(TB):
                            sp.dma_start(mod[S * b:S * b + S, j, :], mod_rows(2 * i + j, 3 * D, 5 * D, b)).then_inc(mod2_in[j], 16)
                if on2(h, off, M_B):
                    i = 2 * h + off - M_B
                    after(sp, fg_ready, 2 * i)
                    for j in range(2):
                        for b in range(TB):
                            sp.dma_start(gate[S * b:S * b + S, j, :], mod_rows(2 * i + j, 5 * D, 6 * D, b)).then_inc(gate2_in[j], 16)
                if on2(h, off, M_C):
                    i = 2 * h + off - M_C
                    sp.wait_ge(out_ready, 2 * i + 2)
                    sp.dma_start(out_t[:, bass.ds(2 * i, 2), :], x_all[:, bass.ds(2 * i, 2), :]).then_inc(out_stored, 16)

            sp.wait_ge(t_ready, T)
            sp.wait_ge(zg_ready, T)
            run_pairs(sp, slot2)
            sp.wait_ge(out_stored, 16 * HALF)

        @block.gpsimd
        def _(pool):
            pool.memset(ident[:, :], 0.0).then_inc(ident_made, 1)
            pool.wait_ge(ident_made, 1)
            pool.affine_select(out=ident[:, :], in_=ident[:, :], compare_op=ALU.not_equal, fill=1.0,
                               base=0, pattern=[[-1, P]], channel_multiplier=1).then_inc(ident_made, 1)
            pool.memset(c_fac[:, 0:2 * H], -0.5 * AM)
            pool.memset(c_fac[:, 2 * H:3 * H], -0.5 * AM / RATIO)
            pool.memset(c_fac[:, 3 * H:3 * H + 2], -0.5 * AM * RATIO)
            pool.memset(c_fac[:, 3 * H + 2:NF], -0.5 * AM)
            pool.memset(c_lim[:, 0:2], RATIO)
            pool.memset(c_lim[:, 2:3], 1.0)
            pool.memset(c_three[:, :], 3.0)
            pool.memset(c_mhalf[:, :], -0.5)
            pool.memset(c_half[:, :], 0.5)
            pool.memset(c_one[:, :], 1.0)
            pool.memset(c_two[:, :], 2.0)
            pool.memset(c_eps2[:, :], EPS2)
            pool.memset(c_tiny[:, :], LN_TINY).then_inc(consts_made, 1)
            pool.memset(qz[:, :, :], 0.0)
            pool.memset(pT[:, :, :], 0.0)
            pool.memset(v[:, :, :, :], 1.0).then_inc(zeros_set, 1)
            pool.wait_ge(consts_made, 1)
            pool.dma_start(wo[:, :, :], w_o.rearrange("(c p) n -> p c n", p=P)).then_inc(rows_in, 16)
            pool.dma_start(bo[:, :], bcast(b_o, D)).then_inc(rows_in, 16)
            pool.dma_start(b2[:, :], bcast(b_f2, D)).then_inc(rows_in, 16)

            def token_root(i, k):
                pool.wait_ge(t_squared, i + 1)
                after(pool, ct_ready, i - 1)
                pool.tensor_tensor(rt[:, k:k + 1], ss_t[:, k:k + 1], c_mhalf[:, 0:1], ALU.pow).then_inc(rt_ready, 1)

            def head_roots(i):
                pool.wait_ge(y0_ready, i + 1)
                pool.wait_ge(rows_summed, i + 1)
                after(pool, roots_ready, i)
                pool.tensor_tensor(nw[:, 0, :], y0[:, :], y0[:, :], ALU.mult).then_inc(newton, 1)
                pool.wait_ge(newton, 4 * i + 1)
                pool.tensor_tensor(nw[:, 1, :], nw[:, 0, :], hs[:, :], ALU.mult).then_inc(newton, 1)
                pool.wait_ge(newton, 4 * i + 2)
                pool.tensor_tensor(nw[:, 2, :], nw[:, 1, :], c_three[:, :], ALU.subtract).then_inc(newton, 1)
                pool.wait_ge(newton, 4 * i + 3)
                pool.tensor_tensor(nw[:, 3, :], nw[:, 2, :], y0[:, :], ALU.mult).then_inc(newton, 1)
                pool.wait_ge(newton, 4 * i + 4)
                after(pool, fac_ready, i)
                pool.tensor_tensor(roots[:, :], nw[:, 3, :], c_fac[:, :], ALU.mult).then_inc(roots_ready, 1)

            def keep_stats(i):
                pool.wait_ge(z_squared, i + 1)
                pool.wait_ge(zg_squared, i + 1)
                pool.wait_ge(xg_summed, i + 1)
                pool.tensor_copy(stats[:, bass.ds(i, 1), :].rearrange("p a n -> p (a n)"), st[:, :]).then_inc(stats_kept, 1)

            def slot(h, off):
                if on(h, off, L_C):
                    token_root(2 * h + off - L_C, (off - L_C) % 2)
                if on(h, off, L_L):
                    keep_stats(2 * h + off - L_L)
                if on(h, off, L_D):
                    head_roots(2 * h + off - L_D)

            run_tiles(pool, slot)

            def token_roots2(i, k):
                pool.wait_ge(t2_squared, 2 * i + 2)
                after(pool, ct2_ready, i)
                pool.tensor_tensor(rt2[:, :], ss2[:, :], c_mhalf[:, :], ALU.pow).then_inc(rt2_ready, 1)

            def inner_roots(i):
                pool.wait_ge(hh_ready, i + 1)
                after(pool, ch_ready, i)
                pool.tensor_tensor(rh[:, :], hh[:, 1, :], c_mhalf[:, :], ALU.pow).then_inc(rh_ready, 1)

            def output_factors(i):
                step = [FIN_STEPS * i]

                def op(k, a, b, f):
                    pool.tensor_tensor(fin[:, k, :], a, b, f).then_inc(fin_step, 1)
                    step[0] = step[0] + 1
                    pool.wait_ge(fin_step, step[0])
                    return fin[:, k, :]

                pool.wait_ge(ff_squared, 2 * i + 2)
                after(pool, cf_ready, i)
                pool.tensor_tensor(rf[:, :], fst[:, 0, :], c_mhalf[:, :], ALU.pow).then_inc(rf_ready, 1)
                after(pool, be2_ready, i)
                pool.wait_ge(fg_squared, 2 * i + 2)
                pool.wait_ge(cf_ready, i + 1)
                a = op(0, cf[:, :], cf[:, :], ALU.mult)
                a = op(1, a, fst[:, 1, :], ALU.mult)
                nn = op(2, a, c_eps2[:, :], ALU.add)
                after(pool, th_ready, i)
                pool.tensor_tensor(na[:, :], nn, c_half[:, :], ALU.pow).then_inc(na_ready, 1)
                rn = op(3, nn, c_mhalf[:, :], ALU.pow)
                pool.wait_ge(th_ready, i + 1)
                a = op(4, th[:, :], rn, ALU.mult)
                kap = op(5, a, cf[:, :], ALU.mult)
                a = op(6, kap, kap, ALU.mult)
                y2 = op(7, a, fst[:, 1, :], ALU.mult)
                pool.wait_ge(xf_summed, 2 * i + 2)
                a = op(8, kap, fst[:, 2, :], ALU.mult)
                a = op(9, a, c_two[:, :], ALU.mult)
                c1 = op(10, a, c_one[:, :], ALU.add)
                pool.tensor_tensor(parts[:, 0, :], arrays[:, XX1, bass.ds(2 * i, 2)], y2, ALU.mult).then_inc(parts_ready, 1)
                pool.tensor_tensor(parts[:, 1, :], c1, y2, ALU.add).then_inc(parts_ready, 1)
                pool.tensor_tensor(parts[:, 2, :], arrays[:, OMX1, bass.ds(2 * i, 2)], kap, ALU.mult).then_inc(parts_ready, 1)

            def add_x(i, j):
                n = 2 * i + j
                pool.wait_ge(yo_ready, n + 1)
                xt = x_all[:, bass.ds(n, 1), :].rearrange("p a d -> p (a d)")
                pool.tensor_tensor(xt, xt, yo[:, j, :], ALU.add).then_inc(out_ready, 1)

            def slot2(h, off):
                if on2(h, off, M_C):
                    output_factors(2 * h + off - M_C)
                if on2(h, off, M_B):
                    inner_roots(2 * h + off - M_B)
                if on2(h, off, M_A):
                    token_roots2(2 * h + off - M_A, (off - M_A) % 2)
                if on2(h, off, M_C):
                    for j in range(2):
                        add_x(2 * h + off - M_C, j)

            pool.wait_ge(factors_made, 1)
            run_pairs(pool, slot2)

        @block.scalar
        def _(act):
            act.dma_start(w1, w_f1.rearrange("(c p) n -> p c n", p=P)).then_inc(w1_in, 16)
            act.dma_start(w2, w_f2.rearrange("(c p) n -> p c n", p=P)).then_inc(w2_in, 16)
            act.dma_start(b1row, b_f1.rearrange("(c n) -> c n", n=P)).then_inc(b1_in, 16)
            for k, (w, b) in enumerate(((w_q, b_q), (w_k, b_k), (w_v, b_v))):
                act.dma_start(wqkv[:, :, k * D:k * D + D], w.rearrange("(c p) n -> p c n", p=P)).then_inc(wqkv_in, 16)
                act.dma_start(bqkv[:, k * D:k * D + D], bcast(b, D)).then_inc(wqkv_in, 16)
            for k in range(FC // 2):
                act.wait_ge(w1T_psum, k + 1)
                act.activation(w1T[:, 2 * k:2 * k + 2, :].rearrange("p c n -> p (c n)"),
                               s_bank[2 + k % 2][:, :], ACT.Copy).then_inc(w1T_made, 1)

            def rsq():
                asked[0] += 1
                act.wait_ge(vec_asks, asked[0])
                act.activation(row(W1_), row(W0), ACT.Ln).then_inc(ln_rows, 1)
                rsqs[0] += 1
                act.wait_ge(ln_rows, rsqs[0])
                act.activation(row(W2_), row(W1_), ACT.Exp, scale=-0.5).then_inc(act_answers, 1)

            def elementwise(f, src, dst):
                asked[0] += 1
                act.wait_ge(vec_asks, asked[0])
                act.activation(row(dst), row(src), f).then_inc(act_answers, 1)

            asked, rsqs = [0], [0]
            act.wait_ge(consts_made, 1)
            rsq()
            elementwise(ACT.Ln, W7, W8)
            rsq()

            def evac_qkT(i):
                act.wait_ge(qkT_psum, i + 1)
                after(act, s_psum, i)
                act.activation(qkT[:, :, :].rearrange("p a n -> p (a n)"), p_s[:, 0:6 * P], ACT.Copy).then_inc(qkT_ready, 1)

            def evac_oT(i):
                act.wait_ge(oT_psum, i + 1)
                after(act, z_psum, i)
                act.activation(oT[:, :, :].rearrange("p c n -> p (c n)"), p_oz[:, 0:D], ACT.Copy).then_inc(oT_ready, 1)

            def evac_tT(i, k):
                act.wait_ge(tT_psum, i + 1)
                after(act, qkv_psum, i - 1)
                act.activation(tT[:, k, :, :].rearrange("p c n -> p (c n)"), p_to[:, 0:D], ACT.Copy).then_inc(tT_ready, 1)

            def square_u(i):
                act.wait_ge(u_ready, i + 1)
                after(act, heads_summed, i)
                act.activation(usq[:, :], u[:, :], ACT.Square).then_inc(u_squared, 1)

            def square_t(i, k):
                act.wait_ge(t_ready, i + 1)
                after(act, rt_ready, i - 1)
                after(act, t_squared, i)
                act.activation(junk[:, 0, :], t[:, :], ACT.Square, accum_out=ss_t[:, k:k + 1]).then_inc(t_squared, 1)

            def inverse_norms(i):
                act.wait_ge(rows_summed, i + 1)
                after(act, y0_ready, i)
                act.activation(lnh[:, :], hs[:, :], ACT.Ln, bias=c_tiny[:, 0:1]).then_inc(ln_taken, 1)
                act.wait_ge(ln_taken, i + 1)
                after(act, roots_ready, i)
                act.activation(y0[:, :], lnh[:, :], ACT.Exp, scale=-0.5).then_inc(y0_ready, 1)

            def square_z(i):
                act.wait_ge(z_ready, i + 1)
                after(act, stats_kept, i)
                after(act, z_squared, i)
                act.activation(junk[:, 1, :], z[:, :], ACT.Square, accum_out=st[:, 0:1]).then_inc(z_squared, 1)
                act.wait_ge(zg_ready, i + 1)
                after(act, zg_squared, i)
                act.activation(junk[:, 2, :], g_all[:, bass.ds(i, 1), :].rearrange("p a d -> p (a d)"),
                               ACT.Square, accum_out=st[:, 3:4]).then_inc(zg_squared, 1)

            def exp_scores(i):
                act.wait_ge(s_psum, i + 1)
                after(act, o_psum, i)
                act.wait_ge(zeros_set, 1)
                for b in range(TB):
                    half = slice(S * b, S * b + S)
                    act.activation(pT[half, :, half].rearrange("p (j o) q -> p j o q", j=4),
                                   p_s[half, :].rearrange("p (j n) -> p j n", j=4)[:, :, 0:4 * S].rearrange(
                                       "p j (o q) -> p j o q", q=S),
                                   ACT.Exp, scale=SCALE).then_inc(p_ready, 1)

            def slot(h, off):
                if on(h, off, L_H):
                    evac_qkT(2 * h + off - L_H)
                if on(h, off, L_L):
                    evac_oT(2 * h + off - L_L)
                if on(h, off, L_B):
                    evac_tT(2 * h + off - L_B, (off - L_B) % 2)
                if on(h, off, L_D):
                    square_u(2 * h + off - L_D)
                if on(h, off, L_A):
                    square_t(2 * h + off - L_A, (off - L_A) % 2)
                if on(h, off, L_D):
                    inverse_norms(2 * h + off - L_D)
                if on(h, off, L_L):
                    square_z(2 * h + off - L_L)
                if on(h, off, L_H):
                    exp_scores(2 * h + off - L_H)

            run_tiles(act, slot)

            rsq()
            rsq()
            elementwise(ACT.Tanh, W7, W8)
            rsq()
            elementwise(ACT.Ln, W7, W8)
            rsq()

            def scale_x(i, j):
                n = 2 * i + j
                after(act, x1_ready, n - 1)
                act.activation(xa[:, j, :], x_all[:, bass.ds(n, 1), :].rearrange("p a d -> p (a d)"), ACT.Copy,
                               scale=arrays[:, ALPHA, bass.ds(n, 1)]).then_inc(xa_ready, 1)

            def square_t2(i, j, k):
                n = 2 * i + j
                act.wait_ge(t2_ready, n + 1)
                after(act, rt2_ready, i)
                after(act, t2_squared, n - 1)
                act.activation(junk2[:, 0, j, :], t2[:, k, j, :], ACT.Square, accum_out=ss2[:, j:j + 1]).then_inc(t2_squared, 1)

            def evac_t2T(i, k):
                act.wait_ge(t2T_psum, i + 1)
                after(act, ff_psum, 2 * (i - 1))
                act.activation(t2T[:, k, :, :, :].rearrange("p j c n -> p (j c n)"), p_to[:, :], ACT.Copy).then_inc(t2T_ready, 1)

            def square_ff(i, j):
                n = 2 * i + j
                act.wait_ge(ff_ready, n + 1)
                after(act, parts_ready, 3 * i)
                after(act, ff_squared, n - 1)
                act.activation(junk2[:, 1, j, :], ff[:, j, :], ACT.Square, accum_out=fst[:, 0, j:j + 1]).then_inc(ff_squared, 1)

            def square_fg(i, j):
                n = 2 * i + j
                act.wait_ge(fg_ready, n + 1)
                after(act, fg_squared, n - 1)
                act.activation(junk2[:, 2, j, :], fg[:, j, :], ACT.Square, accum_out=fst[:, 1, j:j + 1]).then_inc(fg_squared, 1)

            def tanh_norm(i):
                act.wait_ge(na_ready, i + 1)
                after(act, parts_ready, 3 * i)
                act.activation(th[:, :], na[:, :], ACT.Tanh).then_inc(th_ready, 1)

            def scale_x1(i, j):
                n = 2 * i + j
                act.wait_ge(al2_ready, i + 1)
                after(act, yo_ready, n - 1)
                act.activation(xo[:, j, :], g_all[:, bass.ds(n, 1), :].rearrange("p a d -> p (a d)"), ACT.Copy,
                               scale=al2[:, j:j + 1]).then_inc(xo_ready, 1)

            def slot2(h, off):
                if on2(h, off, M_A):
                    i, k = 2 * h + off - M_A, (off - M_A) % 2
                    for j in range(2):
                        scale_x(i, j)
                if on2(h, off, M_C):
                    tanh_norm(2 * h + off - M_C)
                if on2(h, off, M_A):
                    for j in range(2):
                        square_t2(i, j, k)
                    evac_t2T(i, k)
                if on2(h, off, M_C):
                    for j in range(2):
                        scale_x1(2 * h + off - M_C, j)
                if on2(h, off, M_B):
                    for j in range(2):
                        square_ff(2 * h + off - M_B, j)
                        square_fg(2 * h + off - M_B, j)

            act.wait_ge(factors_made, 1)
            run_pairs(act, slot2)

        @block.tensor
        def _(pe):
            pe.wait_ge(ident_made, 2)
            pe.wait_ge(cond_in, 16)
            for c in range(C):
                pe.transpose(p_to[:, c * P:c * P + P], condr[:, c * P:c * P + P], ident[:, :])
            pe.wait_ge(b1_in, 16)
            pe.transpose(p_to[:, D:D + FC], b1row, ident[0:FC, 0:FC]).then_inc(condT_psum, 1)
            pe.wait_ge(w1_in, 16)
            for k in range(FC // 2):
                after(pe, w1T_made, k - 1)
                for m in range(4):
                    fc, c = 2 * k + m // 2, m % 2
                    mm = pe.transpose(s_bank[2 + k % 2][:, m * P:m * P + P], w1[:, c, fc * P:fc * P + P], ident[:, :])
                mm.then_inc(w1T_psum, 1)
            pe.wait_ge(wada_in, 16)
            pe.wait_ge(condT_made, 1)
            for n, bank in enumerate((p_qkv[:, 0:512], p_qkv[:, 512:1024], p_oz[:, :])):
                for c in range(C):
                    mm = pe.matmul(bank, condT[:, c, :], wada[:, c, n * 512:n * 512 + 512], start=c == 0, stop=c == C - 1)
            mm.then_inc(ada_psum, 1)
            pe.wait_ge(w1T_made, FC // 2)
            pe.wait_ge(w2_in, 16)
            pe.wait_ge(b1rep_made, 2)
            pe.wait_ge(ada_made, 3)

            def inner_sum(dst, lhs, rhs):
                for fc in range(FC):
                    mm = pe.matmul(dst, lhs(fc), rhs(fc), start=fc == 0, stop=fc == FC - 1)
                return mm

            for m in range(C):
                w1Tm = lambda fc: w1T[:, fc, m * P:m * P + P]
                inner_sum(p_s[:, m * 512:m * 512 + D], w1Tm, lambda fc: w2[:, fc, :])
                inner_sum(s_bank[2 + m][:, 0:D], w1Tm, lambda fc: w1T[:, fc, :])
                inner_sum(p_to[:, m:m + 1], w1Tm, lambda fc: b1col[:, fc:fc + 1])
            inner_sum(p_oz[:, 0:D], lambda fc: b1rep[:, fc, :], lambda fc: w2[:, fc, :])
            inner_sum(p_to[:, 2:3], lambda fc: b1rep[:, fc, :], lambda fc: b1col[:, fc:fc + 1]).then_inc(ffw_psum, 1)
            pe.wait_ge(ffw_made, 1)
            pe.wait_ge(wqkv_in, 96)
            pe.wait_ge(rows_in, 48)
            pe.wait_ge(zeros_set, 1)

            def transpose_t(i):
                pe.wait_ge(t_ready, i + 1)
                after(pe, tT_ready, i)
                after(pe, o_ready, i + L_B - L_L + 1)
                for c in range(C):
                    mm = pe.transpose(p_to[:, c * P:c * P + P], t[:, c * P:c * P + P], ident[:, :])
                mm.then_inc(tT_psum, 1)

            def transpose_qk(i):
                pe.wait_ge(qk_ready, 2 * i + 2)
                after(pe, p_ready, 2 * i)
                for c in range(C):
                    pe.transpose(p_s[:, c * P:c * P + P], kk[:, c * P:c * P + P], ident[:, :])
                for m in range(4):
                    mm = pe.transpose(p_s[:, (2 + m) * P:(3 + m) * P], qz[:, m // 2, (m % 2) * P:(m % 2) * P + P], ident[:, :])
                mm.then_inc(qkT_psum, 1)

            def transpose_o(i):
                pe.wait_ge(o_ready, i + 1)
                after(pe, z_ready, i)
                for c in range(C):
                    mm = pe.transpose(p_oz[:, c * P:c * P + P], o[:, c * P:c * P + P], ident[:, :])
                mm.then_inc(oT_psum, 1)

            def project_o(i):
                pe.wait_ge(oT_ready, i + 1)
                for c in range(C):
                    mm = pe.matmul(p_oz[:, 0:D], oT[:, c, :], wo[:, c, :], start=c == 0, stop=c == C - 1)
                mm.then_inc(z_psum, 1)

            def scores(i):
                pe.wait_ge(qkT_ready, i + 1)
                for j in range(4):
                    g = slice(32 * j, 32 * j + 32)
                    for c in range(C):
                        for b in range(TB):
                            tok = slice(S * b, S * b + S)
                            col = j * 512 + c * 128
                            q2 = qkT[g, 2:6, :].rearrange("p (l c) n -> p l c n", c=C)[:, :, c, tok]
                            mm = pe.matmul(p_s[tok, col:col + 2 * S], qkT[g, c, tok], q2, start=True, stop=True,
                                           skip_group_check=True)
                mm.then_inc(s_psum, 1)

            def qkv(i, k):
                pe.wait_ge(tT_ready, i + 1)
                after(pe, u_ready, i)
                for lo, hi in ((0, 2 * D), (2 * D, 3 * D)):
                    for c in range(C):
                        mm = pe.matmul(p_qkv[:, lo:hi], tT[:, k, c, :], wqkv[:, c, lo:hi], start=c == 0, stop=c == C - 1)
                mm.then_inc(qkv_psum, 1)

            def attend(i, k):
                pe.wait_ge(p_ready, 2 * i + 2)
                pe.wait_ge(v_ready, i + 1)
                after(pe, o_ready, i)
                after(pe, tT_ready, count(i + L_H - L_B + 1))
                for n in range(H):
                    hd = head_of(n)
                    mm = pe.matmul(p_to[:, hd * VW:hd * VW + VW], pT[:, n, :], v[:, k, hd, :], start=True, stop=True)
                mm.then_inc(o_psum, 1)

            def slot(h, off):
                if on(h, off, L_H):
                    transpose_qk(2 * h + off - L_H)
                if on(h, off, L_B):
                    transpose_t(2 * h + off - L_B)
                if on(h, off, L_L):
                    transpose_o(2 * h + off - L_L)
                    project_o(2 * h + off - L_L)
                if on(h, off, L_H):
                    scores(2 * h + off - L_H)
                if on(h, off, L_C):
                    qkv(2 * h + off - L_C, (off - L_C) % 2)
                if on(h, off, L_H):
                    attend(2 * h + off - L_H, (off - L_H) % 2)

            run_tiles(pe, slot)

            def transpose_t2(i, k):
                pe.wait_ge(t2_ready, 2 * i + 2)
                after(pe, t2T_ready, i)
                for m in range(4):
                    mm = pe.transpose(p_to[:, m * P:m * P + P], t2[:, k, m // 2, (m % 2) * P:(m % 2) * P + P], ident[:, :])
                mm.then_inc(t2T_psum, 1)

            def inner(i, j, k):
                pe.wait_ge(t2T_ready, i + 1)
                after(pe, f1_ready, 2 * (i - 1))
                after(pe, hh_ready, i - 1)
                bank = (p_qkv, p_s)[k]
                for c in range(C):
                    pe.matmul(bank[:, 512 * j:512 * j + 512], t2T[:, k, j, c, :], wff[:, c, :], start=c == 0, stop=c == C - 1)
                for c in range(C):
                    mm = pe.matmul(s_bank[2 + k][:, j:j + 1], t2T[:, k, j, c, :], w1b[:, c:c + 1], start=c == 0, stop=c == C - 1)
                mm.then_inc(ff_psum, 1)

            def slot2(h, off):
                if on2(h, off, M_A):
                    i, k = 2 * h + off - M_A, (off - M_A) % 2
                    transpose_t2(i, k)
                    for j in range(2):
                        inner(i, j, k)

            pe.wait_ge(factors_made, 1)
            run_pairs(pe, slot2)

        @block.vector
        def _(dve):
            dve.wait_ge(condT_psum, 1)
            dve.tensor_copy(condT.rearrange("p c n -> p (c n)"), p_to[:, 0:D]).then_inc(condT_made, 1)
            dve.tensor_copy(b1col, p_to[:, D:D + FC]).then_inc(b1rep_made, 1)
            dve.wait_ge(b1rep_made, 1)
            dve.tensor_copy(b1rep, b1col.unsqueeze(2).broadcast_to([P, FC, P])).then_inc(b1rep_made, 1)
            dve.wait_ge(ada_psum, 1)
            dve.wait_ge(bada_in, 16)
            for n, bank in enumerate((p_qkv[:, 0:512], p_qkv[:, 512:1024], p_oz[:, :])):
                dve.tensor_tensor(ada[:, n * 512:n * 512 + 512], bank, bada[:, n * 512:n * 512 + 512], ALU.add).then_inc(ada_made, 1)
            dve.wait_ge(ada_made, 3)
            for n in (1, 4):
                dve.tensor_scalar(ada[:, n * D:n * D + D], ada[:, n * D:n * D + D], 1.0, None, ALU.add).then_inc(ada_plus, 1)
            n = T // 8
            for k in range(8):
                dve.wait_ge(x_in[k], 16)
                with dve.Fori(n * k, n * k + n) as i:
                    dve.bn_stats(bn[:, bass.ds(i, 1), :].rearrange("p a n -> p (a n)"),
                                 x_all[:, bass.ds(i, 1), :].rearrange("p a d -> p (a d)")).then_inc(bn_done, 1)
            dve.wait_ge(ffw_psum, 1)
            for m in range(C):
                dve.tensor_copy(wff[:, m, 0:D], p_s[:, m * 512:m * 512 + D])
                dve.tensor_copy(wff[:, m, D:2 * D], s_bank[2 + m][:, 0:D])
            dve.tensor_scalar(w1b[:, :], p_to[:, 0:C], 2.0, None, ALU.mult)
            dve.tensor_copy(b12[:, :], p_oz[:, 0:D])
            dve.tensor_copy(bb[:, :], p_to[:, 2:3]).then_inc(ffw_made, 1)

            steps, asks = [0], [0]

            def step(ins):
                ins.then_inc(vec_step, 1)
                steps[0] += 1
                dve.wait_ge(vec_step, steps[0])

            def tt(dst, a, b, f):
                step(dve.tensor_tensor(row(dst), row(a), row(b), f))

            def ts(dst, a, s1, f1_, s2=None, f2_=None):
                if f2_ is None:
                    step(dve.tensor_scalar(row(dst), row(a), s1, None, f1_))
                else:
                    step(dve.tensor_scalar(row(dst), row(a), s1, s2, f1_, f2_))

            def stt(dst, a, s1, b, f1_, f2_):
                step(dve.scalar_tensor_tensor(out=row(dst), in0=row(a), scalar=s1, in1=row(b), op0=f1_, op1=f2_))

            def ask():
                dve.drain().then_inc(vec_asks, 1)
                asks[0] += 1
                dve.wait_ge(act_answers, asks[0])

            def rsq(dst):
                ask()
                tt(W3, W2_, W2_, ALU.mult)
                stt(W3, W3, -0.5, W0, ALU.mult, ALU.mult)
                stt(dst, W3, 1.5, W2_, ALU.add, ALU.mult)

            def log_map_factor(dst, xx):
                ts(W0, xx, EPS2, ALU.max)
                rsq(W4)
                tt(W5, W0, W4, ALU.mult)
                ts(W5, W5, MAX_ARG, ALU.min)
                ts(W6, W5, -1.0, ALU.mult, 1.0, ALU.add)
                step(dve.reciprocal(row(W6), row(W6)))
                stt(W7, W5, 1.0, W6, ALU.add, ALU.mult)
                ask()
                stt(W8, W8, 0.5, W4, ALU.mult, ALU.mult)
                tt(W9, W5, W5, ALU.mult)
                ts(W10, W9, 1.0 / 15, ALU.mult)
                for m in (13, 11, 9, 7, 5, 3):
                    stt(W10, W10, 1.0 / m, W9, ALU.add, ALU.mult)
                ts(W10, W10, 1.0, ALU.add)
                tt(W10, W10, W5, ALU.mult)
                tt(W10, W10, W4, ALU.mult)
                ts(W11, W5, SERIES_BELOW, ALU.is_lt)
                tt(W10, W10, W8, ALU.subtract)
                tt(W10, W10, W11, ALU.mult)
                tt(dst, W8, W10, ALU.add)

            def norm_factor(dst, s, var):
                tt(W0, s, s, ALU.mult)
                tt(W0, W0, var, ALU.mult)
                ts(W0, W0, LN_EPS, ALU.add)
                rsq(W4)
                tt(dst, s, W4, ALU.mult)

            dve.wait_ge(bn_done, T)
            part = lambda k: bn[:, :, k]
            add = lambda dst, a, b, f: step(dve.tensor_tensor(row(dst), a, b, f))
            add(MEAN, part(1), part(4), ALU.add)
            ts(MEAN, MEAN, 0.5, ALU.mult)
            add(W0, part(1), part(4), ALU.subtract)
            add(W1_, part(2), part(5), ALU.add)
            tt(W0, W0, W0, ALU.mult)
            stt(W0, W0, D / 4.0, W1_, ALU.mult, ALU.add)
            ts(VAR, W0, 1.0 / D, ALU.mult)
            tt(W1_, MEAN, MEAN, ALU.mult)
            stt(XX, W1_, float(D), W0, ALU.mult, ALU.add)
            ts(OMX, XX, -1.0, ALU.mult, 1.0, ALU.add)
            log_map_factor(W12, XX)
            norm_factor(R1, W12, VAR)

            dve.wait_ge(wqkv_in, 96)
            dve.wait_ge(rows_in, 48)
            dve.wait_ge(zeros_set, 1)
            dve.wait_ge(ada_stored, 16)

            def tile_of(big, i):
                return big[:, bass.ds(i, 1), :].rearrange("p a d -> p (a d)")

            def modulate(i, k, half):
                dve.wait_ge(mod_in[k], 32 * half + 32)
                after(dve, t_ready, i)
                dve.scalar_tensor_tensor(out=lnx[:, :], in0=tile_of(x_all, i), scalar=arrays[:, MEAN, bass.ds(i, 1)],
                                         in1=mod[:, k, D:2 * D], op0=ALU.subtract, op1=ALU.mult).then_inc(ln_half, 1)
                dve.wait_ge(ln_half, i + 1)
                after(dve, tT_psum, i)
                after(dve, t_squared, i)
                dve.scalar_tensor_tensor(out=t[:, :], in0=lnx[:, :], scalar=arrays[:, R1, bass.ds(i, 1)],
                                         in1=mod[:, k, 0:D], op0=ALU.mult, op1=ALU.add).then_inc(t_ready, 1)

            def project(i, k):
                dve.wait_ge(rt_ready, i + 1)
                after(dve, u_ready, i - 1)
                dve.tensor_scalar(ct[:, k:k + 1], rt[:, k:k + 1], AM, 1.0, ALU.mult, ALU.min).then_inc(ct_ready, 1)
                dve.wait_ge(qkv_psum, i + 1)
                dve.wait_ge(ct_ready, i + 1)
                after(dve, qk_ready, 2 * i)
                after(dve, v_ready, i)
                after(dve, u_squared, i)
                dve.scalar_tensor_tensor(out=u[:, :], in0=p_qkv[:, 0:3 * D], scalar=ct[:, k:k + 1],
                                         in1=bqkv[:, :], op0=ALU.mult, op1=ALU.add).then_inc(u_ready, 1)

            def sum_squares(i):
                dve.wait_ge(u_squared, i + 1)
                after(dve, roots_ready, i)
                dve.tensor_reduce(hs[:, 0:3 * H], usq[:, :].rearrange("p (a d) -> p a d", d=HD), AX.X, ALU.add).then_inc(heads_summed, 1)
                dve.wait_ge(heads_summed, i + 1)
                dve.tensor_reduce(hs[:, 3 * H:NF], hs[:, 0:3 * H].rearrange("p (a h) -> p a h", h=H), AX.X, ALU.add).then_inc(rows_summed, 1)

            def normalise(i):
                dve.wait_ge(o_psum, i + 1)
                after(dve, o_ready, i)
                oh = p_to[:, 0:H * VW].rearrange("p (h n) -> p h n", n=VW)
                dve.reciprocal(rden[:, :].unsqueeze(2), oh[:, :, HD:VW]).then_inc(rden_ready, 1)
                dve.wait_ge(rden_ready, i + 1)
                after(dve, oT_psum, i)
                dve.tensor_tensor(o[:, :].rearrange("p (h n) -> p h n", n=HD), oh[:, :, 0:HD],
                                  rden[:, :].unsqueeze(2).broadcast_to([P, H, HD]), ALU.mult).then_inc(o_ready, 1)

            def gate_z(i, k, half):
                dve.wait_ge(z_psum, i + 1)
                after(dve, z_squared, i)
                after(dve, zg_ready, i)
                dve.tensor_tensor(z[:, :], p_oz[:, 0:D], bo[:, :], ALU.add).then_inc(z_ready, 1)
                dve.wait_ge(z_ready, i + 1)
                dve.wait_ge(gate_in[k], 32 * half + 32)
                after(dve, stats_kept, i)
                dve.scalar_tensor_tensor(out=tile_of(g_all, i), in0=z[:, :], scalar=1.0, in1=gate[:, k, :],
                                         op0=ALU.mult, op1=ALU.mult, accum_out=st[:, 1:2]).then_inc(zg_ready, 1)
                dve.wait_ge(zg_ready, i + 1)
                after(dve, xg_summed, i)
                dve.scalar_tensor_tensor(out=junk[:, 3, :], in0=tile_of(x_all, i), scalar=1.0, in1=tile_of(g_all, i),
                                         op0=ALU.mult, op1=ALU.mult, accum_out=st[:, 2:3]).then_inc(xg_summed, 1)

            qz_out = bass.AP(qz[:, :, :].tensor, 0, [[2 * D, P], [32, 8], [D + 16, 2], [1, 16]])

            def scale_heads(i, k):
                dve.wait_ge(roots_ready, i + 1)
                after(dve, fac_ready, i)
                dve.tensor_tensor(rlim[:, :], roots[:, 3 * H:NF], c_lim[:, :], ALU.min).then_inc(rlim_ready, 1)
                dve.wait_ge(rlim_ready, i + 1)
                after(dve, qk_ready, 2 * i)
                after(dve, v_ready, i)
                dve.tensor_tensor(fac[:, :].rearrange("p (a h) -> p a h", a=3),
                                  roots[:, 0:3 * H].rearrange("p (a h) -> p a h", a=3),
                                  rlim[:, :].unsqueeze(2).broadcast_to([P, 3, H]), ALU.min).then_inc(fac_ready, 1)
                dve.wait_ge(fac_ready, i + 1)
                after(dve, qkT_psum, i)
                dve.tensor_tensor(qz_out, u[:, 0:D].rearrange("p (g l d) -> p g l d", l=2, d=HD),
                                  fac[:, 0:H].rearrange("p (g l) -> p g l", l=2).unsqueeze(3).broadcast_to([P, 8, 2, HD]),
                                  ALU.mult).then_inc(qk_ready, 1)
                dve.tensor_tensor(kk[:, :].rearrange("p (h d) -> p h d", d=HD), u[:, D:2 * D].rearrange("p (h d) -> p h d", d=HD),
                                  fac[:, H:2 * H].unsqueeze(2).broadcast_to([P, H, HD]), ALU.mult).then_inc(qk_ready, 1)
                after(dve, o_psum, i - 1)
                dve.tensor_tensor(v[:, k, :, 0:HD], u[:, 2 * D:3 * D].rearrange("p (h d) -> p h d", d=HD),
                                  fac[:, 2 * H:3 * H].unsqueeze(2).broadcast_to([P, H, HD]), ALU.mult).then_inc(v_ready, 1)

            def slot(h, off):
                if on(h, off, L_L):
                    normalise(2 * h + off - L_L)
                if on(h, off, L_D):
                    project(2 * h + off - L_D, (off - L_D) % 2)
                if on(h, off, L_A):
                    modulate(2 * h + off - L_A, (off - L_A) % 2, h + (off - L_A) // 2)
                if on(h, off, L_D):
                    sum_squares(2 * h + off - L_D)
                if on(h, off, L_L):
                    gate_z(2 * h + off - L_L, (off - L_L) % 2, h + (off - L_L) // 2)
                if on(h, off, L_D):
                    scale_heads(2 * h + off - L_D, (off - L_D) % 2)

            run_tiles(dve, slot)

            dve.wait_ge(stats_kept, T)
            sm = lambda k: stats[:, :, k]
            step(dve.tensor_scalar(row(W0), sm(0), EPS2, None, ALU.max))
            rsq(W4)
            ts(W4, W4, AM, ALU.mult, 1.0, ALU.min)
            tt(W5, W4, W4, ALU.mult)
            add(W0, row(W5), sm(3), ALU.mult)
            ts(W0, W0, EPS2, ALU.max)
            rsq(W6)
            tt(W7, W0, W6, ALU.mult)
            ask()
            tt(W8, W8, W6, ALU.mult)
            tt(W9, W8, W4, ALU.mult)
            tt(W10, W9, W9, ALU.mult)
            add(W10, row(W10), sm(3), ALU.mult)
            add(W11, row(W9), sm(2), ALU.mult)
            ts(W11, W11, 2.0, ALU.mult, 1.0, ALU.add)
            tt(W12, XX, W10, ALU.mult)
            tt(W12, W12, W11, ALU.add)
            ts(W12, W12, EPS, ALU.max)
            step(dve.reciprocal(row(W12), row(W12)))
            tt(W13, W11, W10, ALU.add)
            tt(ALPHA, W13, W12, ALU.mult)
            tt(W13, OMX, W9, ALU.mult)
            tt(BETA, W13, W12, ALU.mult)
            step(dve.tensor_scalar(row(W9), sm(1), 1.0 / D, None, ALU.mult))
            tt(W10, W9, W9, ALU.mult)
            step(dve.scalar_tensor_tensor(out=row(W10), in0=sm(3), scalar=1.0 / D, in1=row(W10), op0=ALU.mult, op1=ALU.subtract))
            tt(W11, W9, MEAN, ALU.mult)
            step(dve.scalar_tensor_tensor(out=row(W11), in0=sm(2), scalar=1.0 / D, in1=row(W11), op0=ALU.mult, op1=ALU.subtract))
            tt(W12, ALPHA, MEAN, ALU.mult)
            tt(W13, BETA, W9, ALU.mult)
            tt(MEAN1, W12, W13, ALU.add)
            tt(W12, ALPHA, ALPHA, ALU.mult)
            tt(W13, ALPHA, BETA, ALU.mult)
            tt(W14, BETA, BETA, ALU.mult)
            tt(W9, W12, VAR, ALU.mult)
            tt(W10, W14, W10, ALU.mult)
            tt(W9, W9, W10, ALU.add)
            tt(W11, W13, W11, ALU.mult)
            stt(W9, W11, 2.0, W9, ALU.mult, ALU.add)
            ts(VAR, W9, 0.0, ALU.max)
            tt(W9, W12, XX, ALU.mult)
            add(W10, row(W14), sm(3), ALU.mult)
            tt(W9, W9, W10, ALU.add)
            add(W10, row(W13), sm(2), ALU.mult)
            stt(W9, W10, 2.0, W9, ALU.mult, ALU.add)
            ts(XX1, W9, 0.0, ALU.max)
            ts(OMX1, XX1, -1.0, ALU.mult, 1.0, ALU.add)
            log_map_factor(W12, XX1)
            norm_factor(R2, W12, VAR)
            dve.drain().then_inc(factors_made, 1)

            def first_sum(i, j):
                n = 2 * i + j
                dve.wait_ge(xa_ready, n + 1)
                g = tile_of(g_all, n)
                dve.scalar_tensor_tensor(out=g, in0=g, scalar=arrays[:, BETA, bass.ds(n, 1)], in1=xa[:, j, :],
                                         op0=ALU.mult, op1=ALU.add).then_inc(x1_ready, 1)

            def modulate2(i, j, k):
                n = 2 * i + j
                dve.wait_ge(mod2_in[j], 32 * i + 32)
                dve.wait_ge(x1_ready, n + 1)
                after(dve, t2_ready, n)
                dve.scalar_tensor_tensor(out=lnx[:, :], in0=tile_of(g_all, n), scalar=arrays[:, MEAN1, bass.ds(n, 1)],
                                         in1=mod[:, j, D:2 * D], op0=ALU.subtract, op1=ALU.mult).then_inc(ln2_half, 1)
                dve.wait_ge(ln2_half, n + 1)
                after(dve, t2T_psum, i - 1)
                after(dve, t2_squared, n - 3)
                after(dve, qf_ready, n - 3)
                dve.scalar_tensor_tensor(out=t2[:, k, j, :], in0=lnx[:, :], scalar=arrays[:, R2, bass.ds(n, 1)],
                                         in1=mod[:, j, 0:D], op0=ALU.mult, op1=ALU.add).then_inc(t2_ready, 1)

            def inner_square(i, k):
                bank, tw = (p_qkv, p_s)[k], s_bank[2 + k]
                for j in range(2):
                    n = 2 * i + j
                    dve.wait_ge(ff_psum, n + 1)
                    after(dve, qf_ready, n - 1)
                    after(dve, hh_half, n - 1)
                    dve.scalar_tensor_tensor(out=junk2[:, 3, j, :], in0=bank[:, 512 * j + D:512 * j + 2 * D], scalar=1.0,
                                             in1=t2[:, k, j, :], op0=ALU.mult, op1=ALU.mult,
                                             accum_out=qf[:, j:j + 1]).then_inc(qf_ready, 1)
                dve.wait_ge(rt2_ready, i + 1)
                after(dve, ca_ready, i - 1)
                dve.tensor_scalar(ct2[:, k, :], rt2[:, :], AM, 1.0, ALU.mult, ALU.min).then_inc(ct2_ready, 1)
                dve.wait_ge(ct2_ready, i + 1)
                for j in range(2):
                    dve.wait_ge(qf_ready, 2 * i + j + 1)
                    after(dve, hh_ready, i)
                    dve.scalar_tensor_tensor(out=hh[:, 0, j:j + 1], in0=qf[:, j:j + 1], scalar=ct2[:, k, j:j + 1],
                                             in1=tw[:, j:j + 1], op0=ALU.mult, op1=ALU.add).then_inc(hh_half, 1)
                dve.wait_ge(hh_half, 2 * i + 2)
                after(dve, rh_ready, i)
                dve.tensor_tensor(hh[:, 2, :], hh[:, 0, :], ct2[:, k, :], ALU.mult).then_inc(hh_scaled, 1)
                dve.wait_ge(hh_scaled, i + 1)
                dve.tensor_scalar(hh[:, 1, :], hh[:, 2, :], bb[:, 0:1], None, ALU.add).then_inc(hh_ready, 1)

            def inner_factors(i, k):
                dve.wait_ge(rh_ready, i + 1)
                after(dve, ff_ready, 2 * i)
                after(dve, ca_ready, i)
                dve.tensor_scalar(ch[:, :], rh[:, :], AM, 1.0, ALU.mult, ALU.min).then_inc(ch_ready, 1)
                dve.wait_ge(ch_ready, i + 1)
                dve.tensor_tensor(ca[:, :], ch[:, :], ct2[:, k, :], ALU.mult).then_inc(ca_ready, 1)

            def mlp_output(i, j, k):
                n = 2 * i + j
                dve.wait_ge(ca_ready, i + 1)
                after(dve, ff_ready, n - 1)
                dve.scalar_tensor_tensor(out=f1[:, j, :], in0=(p_qkv, p_s)[k][:, 512 * j:512 * j + D], scalar=ca[:, j:j + 1],
                                         in1=b2[:, :], op0=ALU.mult, op1=ALU.add).then_inc(f1_ready, 1)
                dve.wait_ge(f1_ready, n + 1)
                after(dve, ff_squared, n - 1)
                after(dve, fg_ready, n - 1)
                dve.scalar_tensor_tensor(out=ff[:, j, :], in0=b12[:, :], scalar=ch[:, j:j + 1], in1=f1[:, j, :],
                                         op0=ALU.mult, op1=ALU.add).then_inc(ff_ready, 1)
                dve.wait_ge(ff_ready, n + 1)
                dve.wait_ge(gate2_in[j], 32 * i + 32)
                after(dve, yo_ready, n - 1)
                after(dve, xf_summed, n - 1)
                after(dve, fg_squared, n - 1)
                dve.tensor_tensor(fg[:, j, :], ff[:, j, :], gate[:, j, :], ALU.mult).then_inc(fg_ready, 1)
                dve.wait_ge(fg_ready, n + 1)
                after(dve, parts_ready, 3 * i)
                dve.scalar_tensor_tensor(out=junk[:, j, :], in0=tile_of(g_all, n), scalar=1.0, in1=fg[:, j, :],
                                         op0=ALU.mult, op1=ALU.mult, accum_out=fst[:, 2, j:j + 1]).then_inc(xf_summed, 1)

            def output_clip(i):
                dve.wait_ge(rf_ready, i + 1)
                after(dve, parts_ready, 3 * i)
                dve.tensor_scalar(cf[:, :], rf[:, :], AM, 1.0, ALU.mult, ALU.min).then_inc(cf_ready, 1)

            def sum_factors(i):
                dve.wait_ge(parts_ready, 3 * i + 3)
                dve.wait_ge(fin_step, FIN_STEPS * i + FIN_STEPS)
                after(dve, al2_ready, i)
                after(dve, be2_ready, i)
                dve.tensor_tensor(den[:, 0, :], parts[:, 0, :], fin[:, 10, :], ALU.add).then_inc(den_step, 1)
                dve.wait_ge(den_step, 3 * i + 1)
                dve.tensor_scalar(den[:, 1, :], den[:, 0, :], EPS, None, ALU.max).then_inc(den_step, 1)
                dve.wait_ge(den_step, 3 * i + 2)
                dve.reciprocal(den[:, 2, :], den[:, 1, :]).then_inc(den_step, 1)
                dve.wait_ge(den_step, 3 * i + 3)
                after(dve, xo_ready, 2 * i)
                after(dve, yo_ready, 2 * i)
                dve.tensor_tensor(al2[:, :], parts[:, 1, :], den[:, 2, :], ALU.mult).then_inc(al2_ready, 1)
                dve.tensor_tensor(be2[:, :], parts[:, 2, :], den[:, 2, :], ALU.mult).then_inc(be2_ready, 1)

            def second_sum(i, j):
                n = 2 * i + j
                dve.wait_ge(be2_ready, i + 1)
                dve.wait_ge(xo_ready, n + 1)
                after(dve, out_ready, n - 1)
                dve.scalar_tensor_tensor(out=yo[:, j, :], in0=fg[:, j, :], scalar=be2[:, j:j + 1], in1=xo[:, j, :],
                                         op0=ALU.mult, op1=ALU.add).then_inc(yo_ready, 1)

            def slot2(h, off):
                if on2(h, off, M_C):
                    output_clip(2 * h + off - M_C)
                if on2(h, off, M_A):
                    i, k = 2 * h + off - M_A, (off - M_A) % 2
                    for j in range(2):
                        first_sum(i, j)
                        modulate2(i, j, k)
                if on2(h, off, M_B):
                    inner_square(2 * h + off - M_B, (off - M_B) % 2)
                if on2(h, off, M_C):
                    sum_factors(2 * h + off - M_C)
                    for j in range(2):
                        second_sum(2 * h + off - M_C, j)
                if on2(h, off, M_B):
                    i, k = 2 * h + off - M_B, (off - M_B) % 2
                    inner_factors(i, k)
                    for j in range(2):
                        mlp_output(i, j, k)

            run_pairs(dve, slot2)


_WEIGHTS = ["w_q", "b_q", "w_k", "b_k", "w_v", "b_v", "w_o", "b_o", "w_f1", "b_f1", "w_f2", "b_f2", "w_ada", "b_ada"]
_INS = ["x", "cond_1024"] + ["L0_cond_" + n for n in _WEIGHTS]


def kernel(**inputs):
    import concourse.bacc as bacc
    from concourse.bass_utils import run_bass_kernel_spmd

    nc = bacc.Bacc("TRN2", target_bir_lowering=False, num_devices=1)
    arrays, args = {}, []
    for name in _INS:
        a = np.ascontiguousarray(inputs[name])
        arrays[f"in_{name}"] = a
        args.append(nc.dram_tensor(f"in_{name}", a.shape, mybir.dt.from_np(a.dtype), kind="ExternalInput").ap())
    out = nc.dram_tensor("out", inputs["x"].shape, F32, kind="ExternalOutput").ap()
    build(nc, *args, out)
    r = run_bass_kernel_spmd(nc, [arrays], core_ids=[0])
    return r.results[0]["out"]
```

```python
import math
from contextlib import ExitStack

import numpy as np

import concourse.bass as bass
from concourse import mybir

F32 = mybir.dt.float32
BF16 = mybir.dt.bfloat16
F16 = mybir.dt.float16
ALU = mybir.AluOpType
ACT = mybir.ActivationFunctionType
AX = mybir.AxisListType

P = 128
EPS = 1e-7
EPS2 = 1e-14
LN_TINY = 1e-18
LN_EPS = 1e-6
MAX_ARG = float(np.float32(1.0 - 1e-5))
AM = 0.5 * math.log((1 + MAX_ARG) / (1 - MAX_ARG))
QK_UP = 64.0
SERIES_BELOW = 0.25


def _beta(a, b):
    return math.exp(math.lgamma(a) + math.lgamma(b) - math.lgamma(a + b))


def after(eng, sem, count):
    if isinstance(count, int) and count <= 0:
        return
    eng.wait_ge(sem, count)


def build(nc, x, cond, w_q, b_q, w_k, b_k, w_v, b_v, w_o, b_o, w_f1, b_f1, w_f2, b_f2, w_ada, b_ada, out):
    B, S, D = x.shape
    FF = w_f1.shape[1]
    H = 16
    HD = D // H
    C = D // P
    FC = FF // P
    TB = P // S
    T = B // TB
    HALF = T // 2
    RATIO = _beta(HD / 2, 0.5) / _beta(D / 2, 0.5)
    G = H // 2
    VW = HD + 1
    NF = 3 * H + 3
    SCALE = 1.0 / math.sqrt(HD)
    assert TB == 2 and C == 2 and H == 16 and HD == 16

    with ExitStack() as ctx:
        def sb(name, shape, dt=F32):
            return ctx.enter_context(nc.sbuf_tensor(name, shape, dt))

        def ps(name, shape):
            return ctx.enter_context(nc.psum_tensor(name, shape, F32))

        def sem(name):
            return ctx.enter_context(nc.semaphore(name))

        mod_dram = nc.dram_tensor("mod_rows", (B, 6 * D), F32).ap()

        x_all = sb("x_all", [P, T, D])
        g_all = sb("g_all", [P, T, D])
        flat = g_all[:, :, :].rearrange("p t d -> p (t d)")
        at = [0]

        def scratch(n):
            at[0] += n
            return flat[:, at[0] - n:at[0]]

        w1 = scratch(C * FF).rearrange("p (c n) -> p c n", c=C)
        w1T = scratch(FC * D).rearrange("p (c n) -> p c n", c=FC)
        w2 = scratch(FC * D).rearrange("p (c n) -> p c n", c=FC)
        b1rep = scratch(FC * P).rearrange("p (c n) -> p c n", c=FC)
        wada = scratch(C * 6 * D).rearrange("p (c n) -> p c n", c=C)
        bada = scratch(6 * D)
        ada = scratch(6 * D)
        condr = scratch(D)
        condT = scratch(D).rearrange("p (c n) -> p c n", c=C)
        b1col = scratch(FC)
        b1row = scratch(P)[0:FC, :]

        wqkv = sb("wqkv", [P, C, 3 * D])
        wo = sb("wo", [P, C, D])
        wff = sb("wff", [P, C, 2 * D])
        w1b = sb("w1b", [P, C])
        bqkv = sb("bqkv", [P, 3 * D])
        bo = sb("bo", [P, D])
        b2 = sb("b2", [P, D])
        b12 = sb("b12", [P, D])
        bb = sb("bb", [P, 1])
        ident = sb("ident", [P, P])
        ident16 = sb("ident16", [P, P], F16)

        bn = sb("bn", [P, T, 6])
        arrays = sb("arrays", [P, 26, T])
        stats = sb("stats", [P, T, 4])

        mod = sb("mod", [P, 2, 2 * D])
        gate = sb("gate", [P, 2, D])
        lnx = sb("lnx", [P, D])
        t = sb("t", [P, D])
        tT = sb("tT", [P, 2, C, P])
        u = sb("u", [P, 2, 3 * D])
        usq = sb("usq", [P, 3 * D])
        ss_t = sb("ss_t", [P, 2])
        rt = sb("rt", [P, 2])
        ct = sb("ct", [P, 2])
        hs = sb("hs", [P, NF])
        lnh = sb("lnh", [P, NF])
        y0 = sb("y0", [P, NF])
        nw = sb("nw", [P, 4, NF])
        roots = sb("roots", [P, NF])
        rlim = sb("rlim", [P, 3])
        fac = sb("fac", [P, 3 * H])
        qk = sb("qk", [P, 2 * D])
        qk4 = sb("qk4", [P, 2, H, 4, HD], F16)
        v = sb("v", [P, 2, H, TB, VW])
        qkT = sb("qkT", [P, 2, G, P], F16)
        pT = sb("pT", [P, 2, G, S])
        rden = sb("rden", [S, H, TB])
        o = sb("o", [S, TB, H, HD])
        oT = sb("oT", [P, C, P])
        z = sb("z", [P, D])
        st = sb("st", [P, 4])
        junk = sb("junk", [P, 4, D], BF16)

        c_fac = sb("c_fac", [P, NF])
        c_lim = sb("c_lim", [P, 3])
        c_three = sb("c_three", [P, NF])
        c_mhalf = sb("c_mhalf", [P, 2])
        c_half = sb("c_half", [P, 2])
        c_one = sb("c_one", [P, 2])
        c_two = sb("c_two", [P, 2])
        c_eps2 = sb("c_eps2", [P, 2])
        c_tiny = sb("c_tiny", [P, 1])

        f1, ff = (pT[:, n, :, :].rearrange("p g n -> p (g n)").rearrange("p (j d) -> p j d", j=2) for n in range(2))
        fg = qk[:, :].rearrange("p (j d) -> p j d", j=2)
        xo = u[:, 0, 0:2 * D].rearrange("p (j d) -> p j d", j=2)
        yo = usq[:, 0:2 * D].rearrange("p (j d) -> p j d", j=2)
        xa = sb("xa", [P, 2, D])
        t2 = qkT[:, :, :, :].rearrange("p a g n -> p (a g n)").bitcast(F32).rearrange(
            "p (k j d) -> p k j d", k=2, j=2)
        t2T = qk4[:, :, :, :, :].rearrange("p a h r d -> p (a h r d)").bitcast(F32).rearrange(
            "p (k j c n) -> p k j c n", k=2, j=2, c=C)
        ss2 = sb("ss2", [P, 2])
        rt2 = sb("rt2", [P, 2])
        ct2 = sb("ct2", [P, 2, 2])
        rh = sb("rh", [P, 2])
        rf = sb("rf", [P, 2])
        cf = sb("cf", [P, 2])
        parts = sb("parts", [P, 3, 2])
        den = sb("den", [P, 3, 2])
        qf = sb("qf", [P, 2])
        hh = sb("hh", [P, 3, 2])
        ch = sb("ch", [P, 2])
        ca = sb("ca", [P, 2])
        fst = sb("fst", [P, 3, 2])
        fin = sb("fin", [P, 11, 2])
        na = sb("na", [P, 2])
        th = sb("th", [P, 2])
        al2 = sb("al2", [P, 2])
        be2 = sb("be2", [P, 2])
        junk2 = wqkv[:, :, :].rearrange("p c n -> p (c n)")[:, 0:4 * D].bitcast(BF16).rearrange(
            "p (a j d) -> p a j d", a=4, j=2)

        p_t = ps("p_t", [P, 512])
        p_o = ps("p_o", [P, 1024])
        p_oz = ps("p_oz", [P, 512])
        p_qkv = ps("p_qkv", [P, 1024])
        p_s = ps("p_s", [P, 1024])
        s_bank = [p_s[:, 0:512], p_s[:, 512:1024], p_o[:, 0:512], p_o[:, 512:1024]]
        p_qkT = p_s[:, :].bitcast(F16).rearrange("p (a g n) -> p a g n", a=2, g=G)

        cond_in = sem("cond_in"); wada_in = sem("wada_in"); bada_in = sem("bada_in")
        w1_in = sem("w1_in"); w2_in = sem("w2_in"); b1_in = sem("b1_in")
        wqkv_in = sem("wqkv_in"); rows_in = sem("rows_in")
        x_in = [sem(f"x_in{k}") for k in range(8)]
        ident_made = sem("ident_made"); ident16_made = sem("ident16_made"); consts_made = sem("consts_made")
        condT_psum = sem("condT_psum"); condT_made = sem("condT_made")
        ada_psum = sem("ada_psum"); ada_made = sem("ada_made"); ada_plus = sem("ada_plus")
        ada_stored = sem("ada_stored")
        w1T_psum = sem("w1T_psum"); w1T_made = sem("w1T_made"); b1rep_made = sem("b1rep_made")
        ffw_psum = sem("ffw_psum"); ffw_made = sem("ffw_made")
        zeros_set = sem("zeros_set")
        bn_done = sem("bn_done")
        vec_step = sem("vec_step"); vec_asks = sem("vec_asks"); act_answers = sem("act_answers")
        mod_in = [sem(f"mod_in{k}") for k in range(2)]
        gate_in = [sem(f"gate_in{k}") for k in range(2)]
        ln_half = sem("ln_half"); t_ready = sem("t_ready"); t_squared = sem("t_squared")
        rt_ready = sem("rt_ready"); ln_rows = sem("ln_rows"); ct_ready = sem("ct_ready")
        tT_psum = sem("tT_psum"); tT_ready = sem("tT_ready")
        qkv_psum = sem("qkv_psum"); u_ready = sem("u_ready"); u_squared = sem("u_squared")
        heads_summed = sem("heads_summed"); rows_summed = sem("rows_summed"); roots_ready = sem("roots_ready"); rlim_ready = sem("rlim_ready")
        ln_taken = sem("ln_taken"); y0_ready = sem("y0_ready"); newton = sem("newton"); fac_ready = sem("fac_ready")
        qk_ready = sem("qk_ready"); high_ready = sem("high_ready"); low_ready = sem("low_ready"); again_ready = sem("again_ready"); v_ready = sem("v_ready")
        qkT_psum = sem("qkT_psum"); qkT_ready = sem("qkT_ready")
        s_psum = sem("s_psum"); p_ready = sem("p_ready")
        o_psum = sem("o_psum"); rden_ready = sem("rden_ready"); o_ready = sem("o_ready")
        oT_psum = sem("oT_psum"); oT_ready = sem("oT_ready")
        z_psum = sem("z_psum"); z_ready = sem("z_ready"); zg_ready = sem("zg_ready")
        xg_summed = sem("xg_summed"); z_squared = sem("z_squared"); zg_squared = sem("zg_squared")
        stats_kept = sem("stats_kept")
        factors_made = sem("factors_made")
        mod2_in = [sem(f"mod2_in{k}") for k in range(2)]
        gate2_in = [sem(f"gate2_in{k}") for k in range(2)]
        xa_ready = sem("xa_ready"); x1_ready = sem("x1_ready"); ln2_half = sem("ln2_half")
        t2_ready = sem("t2_ready"); t2_squared = sem("t2_squared"); rt2_ready = sem("rt2_ready"); rh_ready = sem("rh_ready"); rf_ready = sem("rf_ready"); cf_ready = sem("cf_ready"); parts_ready = sem("parts_ready"); den_step = sem("den_step")
        ct2_ready = sem("ct2_ready"); t2T_psum = sem("t2T_psum"); t2T_ready = sem("t2T_ready")
        ff_psum = sem("ff_psum"); qf_ready = sem("qf_ready"); hh_half = sem("hh_half"); hh_scaled = sem("hh_scaled"); hh_ready = sem("hh_ready")
        ch_ready = sem("ch_ready"); ca_ready = sem("ca_ready")
        f1_ready = sem("f1_ready"); ff_ready = sem("ff_ready"); fg_ready = sem("fg_ready")
        ff_squared = sem("ff_squared"); fg_squared = sem("fg_squared"); xf_summed = sem("xf_summed")
        fin_step = sem("fin_step"); na_ready = sem("na_ready"); th_ready = sem("th_ready")
        al2_ready = sem("al2_ready"); be2_ready = sem("be2_ready"); xo_ready = sem("xo_ready"); yo_ready = sem("yo_ready")
        out_ready = sem("out_ready"); out_stored = sem("out_stored")

        (MEAN, VAR, XX, R1, OMX, ALPHA, BETA, MEAN1, R2, XX1, OMX1, W0, W1_, W2_, W3, W4, W5, W6, W7, W8,
         W9, W10, W11, W12, W13, W14) = range(26)

        def row(k):
            return arrays[:, k, :]

        x_t = x.rearrange("(t b) s d -> (b s) t d", b=TB)
        out_t = out.rearrange("(t b) s d -> (b s) t d", b=TB)

        def bcast(vec, n):
            return vec.rearrange("(a n) -> a n", a=1).broadcast_to([P, n])

        def mod_rows(i, lo, hi, b):
            return mod_dram[bass.ds(TB * i + b, 1), lo:hi].broadcast_to([S, hi - lo])

        L_A, L_B, L_C, L_D, L_E, L_H, L_L = 0, 1, 2, 3, 4, 5, 6
        FIRST = 8
        M_A, M_B, M_C = 0, 1, 2
        FIRST2 = 4
        FIN_STEPS = 11

        def run_slots(eng, slot, first, items, slots):
            for s in range(first):
                slot(s // 2, s % 2)
            with eng.Fori(first // 2, items // 2) as h:
                slot(h, 0)
                slot(h, 1)
            for s in range(items, slots):
                slot(s // 2, s % 2)

        def count(n):
            return min(n, T) if isinstance(n, int) else n

        def run_tiles(eng, slot):
            run_slots(eng, slot, FIRST, T, T + L_L)

        def run_pairs(eng, slot):
            run_slots(eng, slot, FIRST2, HALF, HALF + M_C)

        def on(h, off, lag, items=T):
            return not isinstance(h, int) or 0 <= 2 * h + off - lag < items

        def on2(h, off, lag):
            return on(h, off, lag, HALF)

        block = ctx.enter_context(nc.Block())

        @block.sync
        def _(sp):
            sp.dma_start(condr, cond[:, :]).then_inc(cond_in, 16)
            sp.dma_start(wada, w_ada.rearrange("(c p) n -> p c n", p=P)).then_inc(wada_in, 16)
            sp.dma_start(bada, bcast(b_ada, 6 * D)).then_inc(bada_in, 16)
            for k in range(8):
                n = T // 8
                sp.dma_start(x_all[:, n * k:n * k + n, :], x_t[:, n * k:n * k + n, :]).then_inc(x_in[k], 16)
            sp.wait_ge(ada_plus, 2)
            sp.dma_start(mod_dram[:, :], ada).then_inc(ada_stored, 16)
            sp.wait_ge(ada_stored, 16)

            def slot(h, off):
                if on(h, off, L_A):
                    i, k = 2 * h + off, off % 2
                    after(sp, t_ready, i - 1)
                    for b in range(TB):
                        sp.dma_start(mod[S * b:S * b + S, k, 0:2 * D], mod_rows(i, 0, 2 * D, b)).then_inc(mod_in[k], 16)
                if on(h, off, L_H):
                    i, k = 2 * h + off - L_H, (off - L_H) % 2
                    after(sp, zg_ready, i - 1)
                    for b in range(TB):
                        sp.dma_start(gate[S * b:S * b + S, k, :], mod_rows(i, 2 * D, 3 * D, b)).then_inc(gate_in[k], 16)

            run_tiles(sp, slot)

            def slot2(h, off):
                if on2(h, off, M_A):
                    i = 2 * h + off - M_A
                    after(sp, t2_ready, 2 * i)
                    for j in range(2):
                        for b in range(TB):
                            sp.dma_start(mod[S * b:S * b + S, j, :], mod_rows(2 * i + j, 3 * D, 5 * D, b)).then_inc(mod2_in[j], 16)
                if on2(h, off, M_B):
                    i = 2 * h + off - M_B
                    after(sp, fg_ready, 2 * i)
                    for j in range(2):
                        for b in range(TB):
                            sp.dma_start(gate[S * b:S * b + S, j, :], mod_rows(2 * i + j, 5 * D, 6 * D, b)).then_inc(gate2_in[j], 16)
                if on2(h, off, M_C):
                    i = 2 * h + off - M_C
                    sp.wait_ge(out_ready, 2 * i + 2)
                    sp.dma_start(out_t[:, bass.ds(2 * i, 2), :], x_all[:, bass.ds(2 * i, 2), :]).then_inc(out_stored, 16)

            sp.wait_ge(t_ready, T)
            sp.wait_ge(zg_ready, T)
            run_pairs(sp, slot2)
            sp.wait_ge(out_stored, 16 * HALF)

        @block.gpsimd
        def _(pool):
            pool.memset(ident[:, :], 0.0).then_inc(ident_made, 1)
            pool.wait_ge(ident_made, 1)
            pool.affine_select(out=ident[:, :], in_=ident[:, :], compare_op=ALU.not_equal, fill=1.0,
                               base=0, pattern=[[-1, P]], channel_multiplier=1).then_inc(ident_made, 1)
            pool.memset(c_fac[:, 0:2 * H], -0.5 * AM * QK_UP)
            pool.memset(c_fac[:, 2 * H:3 * H], -0.5 * AM / RATIO)
            pool.memset(c_fac[:, 3 * H:3 * H + 2], -0.5 * AM * RATIO * QK_UP)
            pool.memset(c_fac[:, 3 * H + 2:NF], -0.5 * AM)
            pool.memset(c_lim[:, 0:2], RATIO * QK_UP)
            pool.memset(c_lim[:, 2:3], 1.0)
            pool.memset(c_three[:, :], 3.0)
            pool.memset(c_mhalf[:, :], -0.5)
            pool.memset(c_half[:, :], 0.5)
            pool.memset(c_one[:, :], 1.0)
            pool.memset(c_two[:, :], 2.0)
            pool.memset(c_eps2[:, :], EPS2)
            pool.memset(c_tiny[:, :], LN_TINY).then_inc(consts_made, 1)
            pool.wait_ge(consts_made, 1)
            for n, (b, c, value) in enumerate(((0, 0, 1.0), (0, 1, 0.0), (1, 0, 0.0), (1, 1, 1.0))):
                after(pool, zeros_set, n)
                pool.memset(v[S * b:S * b + S, :, :, c, :], value).then_inc(zeros_set, 1)
            pool.dma_start(wo[:, :, :], w_o.rearrange("(c p) n -> p c n", p=P)).then_inc(rows_in, 16)
            pool.dma_start(bo[:, :], bcast(b_o, D)).then_inc(rows_in, 16)
            pool.dma_start(b2[:, :], bcast(b_f2, D)).then_inc(rows_in, 16)

            def token_root(i, k):
                pool.wait_ge(t_squared, i + 1)
                after(pool, ct_ready, i - 1)
                pool.tensor_tensor(rt[:, k:k + 1], ss_t[:, k:k + 1], c_mhalf[:, 0:1], ALU.pow).then_inc(rt_ready, 1)

            def head_roots(i):
                pool.wait_ge(y0_ready, i + 1)
                pool.wait_ge(rows_summed, i + 1)
                after(pool, roots_ready, i)
                pool.tensor_tensor(nw[:, 0, :], y0[:, :], y0[:, :], ALU.mult).then_inc(newton, 1)
                pool.wait_ge(newton, 4 * i + 1)
                pool.tensor_tensor(nw[:, 1, :], nw[:, 0, :], hs[:, :], ALU.mult).then_inc(newton, 1)
                pool.wait_ge(newton, 4 * i + 2)
                pool.tensor_tensor(nw[:, 2, :], nw[:, 1, :], c_three[:, :], ALU.subtract).then_inc(newton, 1)
                pool.wait_ge(newton, 4 * i + 3)
                pool.tensor_tensor(nw[:, 3, :], nw[:, 2, :], y0[:, :], ALU.mult).then_inc(newton, 1)
                pool.wait_ge(newton, 4 * i + 4)
                after(pool, fac_ready, i)
                pool.tensor_tensor(roots[:, :], nw[:, 3, :], c_fac[:, :], ALU.mult).then_inc(roots_ready, 1)

            def low_parts(i):
                pool.wait_ge(high_ready, i + 1)
                pool.wait_ge(qk_ready, 2 * i + 2)
                after(pool, qkT_psum, i)
                low = bass.AP(qk4[:, :, :, :, :].tensor, 2 * HD, [[8 * H * HD, P], [4 * H * HD - HD, 2], [4 * HD, H], [1, HD]])
                pool.tensor_tensor(low, qk[:, :].rearrange("p (a h d) -> p a h d", a=2, d=HD), qk4[:, :, :, 0, :],
                                   ALU.subtract).then_inc(low_ready, 1)

            def keep_stats(i):
                pool.wait_ge(z_squared, i + 1)
                pool.wait_ge(zg_squared, i + 1)
                pool.wait_ge(xg_summed, i + 1)
                pool.tensor_copy(stats[:, bass.ds(i, 1), :].rearrange("p a n -> p (a n)"), st[:, :]).then_inc(stats_kept, 1)

            def slot(h, off):
                if on(h, off, L_E):
                    low_parts(2 * h + off - L_E)
                if on(h, off, L_C):
                    token_root(2 * h + off - L_C, (off - L_C) % 2)
                if on(h, off, L_D):
                    head_roots(2 * h + off - L_D)
                if on(h, off, L_L):
                    keep_stats(2 * h + off - L_L)

            run_tiles(pool, slot)

            def token_roots2(i, k):
                pool.wait_ge(t2_squared, 2 * i + 2)
                after(pool, ct2_ready, i)
                pool.tensor_tensor(rt2[:, :], ss2[:, :], c_mhalf[:, :], ALU.pow).then_inc(rt2_ready, 1)

            def inner_roots(i):
                pool.wait_ge(hh_ready, i + 1)
                after(pool, ch_ready, i)
                pool.tensor_tensor(rh[:, :], hh[:, 1, :], c_mhalf[:, :], ALU.pow).then_inc(rh_ready, 1)

            def output_factors(i):
                step = [FIN_STEPS * i]

                def op(k, a, b, f):
                    pool.tensor_tensor(fin[:, k, :], a, b, f).then_inc(fin_step, 1)
                    step[0] = step[0] + 1
                    pool.wait_ge(fin_step, step[0])
                    return fin[:, k, :]

                pool.wait_ge(ff_squared, 2 * i + 2)
                after(pool, cf_ready, i)
                pool.tensor_tensor(rf[:, :], fst[:, 0, :], c_mhalf[:, :], ALU.pow).then_inc(rf_ready, 1)
                after(pool, be2_ready, i)
                pool.wait_ge(fg_squared, 2 * i + 2)
                pool.wait_ge(cf_ready, i + 1)
                a = op(0, cf[:, :], cf[:, :], ALU.mult)
                a = op(1, a, fst[:, 1, :], ALU.mult)
                nn = op(2, a, c_eps2[:, :], ALU.add)
                after(pool, th_ready, i)
                pool.tensor_tensor(na[:, :], nn, c_half[:, :], ALU.pow).then_inc(na_ready, 1)
                rn = op(3, nn, c_mhalf[:, :], ALU.pow)
                pool.wait_ge(th_ready, i + 1)
                a = op(4, th[:, :], rn, ALU.mult)
                kap = op(5, a, cf[:, :], ALU.mult)
                a = op(6, kap, kap, ALU.mult)
                y2 = op(7, a, fst[:, 1, :], ALU.mult)
                pool.wait_ge(xf_summed, 2 * i + 2)
                a = op(8, kap, fst[:, 2, :], ALU.mult)
                a = op(9, a, c_two[:, :], ALU.mult)
                c1 = op(10, a, c_one[:, :], ALU.add)
                pool.tensor_tensor(parts[:, 0, :], arrays[:, XX1, bass.ds(2 * i, 2)], y2, ALU.mult).then_inc(parts_ready, 1)
                pool.tensor_tensor(parts[:, 1, :], c1, y2, ALU.add).then_inc(parts_ready, 1)
                pool.tensor_tensor(parts[:, 2, :], arrays[:, OMX1, bass.ds(2 * i, 2)], kap, ALU.mult).then_inc(parts_ready, 1)

            def add_x(i, j):
                n = 2 * i + j
                pool.wait_ge(yo_ready, n + 1)
                xt = x_all[:, bass.ds(n, 1), :].rearrange("p a d -> p (a d)")
                pool.tensor_tensor(xt, xt, yo[:, j, :], ALU.add).then_inc(out_ready, 1)

            def slot2(h, off):
                if on2(h, off, M_C):
                    output_factors(2 * h + off - M_C)
                if on2(h, off, M_B):
                    inner_roots(2 * h + off - M_B)
                if on2(h, off, M_A):
                    token_roots2(2 * h + off - M_A, (off - M_A) % 2)
                if on2(h, off, M_C):
                    for j in range(2):
                        add_x(2 * h + off - M_C, j)

            pool.wait_ge(factors_made, 1)
            run_pairs(pool, slot2)

        @block.scalar
        def _(act):
            act.dma_start(w1, w_f1.rearrange("(c p) n -> p c n", p=P)).then_inc(w1_in, 16)
            act.dma_start(w2, w_f2.rearrange("(c p) n -> p c n", p=P)).then_inc(w2_in, 16)
            act.dma_start(b1row, b_f1.rearrange("(c n) -> c n", n=P)).then_inc(b1_in, 16)
            for k, (w, b) in enumerate(((w_q, b_q), (w_k, b_k), (w_v, b_v))):
                act.dma_start(wqkv[:, :, k * D:k * D + D], w.rearrange("(c p) n -> p c n", p=P)).then_inc(wqkv_in, 16)
                act.dma_start(bqkv[:, k * D:k * D + D], bcast(b, D)).then_inc(wqkv_in, 16)
            for k in range(FC // 2):
                act.wait_ge(w1T_psum, k + 1)
                act.activation(w1T[:, 2 * k:2 * k + 2, :].rearrange("p c n -> p (c n)"),
                               s_bank[2 + k % 2][:, :], ACT.Copy).then_inc(w1T_made, 1)

            def rsq():
                asked[0] += 1
                act.wait_ge(vec_asks, asked[0])
                act.activation(row(W1_), row(W0), ACT.Ln).then_inc(ln_rows, 1)
                rsqs[0] += 1
                act.wait_ge(ln_rows, rsqs[0])
                act.activation(row(W2_), row(W1_), ACT.Exp, scale=-0.5).then_inc(act_answers, 1)

            def elementwise(f, src, dst):
                asked[0] += 1
                act.wait_ge(vec_asks, asked[0])
                act.activation(row(dst), row(src), f).then_inc(act_answers, 1)

            asked, rsqs = [0], [0]
            act.wait_ge(consts_made, 1)
            act.preload_act_table_set("natural_log_exp_and_others")
            rsq()
            elementwise(ACT.Ln, W7, W8)
            rsq()

            def high_parts(i):
                act.wait_ge(qk_ready, 2 * i + 2)
                after(act, qkT_psum, i)
                after(act, low_ready, i)
                after(act, again_ready, 2 * i)
                act.activation(qk4[:, :, :, 0, :], qk[:, :].rearrange("p (a h d) -> p a h d", a=2, d=HD), ACT.Copy).then_inc(high_ready, 1)

            def evac_qkT(i):
                act.wait_ge(qkT_psum, i + 1)
                after(act, s_psum, i)
                act.activation(qkT[:, :, :, :].rearrange("p a g n -> p (a g n)"), p_s[:, :].bitcast(F16), ACT.Copy).then_inc(qkT_ready, 1)

            def evac_oT(i):
                act.wait_ge(oT_psum, i + 1)
                after(act, z_psum, i)
                act.activation(oT[:, :, :].rearrange("p c n -> p (c n)"), p_oz[:, 0:D], ACT.Copy).then_inc(oT_ready, 1)

            def evac_tT(i, k):
                act.wait_ge(tT_psum, i + 1)
                after(act, qkv_psum, i - 1)
                act.activation(tT[:, k, :, :].rearrange("p c n -> p (c n)"), p_t[:, 0:D], ACT.Copy).then_inc(tT_ready, 1)

            def square_u(i, k):
                act.wait_ge(u_ready, i + 1)
                after(act, heads_summed, i)
                act.activation(usq[:, :], u[:, k, :], ACT.Square).then_inc(u_squared, 1)

            def square_t(i, k):
                act.wait_ge(t_ready, i + 1)
                after(act, rt_ready, i - 1)
                after(act, t_squared, i)
                act.activation(junk[:, 0, :], t[:, :], ACT.Square, accum_out=ss_t[:, k:k + 1]).then_inc(t_squared, 1)

            def inverse_norms(i):
                act.wait_ge(rows_summed, i + 1)
                after(act, y0_ready, i)
                act.activation(lnh[:, :], hs[:, :], ACT.Ln, bias=c_tiny[:, 0:1]).then_inc(ln_taken, 1)
                act.wait_ge(ln_taken, i + 1)
                after(act, roots_ready, i)
                act.activation(y0[:, :], lnh[:, :], ACT.Exp, scale=-0.5).then_inc(y0_ready, 1)

            def square_z(i):
                act.wait_ge(z_ready, i + 1)
                after(act, stats_kept, i)
                after(act, z_squared, i)
                act.activation(junk[:, 1, :], z[:, :], ACT.Square, accum_out=st[:, 0:1]).then_inc(z_squared, 1)
                act.wait_ge(zg_ready, i + 1)
                after(act, zg_squared, i)
                act.activation(junk[:, 2, :], g_all[:, bass.ds(i, 1), :].rearrange("p a d -> p (a d)"),
                               ACT.Square, accum_out=st[:, 3:4]).then_inc(zg_squared, 1)

            def exp_scores(i):
                act.wait_ge(s_psum, i + 1)
                after(act, o_psum, i)
                act.activation(pT[:, :, :, :].rearrange("p e g n -> p (e g n)"), p_s[:, :],
                               ACT.Exp, scale=SCALE / (QK_UP * QK_UP)).then_inc(p_ready, 1)

            def slot(h, off):
                if on(h, off, L_H):
                    evac_qkT(2 * h + off - L_H)
                if on(h, off, L_B):
                    evac_tT(2 * h + off - L_B, (off - L_B) % 2)
                if on(h, off, L_D):
                    square_u(2 * h + off - L_D, (off - L_D) % 2)
                if on(h, off, L_L):
                    evac_oT(2 * h + off - L_L)
                if on(h, off, L_E):
                    high_parts(2 * h + off - L_E)
                if on(h, off, L_H):
                    exp_scores(2 * h + off - L_H)
                if on(h, off, L_D):
                    inverse_norms(2 * h + off - L_D)
                if on(h, off, L_A):
                    square_t(2 * h + off - L_A, (off - L_A) % 2)
                if on(h, off, L_L):
                    square_z(2 * h + off - L_L)

            run_tiles(act, slot)

            rsq()
            rsq()
            elementwise(ACT.Tanh, W7, W8)
            act.preload_act_table_set("natural_log_exp_and_others")
            rsq()
            elementwise(ACT.Ln, W7, W8)
            rsq()

            def scale_x(i, j):
                n = 2 * i + j
                after(act, x1_ready, n - 1)
                act.activation(xa[:, j, :], x_all[:, bass.ds(n, 1), :].rearrange("p a d -> p (a d)"), ACT.Copy,
                               scale=arrays[:, ALPHA, bass.ds(n, 1)]).then_inc(xa_ready, 1)

            def square_t2(i, j, k):
                n = 2 * i + j
                act.wait_ge(t2_ready, n + 1)
                after(act, rt2_ready, i)
                after(act, t2_squared, n - 1)
                act.activation(junk2[:, 0, j, :], t2[:, k, j, :], ACT.Square, accum_out=ss2[:, j:j + 1]).then_inc(t2_squared, 1)

            def evac_t2T(i, k):
                act.wait_ge(t2T_psum, i + 1)
                after(act, ff_psum, 2 * (i - 1))
                act.activation(t2T[:, k, :, :, :].rearrange("p j c n -> p (j c n)"), p_t[:, :], ACT.Copy).then_inc(t2T_ready, 1)

            def square_ff(i, j):
                n = 2 * i + j
                act.wait_ge(ff_ready, n + 1)
                after(act, parts_ready, 3 * i)
                after(act, ff_squared, n - 1)
                act.activation(junk2[:, 1, j, :], ff[:, j, :], ACT.Square, accum_out=fst[:, 0, j:j + 1]).then_inc(ff_squared, 1)

            def square_fg(i, j):
                n = 2 * i + j
                act.wait_ge(fg_ready, n + 1)
                after(act, fg_squared, n - 1)
                act.activation(junk2[:, 2, j, :], fg[:, j, :], ACT.Square, accum_out=fst[:, 1, j:j + 1]).then_inc(fg_squared, 1)

            def tanh_norm(i):
                act.wait_ge(na_ready, i + 1)
                after(act, parts_ready, 3 * i)
                act.activation(th[:, :], na[:, :], ACT.Tanh).then_inc(th_ready, 1)

            def scale_x1(i, j):
                n = 2 * i + j
                act.wait_ge(al2_ready, i + 1)
                after(act, yo_ready, n - 1)
                act.activation(xo[:, j, :], g_all[:, bass.ds(n, 1), :].rearrange("p a d -> p (a d)"), ACT.Copy,
                               scale=al2[:, j:j + 1]).then_inc(xo_ready, 1)

            def slot2(h, off):
                if on2(h, off, M_A):
                    i, k = 2 * h + off - M_A, (off - M_A) % 2
                    for j in range(2):
                        scale_x(i, j)
                if on2(h, off, M_C):
                    tanh_norm(2 * h + off - M_C)
                if on2(h, off, M_A):
                    for j in range(2):
                        square_t2(i, j, k)
                    evac_t2T(i, k)
                if on2(h, off, M_C):
                    for j in range(2):
                        scale_x1(2 * h + off - M_C, j)
                if on2(h, off, M_B):
                    for j in range(2):
                        square_ff(2 * h + off - M_B, j)
                        square_fg(2 * h + off - M_B, j)

            act.preload_act_table(ACT.Tanh)
            act.wait_ge(factors_made, 1)
            run_pairs(act, slot2)

        @block.tensor
        def _(pe):
            pe.wait_ge(ident_made, 2)
            pe.wait_ge(cond_in, 16)
            for c in range(C):
                pe.transpose(p_t[:, c * P:c * P + P], condr[:, c * P:c * P + P], ident[:, :])
            pe.wait_ge(b1_in, 16)
            pe.transpose(p_t[:, D:D + FC], b1row, ident[0:FC, 0:FC]).then_inc(condT_psum, 1)
            pe.wait_ge(w1_in, 16)
            for k in range(FC // 2):
                after(pe, w1T_made, k - 1)
                for m in range(4):
                    fc, c = 2 * k + m // 2, m % 2
                    mm = pe.transpose(s_bank[2 + k % 2][:, m * P:m * P + P], w1[:, c, fc * P:fc * P + P], ident[:, :])
                mm.then_inc(w1T_psum, 1)
            pe.wait_ge(wada_in, 16)
            pe.wait_ge(condT_made, 1)
            for n, bank in enumerate((p_qkv[:, 0:512], p_qkv[:, 512:1024], p_oz[:, :])):
                for c in range(C):
                    mm = pe.matmul(bank, condT[:, c, :], wada[:, c, n * 512:n * 512 + 512], start=c == 0, stop=c == C - 1)
            mm.then_inc(ada_psum, 1)
            pe.wait_ge(w1T_made, FC // 2)
            pe.wait_ge(w2_in, 16)
            pe.wait_ge(b1rep_made, 2)
            pe.wait_ge(ada_made, 3)

            def inner_sum(dst, lhs, rhs):
                for fc in range(FC):
                    mm = pe.matmul(dst, lhs(fc), rhs(fc), start=fc == 0, stop=fc == FC - 1)
                return mm

            for m in range(C):
                w1Tm = lambda fc: w1T[:, fc, m * P:m * P + P]
                inner_sum(p_s[:, m * 512:m * 512 + D], w1Tm, lambda fc: w2[:, fc, :])
                inner_sum(s_bank[2 + m][:, 0:D], w1Tm, lambda fc: w1T[:, fc, :])
                inner_sum(p_t[:, m:m + 1], w1Tm, lambda fc: b1col[:, fc:fc + 1])
            inner_sum(p_oz[:, 0:D], lambda fc: b1rep[:, fc, :], lambda fc: w2[:, fc, :])
            inner_sum(p_t[:, 2:3], lambda fc: b1rep[:, fc, :], lambda fc: b1col[:, fc:fc + 1]).then_inc(ffw_psum, 1)
            pe.wait_ge(ffw_made, 1)
            pe.wait_ge(wqkv_in, 96)
            pe.wait_ge(rows_in, 48)
            pe.wait_ge(zeros_set, 4)
            pe.wait_ge(ident16_made, 1)

            def transpose_t(i):
                pe.wait_ge(t_ready, i + 1)
                after(pe, tT_ready, i)
                for c in range(C):
                    mm = pe.transpose(p_t[:, c * P:c * P + P], t[:, c * P:c * P + P], ident[:, :])
                mm.then_inc(tT_psum, 1)

            def transpose_qk(i):
                pe.wait_ge(again_ready, 2 * i + 2)
                after(pe, p_ready, i)
                for a in range(2):
                    for g in range(G):
                        mm = pe.transpose(p_qkT[:, a, g, :], qk4[:, a, 2 * g:2 * g + 2, :, :].rearrange("p h r d -> p (h r d)"),
                                          ident16[:, :])
                mm.then_inc(qkT_psum, 1)

            def output_waits(i):
                pe.wait_ge(o_ready, 2 * i + 2)
                after(pe, z_ready, i)

            def transpose_o(i):
                for c in range(C):
                    for b in range(TB):
                        mm = pe.transpose(p_oz[:, c * P + b * S:c * P + b * S + S],
                                          o[:, b, c * G:c * G + G, :].rearrange("p h d -> p (h d)"), ident[0:S, 0:S])
                mm.then_inc(oT_psum, 1)

            def project_o(i):
                pe.wait_ge(oT_ready, i + 1)
                for c in range(C):
                    mm = pe.matmul(p_oz[:, 0:D], oT[:, c, :], wo[:, c, :], start=c == 0, stop=c == C - 1)
                mm.then_inc(z_psum, 1)

            def scores_wait(i):
                pe.wait_ge(qkT_ready, i + 1)

            def scores(i):
                for g in range(G):
                    for e in range(2):
                        rows = slice(64 * e, 64 * e + 64)
                        for b in range(TB):
                            tok = slice(S * b, S * b + S)
                            col = 512 * e + S * g
                            mm = pe.matmul(p_s[tok, col:col + S], qkT[rows, 1, g, tok], qkT[rows, 0, g, tok], start=True, stop=True,
                                           skip_group_check=True)
                mm.then_inc(s_psum, 1)

            def qkv(i, k, a):
                if a == 0:
                    pe.wait_ge(tT_ready, i + 1)
                    after(pe, u_ready, i)
                for c in range(C):
                    mm = pe.matmul(p_qkv[:, a * D:a * D + D], tT[:, k, c, :], wqkv[:, c, a * D:a * D + D], start=c == 0, stop=c == C - 1)
                return mm

            def attend(i, k):
                pe.wait_ge(p_ready, i + 1)
                pe.wait_ge(v_ready, 2 * i + 2)
                after(pe, o_ready, 2 * i)
                for n in range(H):
                    col = 512 * (n // G) + n % G * TB * VW
                    mm = pe.matmul(p_o[0:S, col:col + TB * VW], pT[:, n % 2, n // 2, :],
                                   v[:, k, n, :, :].rearrange("p b n -> p (b n)"), start=True, stop=True)
                mm.then_inc(o_psum, 1)

            def slot(h, off):
                if on(h, off, L_H):
                    transpose_qk(2 * h + off - L_H)
                if on(h, off, L_B):
                    transpose_t(2 * h + off - L_B)
                if on(h, off, L_C):
                    i, k = 2 * h + off - L_C, (off - L_C) % 2
                    qkv(i, k, 0)
                if on(h, off, L_L):
                    output_waits(2 * h + off - L_L)
                if on(h, off, L_C):
                    qkv(i, k, 1)
                if on(h, off, L_L):
                    transpose_o(2 * h + off - L_L)
                if on(h, off, L_H):
                    scores_wait(2 * h + off - L_H)
                if on(h, off, L_C):
                    qkv(i, k, 2).then_inc(qkv_psum, 1)
                if on(h, off, L_H):
                    scores(2 * h + off - L_H)
                if on(h, off, L_L):
                    project_o(2 * h + off - L_L)
                if on(h, off, L_H):
                    attend(2 * h + off - L_H, (off - L_H) % 2)

            run_tiles(pe, slot)

            def transpose_t2(i, k):
                pe.wait_ge(t2_ready, 2 * i + 2)
                after(pe, t2T_ready, i)
                for m in range(4):
                    mm = pe.transpose(p_t[:, m * P:m * P + P], t2[:, k, m // 2, (m % 2) * P:(m % 2) * P + P], ident[:, :])
                mm.then_inc(t2T_psum, 1)

            def inner(i, j, k):
                pe.wait_ge(t2T_ready, i + 1)
                after(pe, f1_ready, 2 * (i - 1))
                after(pe, hh_ready, i - 1)
                bank = (p_qkv, p_s)[k]
                for c in range(C):
                    pe.matmul(bank[:, 512 * j:512 * j + 512], t2T[:, k, j, c, :], wff[:, c, :], start=c == 0, stop=c == C - 1)
                for c in range(C):
                    mm = pe.matmul(s_bank[2 + k][:, j:j + 1], t2T[:, k, j, c, :], w1b[:, c:c + 1], start=c == 0, stop=c == C - 1)
                mm.then_inc(ff_psum, 1)

            def slot2(h, off):
                if on2(h, off, M_A):
                    i, k = 2 * h + off - M_A, (off - M_A) % 2
                    transpose_t2(i, k)
                    for j in range(2):
                        inner(i, j, k)

            pe.wait_ge(factors_made, 1)
            run_pairs(pe, slot2)

        @block.vector
        def _(dve):
            dve.wait_ge(ident_made, 2)
            dve.tensor_copy(ident16[:, :], ident[:, :]).then_inc(ident16_made, 1)
            dve.wait_ge(condT_psum, 1)
            dve.tensor_copy(condT.rearrange("p c n -> p (c n)"), p_t[:, 0:D]).then_inc(condT_made, 1)
            dve.tensor_copy(b1col, p_t[:, D:D + FC]).then_inc(b1rep_made, 1)
            dve.wait_ge(b1rep_made, 1)
            dve.tensor_copy(b1rep, b1col.unsqueeze(2).broadcast_to([P, FC, P])).then_inc(b1rep_made, 1)
            dve.wait_ge(ada_psum, 1)
            dve.wait_ge(bada_in, 16)
            for n, bank in enumerate((p_qkv[:, 0:512], p_qkv[:, 512:1024], p_oz[:, :])):
                dve.tensor_tensor(ada[:, n * 512:n * 512 + 512], bank, bada[:, n * 512:n * 512 + 512], ALU.add).then_inc(ada_made, 1)
            dve.wait_ge(ada_made, 3)
            for n in (1, 4):
                dve.tensor_scalar(ada[:, n * D:n * D + D], ada[:, n * D:n * D + D], 1.0, None, ALU.add).then_inc(ada_plus, 1)
            n = T // 8
            for k in range(8):
                dve.wait_ge(x_in[k], 16)
                with dve.Fori(n * k, n * k + n) as i:
                    dve.bn_stats(bn[:, bass.ds(i, 1), :].rearrange("p a n -> p (a n)"),
                                 x_all[:, bass.ds(i, 1), :].rearrange("p a d -> p (a d)")).then_inc(bn_done, 1)
            dve.wait_ge(ffw_psum, 1)
            for m in range(C):
                dve.tensor_copy(wff[:, m, 0:D], p_s[:, m * 512:m * 512 + D])
                dve.tensor_copy(wff[:, m, D:2 * D], s_bank[2 + m][:, 0:D])
            dve.tensor_scalar(w1b[:, :], p_t[:, 0:C], 2.0, None, ALU.mult)
            dve.tensor_copy(b12[:, :], p_oz[:, 0:D])
            dve.tensor_copy(bb[:, :], p_t[:, 2:3]).then_inc(ffw_made, 1)

            steps, asks = [0], [0]

            def step(ins):
                ins.then_inc(vec_step, 1)
                steps[0] += 1
                dve.wait_ge(vec_step, steps[0])

            def tt(dst, a, b, f):
                step(dve.tensor_tensor(row(dst), row(a), row(b), f))

            def ts(dst, a, s1, f1_, s2=None, f2_=None):
                if f2_ is None:
                    step(dve.tensor_scalar(row(dst), row(a), s1, None, f1_))
                else:
                    step(dve.tensor_scalar(row(dst), row(a), s1, s2, f1_, f2_))

            def stt(dst, a, s1, b, f1_, f2_):
                step(dve.scalar_tensor_tensor(out=row(dst), in0=row(a), scalar=s1, in1=row(b), op0=f1_, op1=f2_))

            def ask():
                dve.drain().then_inc(vec_asks, 1)
                asks[0] += 1
                dve.wait_ge(act_answers, asks[0])

            def rsq(dst):
                ask()
                tt(W3, W2_, W2_, ALU.mult)
                stt(W3, W3, -0.5, W0, ALU.mult, ALU.mult)
                stt(dst, W3, 1.5, W2_, ALU.add, ALU.mult)

            def log_map_factor(dst, xx):
                ts(W0, xx, EPS2, ALU.max)
                rsq(W4)
                tt(W5, W0, W4, ALU.mult)
                ts(W5, W5, MAX_ARG, ALU.min)
                ts(W6, W5, -1.0, ALU.mult, 1.0, ALU.add)
                step(dve.reciprocal(row(W6), row(W6)))
                stt(W7, W5, 1.0, W6, ALU.add, ALU.mult)
                ask()
                stt(W8, W8, 0.5, W4, ALU.mult, ALU.mult)
                tt(W9, W5, W5, ALU.mult)
                ts(W10, W9, 1.0 / 15, ALU.mult)
                for m in (13, 11, 9, 7, 5, 3):
                    stt(W10, W10, 1.0 / m, W9, ALU.add, ALU.mult)
                ts(W10, W10, 1.0, ALU.add)
                tt(W10, W10, W5, ALU.mult)
                tt(W10, W10, W4, ALU.mult)
                ts(W11, W5, SERIES_BELOW, ALU.is_lt)
                tt(W10, W10, W8, ALU.subtract)
                tt(W10, W10, W11, ALU.mult)
                tt(dst, W8, W10, ALU.add)

            def norm_factor(dst, s, var):
                tt(W0, s, s, ALU.mult)
                tt(W0, W0, var, ALU.mult)
                ts(W0, W0, LN_EPS, ALU.add)
                rsq(W4)
                tt(dst, s, W4, ALU.mult)

            dve.wait_ge(bn_done, T)
            part = lambda k: bn[:, :, k]
            add = lambda dst, a, b, f: step(dve.tensor_tensor(row(dst), a, b, f))
            add(MEAN, part(1), part(4), ALU.add)
            ts(MEAN, MEAN, 0.5, ALU.mult)
            add(W0, part(1), part(4), ALU.subtract)
            add(W1_, part(2), part(5), ALU.add)
            tt(W0, W0, W0, ALU.mult)
            stt(W0, W0, D / 4.0, W1_, ALU.mult, ALU.add)
            ts(VAR, W0, 1.0 / D, ALU.mult)
            tt(W1_, MEAN, MEAN, ALU.mult)
            stt(XX, W1_, float(D), W0, ALU.mult, ALU.add)
            ts(OMX, XX, -1.0, ALU.mult, 1.0, ALU.add)
            log_map_factor(W12, XX)
            norm_factor(R1, W12, VAR)

            dve.wait_ge(wqkv_in, 96)
            dve.wait_ge(rows_in, 48)
            dve.wait_ge(zeros_set, 4)
            dve.wait_ge(ada_stored, 16)

            def tile_of(big, i):
                return big[:, bass.ds(i, 1), :].rearrange("p a d -> p (a d)")

            def modulate(i, k, half):
                dve.wait_ge(mod_in[k], 32 * half + 32)
                after(dve, t_ready, i)
                dve.scalar_tensor_tensor(out=lnx[:, :], in0=tile_of(x_all, i), scalar=arrays[:, MEAN, bass.ds(i, 1)],
                                         in1=mod[:, k, D:2 * D], op0=ALU.subtract, op1=ALU.mult).then_inc(ln_half, 1)
                dve.wait_ge(ln_half, i + 1)
                after(dve, tT_psum, i)
                after(dve, t_squared, i)
                dve.scalar_tensor_tensor(out=t[:, :], in0=lnx[:, :], scalar=arrays[:, R1, bass.ds(i, 1)],
                                         in1=mod[:, k, 0:D], op0=ALU.mult, op1=ALU.add).then_inc(t_ready, 1)

            def project(i, k):
                dve.wait_ge(rt_ready, i + 1)
                after(dve, u_ready, i - 1)
                dve.tensor_scalar(ct[:, k:k + 1], rt[:, k:k + 1], AM, 1.0, ALU.mult, ALU.min).then_inc(ct_ready, 1)
                dve.wait_ge(qkv_psum, i + 1)
                dve.wait_ge(ct_ready, i + 1)
                after(dve, qk_ready, 2 * i - 2)
                after(dve, v_ready, 2 * i - 2)
                after(dve, u_squared, i - 1)
                dve.scalar_tensor_tensor(out=u[:, k, :], in0=p_qkv[:, 0:3 * D], scalar=ct[:, k:k + 1],
                                         in1=bqkv[:, :], op0=ALU.mult, op1=ALU.add).then_inc(u_ready, 1)

            def sum_squares(i):
                dve.wait_ge(u_squared, i + 1)
                after(dve, roots_ready, i)
                dve.tensor_reduce(hs[:, 0:3 * H], usq[:, :].rearrange("p (a d) -> p a d", d=HD), AX.X, ALU.add).then_inc(heads_summed, 1)
                dve.wait_ge(heads_summed, i + 1)
                dve.tensor_reduce(hs[:, 3 * H:NF], hs[:, 0:3 * H].rearrange("p (a h) -> p a h", h=H), AX.X, ALU.add).then_inc(rows_summed, 1)

            def normalise(i):
                dve.wait_ge(o_psum, i + 1)
                after(dve, o_ready, 2 * i)
                oh = p_o[0:S, :].rearrange("p (c n) -> p c n", c=2)[:, :, 0:G * TB * VW].rearrange(
                    "p c (g b n) -> p c g b n", b=TB, n=VW)
                for c in range(2):
                    dve.reciprocal(rden[:, c * G:c * G + G, :], oh[:, c, :, :, HD]).then_inc(rden_ready, 1)
                dve.wait_ge(rden_ready, 2 * i + 2)
                after(dve, oT_psum, i)
                for b in range(TB):
                    dve.tensor_tensor(o[:, b, :, :].rearrange("p (c g) d -> p c g d", c=2), oh[:, :, :, b, 0:HD],
                                      rden[:, :, b].rearrange("p (c g) -> p c g", c=2).unsqueeze(3).broadcast_to([S, 2, G, HD]),
                                      ALU.mult).then_inc(o_ready, 1)

            def gate_z(i, k, half):
                dve.wait_ge(z_psum, i + 1)
                after(dve, z_squared, i)
                after(dve, zg_ready, i)
                dve.tensor_tensor(z[:, :], p_oz[:, 0:D], bo[:, :], ALU.add).then_inc(z_ready, 1)
                dve.wait_ge(z_ready, i + 1)
                dve.wait_ge(gate_in[k], 32 * half + 32)
                after(dve, stats_kept, i)
                dve.scalar_tensor_tensor(out=tile_of(g_all, i), in0=z[:, :], scalar=1.0, in1=gate[:, k, :],
                                         op0=ALU.mult, op1=ALU.mult, accum_out=st[:, 1:2]).then_inc(zg_ready, 1)
                dve.wait_ge(zg_ready, i + 1)
                after(dve, xg_summed, i)
                dve.scalar_tensor_tensor(out=junk[:, 3, :], in0=tile_of(x_all, i), scalar=1.0, in1=tile_of(g_all, i),
                                         op0=ALU.mult, op1=ALU.mult, accum_out=st[:, 2:3]).then_inc(xg_summed, 1)

            def scale_qk(i, k):
                dve.wait_ge(roots_ready, i + 1)
                after(dve, fac_ready, i)
                dve.tensor_tensor(rlim[:, :], roots[:, 3 * H:NF], c_lim[:, :], ALU.min).then_inc(rlim_ready, 1)
                dve.wait_ge(rlim_ready, i + 1)
                after(dve, qk_ready, 2 * i)
                after(dve, v_ready, 2 * i)
                dve.tensor_tensor(fac[:, :].rearrange("p (a h) -> p a h", a=3),
                                  roots[:, 0:3 * H].rearrange("p (a h) -> p a h", a=3),
                                  rlim[:, :].unsqueeze(2).broadcast_to([P, 3, H]), ALU.min).then_inc(fac_ready, 1)
                dve.wait_ge(fac_ready, i + 1)
                after(dve, low_ready, i)
                for a in range(2):
                    part = slice(a * D, a * D + D)
                    dve.tensor_tensor(qk[:, part].rearrange("p (h d) -> p h d", d=HD), u[:, k, part].rearrange("p (h d) -> p h d", d=HD),
                                      fac[:, a * H:a * H + H].unsqueeze(2).broadcast_to([P, H, HD]), ALU.mult).then_inc(qk_ready, 1)

            def scale_v(i, k):
                after(dve, o_psum, i - 1)
                for b in range(TB):
                    own = slice(S * b, S * b + S)
                    dve.tensor_tensor(v[own, k, :, b, 0:HD], u[own, k, 2 * D:3 * D].rearrange("p (h d) -> p h d", d=HD),
                                      fac[own, 2 * H:3 * H].unsqueeze(2).broadcast_to([S, H, HD]), ALU.mult).then_inc(v_ready, 1)

            def repeat_parts(i):
                dve.wait_ge(high_ready, i + 1)
                dve.wait_ge(low_ready, i + 1)
                after(dve, qkT_psum, i)
                q4, k4 = (qk4[:, a, :, :, :].rearrange("p h (y z) d -> p h y z d", y=2) for a in range(2))
                dve.tensor_copy(q4[:, :, :, 1, :], q4[:, :, :, 0, :]).then_inc(again_ready, 1)
                dve.tensor_copy(k4[:, :, 1, :, :], k4[:, :, 0, :, :]).then_inc(again_ready, 1)

            def slot(h, off):
                if on(h, off, L_D):
                    project(2 * h + off - L_D, (off - L_D) % 2)
                if on(h, off, L_L):
                    normalise(2 * h + off - L_L)
                if on(h, off, L_E):
                    scale_qk(2 * h + off - L_E, (off - L_E) % 2)
                if on(h, off, L_D):
                    sum_squares(2 * h + off - L_D)
                if on(h, off, L_A):
                    modulate(2 * h + off - L_A, (off - L_A) % 2, h + (off - L_A) // 2)
                if on(h, off, L_E):
                    scale_v(2 * h + off - L_E, (off - L_E) % 2)
                    repeat_parts(2 * h + off - L_E)
                if on(h, off, L_L):
                    gate_z(2 * h + off - L_L, (off - L_L) % 2, h + (off - L_L) // 2)

            run_tiles(dve, slot)

            dve.wait_ge(stats_kept, T)
            sm = lambda k: stats[:, :, k]
            step(dve.tensor_scalar(row(W0), sm(0), EPS2, None, ALU.max))
            rsq(W4)
            ts(W4, W4, AM, ALU.mult, 1.0, ALU.min)
            tt(W5, W4, W4, ALU.mult)
            add(W0, row(W5), sm(3), ALU.mult)
            ts(W0, W0, EPS2, ALU.max)
            rsq(W6)
            tt(W7, W0, W6, ALU.mult)
            ask()
            tt(W8, W8, W6, ALU.mult)
            tt(W9, W8, W4, ALU.mult)
            tt(W10, W9, W9, ALU.mult)
            add(W10, row(W10), sm(3), ALU.mult)
            add(W11, row(W9), sm(2), ALU.mult)
            ts(W11, W11, 2.0, ALU.mult, 1.0, ALU.add)
            tt(W12, XX, W10, ALU.mult)
            tt(W12, W12, W11, ALU.add)
            ts(W12, W12, EPS, ALU.max)
            step(dve.reciprocal(row(W12), row(W12)))
            tt(W13, W11, W10, ALU.add)
            tt(ALPHA, W13, W12, ALU.mult)
            tt(W13, OMX, W9, ALU.mult)
            tt(BETA, W13, W12, ALU.mult)
            step(dve.tensor_scalar(row(W9), sm(1), 1.0 / D, None, ALU.mult))
            tt(W10, W9, W9, ALU.mult)
            step(dve.scalar_tensor_tensor(out=row(W10), in0=sm(3), scalar=1.0 / D, in1=row(W10), op0=ALU.mult, op1=ALU.subtract))
            tt(W11, W9, MEAN, ALU.mult)
            step(dve.scalar_tensor_tensor(out=row(W11), in0=sm(2), scalar=1.0 / D, in1=row(W11), op0=ALU.mult, op1=ALU.subtract))
            tt(W12, ALPHA, MEAN, ALU.mult)
            tt(W13, BETA, W9, ALU.mult)
            tt(MEAN1, W12, W13, ALU.add)
            tt(W12, ALPHA, ALPHA, ALU.mult)
            tt(W13, ALPHA, BETA, ALU.mult)
            tt(W14, BETA, BETA, ALU.mult)
            tt(W9, W12, VAR, ALU.mult)
            tt(W10, W14, W10, ALU.mult)
            tt(W9, W9, W10, ALU.add)
            tt(W11, W13, W11, ALU.mult)
            stt(W9, W11, 2.0, W9, ALU.mult, ALU.add)
            ts(VAR, W9, 0.0, ALU.max)
            tt(W9, W12, XX, ALU.mult)
            add(W10, row(W14), sm(3), ALU.mult)
            tt(W9, W9, W10, ALU.add)
            add(W10, row(W13), sm(2), ALU.mult)
            stt(W9, W10, 2.0, W9, ALU.mult, ALU.add)
            ts(XX1, W9, 0.0, ALU.max)
            ts(OMX1, XX1, -1.0, ALU.mult, 1.0, ALU.add)
            log_map_factor(W12, XX1)
            norm_factor(R2, W12, VAR)
            dve.drain().then_inc(factors_made, 1)

            def first_sum(i, j):
                n = 2 * i + j
                dve.wait_ge(xa_ready, n + 1)
                g = tile_of(g_all, n)
                dve.scalar_tensor_tensor(out=g, in0=g, scalar=arrays[:, BETA, bass.ds(n, 1)], in1=xa[:, j, :],
                                         op0=ALU.mult, op1=ALU.add).then_inc(x1_ready, 1)

            def modulate2(i, j, k):
                n = 2 * i + j
                dve.wait_ge(mod2_in[j], 32 * i + 32)
                dve.wait_ge(x1_ready, n + 1)
                after(dve, t2_ready, n)
                dve.scalar_tensor_tensor(out=lnx[:, :], in0=tile_of(g_all, n), scalar=arrays[:, MEAN1, bass.ds(n, 1)],
                                         in1=mod[:, j, D:2 * D], op0=ALU.subtract, op1=ALU.mult).then_inc(ln2_half, 1)
                dve.wait_ge(ln2_half, n + 1)
                after(dve, t2T_psum, i - 1)
                after(dve, t2_squared, n - 3)
                after(dve, qf_ready, n - 3)
                dve.scalar_tensor_tensor(out=t2[:, k, j, :], in0=lnx[:, :], scalar=arrays[:, R2, bass.ds(n, 1)],
                                         in1=mod[:, j, 0:D], op0=ALU.mult, op1=ALU.add).then_inc(t2_ready, 1)

            def inner_square(i, k):
                bank, tw = (p_qkv, p_s)[k], s_bank[2 + k]
                for j in range(2):
                    n = 2 * i + j
                    dve.wait_ge(ff_psum, n + 1)
                    after(dve, qf_ready, n - 1)
                    after(dve, hh_half, n - 1)
                    dve.scalar_tensor_tensor(out=junk2[:, 3, j, :], in0=bank[:, 512 * j + D:512 * j + 2 * D], scalar=1.0,
                                             in1=t2[:, k, j, :], op0=ALU.mult, op1=ALU.mult,
                                             accum_out=qf[:, j:j + 1]).then_inc(qf_ready, 1)
                dve.wait_ge(rt2_ready, i + 1)
                after(dve, ca_ready, i - 1)
                dve.tensor_scalar(ct2[:, k, :], rt2[:, :], AM, 1.0, ALU.mult, ALU.min).then_inc(ct2_ready, 1)
                dve.wait_ge(ct2_ready, i + 1)
                for j in range(2):
                    dve.wait_ge(qf_ready, 2 * i + j + 1)
                    after(dve, hh_ready, i)
                    dve.scalar_tensor_tensor(out=hh[:, 0, j:j + 1], in0=qf[:, j:j + 1], scalar=ct2[:, k, j:j + 1],
                                             in1=tw[:, j:j + 1], op0=ALU.mult, op1=ALU.add).then_inc(hh_half, 1)
                dve.wait_ge(hh_half, 2 * i + 2)
                after(dve, rh_ready, i)
                dve.tensor_tensor(hh[:, 2, :], hh[:, 0, :], ct2[:, k, :], ALU.mult).then_inc(hh_scaled, 1)
                dve.wait_ge(hh_scaled, i + 1)
                dve.tensor_scalar(hh[:, 1, :], hh[:, 2, :], bb[:, 0:1], None, ALU.add).then_inc(hh_ready, 1)

            def inner_factors(i, k):
                dve.wait_ge(rh_ready, i + 1)
                after(dve, ff_ready, 2 * i)
                after(dve, ca_ready, i)
                dve.tensor_scalar(ch[:, :], rh[:, :], AM, 1.0, ALU.mult, ALU.min).then_inc(ch_ready, 1)
                dve.wait_ge(ch_ready, i + 1)
                dve.tensor_tensor(ca[:, :], ch[:, :], ct2[:, k, :], ALU.mult).then_inc(ca_ready, 1)

            def mlp_output(i, j, k):
                n = 2 * i + j
                dve.wait_ge(ca_ready, i + 1)
                after(dve, ff_ready, n - 1)
                dve.scalar_tensor_tensor(out=f1[:, j, :], in0=(p_qkv, p_s)[k][:, 512 * j:512 * j + D], scalar=ca[:, j:j + 1],
                                         in1=b2[:, :], op0=ALU.mult, op1=ALU.add).then_inc(f1_ready, 1)
                dve.wait_ge(f1_ready, n + 1)
                after(dve, ff_squared, n - 1)
                after(dve, fg_ready, n - 1)
                dve.scalar_tensor_tensor(out=ff[:, j, :], in0=b12[:, :], scalar=ch[:, j:j + 1], in1=f1[:, j, :],
                                         op0=ALU.mult, op1=ALU.add).then_inc(ff_ready, 1)
                dve.wait_ge(ff_ready, n + 1)
                dve.wait_ge(gate2_in[j], 32 * i + 32)
                after(dve, yo_ready, n - 1)
                after(dve, xf_summed, n - 1)
                after(dve, fg_squared, n - 1)
                dve.tensor_tensor(fg[:, j, :], ff[:, j, :], gate[:, j, :], ALU.mult).then_inc(fg_ready, 1)
                dve.wait_ge(fg_ready, n + 1)
                after(dve, parts_ready, 3 * i)
                dve.scalar_tensor_tensor(out=junk[:, j, :], in0=tile_of(g_all, n), scalar=1.0, in1=fg[:, j, :],
                                         op0=ALU.mult, op1=ALU.mult, accum_out=fst[:, 2, j:j + 1]).then_inc(xf_summed, 1)

            def output_clip(i):
                dve.wait_ge(rf_ready, i + 1)
                after(dve, parts_ready, 3 * i)
                dve.tensor_scalar(cf[:, :], rf[:, :], AM, 1.0, ALU.mult, ALU.min).then_inc(cf_ready, 1)

            def sum_factors(i):
                dve.wait_ge(parts_ready, 3 * i + 3)
                dve.wait_ge(fin_step, FIN_STEPS * i + FIN_STEPS)
                after(dve, al2_ready, i)
                after(dve, be2_ready, i)
                dve.tensor_tensor(den[:, 0, :], parts[:, 0, :], fin[:, 10, :], ALU.add).then_inc(den_step, 1)
                dve.wait_ge(den_step, 3 * i + 1)
                dve.tensor_scalar(den[:, 1, :], den[:, 0, :], EPS, None, ALU.max).then_inc(den_step, 1)
                dve.wait_ge(den_step, 3 * i + 2)
                dve.reciprocal(den[:, 2, :], den[:, 1, :]).then_inc(den_step, 1)
                dve.wait_ge(den_step, 3 * i + 3)
                after(dve, xo_ready, 2 * i)
                after(dve, yo_ready, 2 * i)
                dve.tensor_tensor(al2[:, :], parts[:, 1, :], den[:, 2, :], ALU.mult).then_inc(al2_ready, 1)
                dve.tensor_tensor(be2[:, :], parts[:, 2, :], den[:, 2, :], ALU.mult).then_inc(be2_ready, 1)

            def second_sum(i, j):
                n = 2 * i + j
                dve.wait_ge(be2_ready, i + 1)
                dve.wait_ge(xo_ready, n + 1)
                after(dve, out_ready, n - 1)
                dve.scalar_tensor_tensor(out=yo[:, j, :], in0=fg[:, j, :], scalar=be2[:, j:j + 1], in1=xo[:, j, :],
                                         op0=ALU.mult, op1=ALU.add).then_inc(yo_ready, 1)

            def slot2(h, off):
                if on2(h, off, M_C):
                    output_clip(2 * h + off - M_C)
                if on2(h, off, M_A):
                    i, k = 2 * h + off - M_A, (off - M_A) % 2
                    for j in range(2):
                        first_sum(i, j)
                        modulate2(i, j, k)
                if on2(h, off, M_B):
                    inner_square(2 * h + off - M_B, (off - M_B) % 2)
                if on2(h, off, M_C):
                    sum_factors(2 * h + off - M_C)
                    for j in range(2):
                        second_sum(2 * h + off - M_C, j)
                if on2(h, off, M_B):
                    i, k = 2 * h + off - M_B, (off - M_B) % 2
                    inner_factors(i, k)
                    for j in range(2):
                        mlp_output(i, j, k)

            run_pairs(dve, slot2)


_WEIGHTS = ["w_q", "b_q", "w_k", "b_k", "w_v", "b_v", "w_o", "b_o", "w_f1", "b_f1", "w_f2", "b_f2", "w_ada", "b_ada"]
_INS = ["x", "cond_1024"] + ["L0_cond_" + n for n in _WEIGHTS]


def kernel(**inputs):
    import concourse.bacc as bacc
    from concourse.bass_utils import run_bass_kernel_spmd

    nc = bacc.Bacc("TRN2", target_bir_lowering=False, num_devices=1)
    arrays, args = {}, []
    for name in _INS:
        a = np.ascontiguousarray(inputs[name])
        arrays[f"in_{name}"] = a
        args.append(nc.dram_tensor(f"in_{name}", a.shape, mybir.dt.from_np(a.dtype), kind="ExternalInput").ap())
    out = nc.dram_tensor("out", inputs["x"].shape, F32, kind="ExternalOutput").ap()
    build(nc, *args, out)
    r = run_bass_kernel_spmd(nc, [arrays], core_ids=[0])
    return r.results[0]["out"]
```

```python
import math
from contextlib import ExitStack

import numpy as np

import concourse.bass as bass
from concourse import mybir

F32 = mybir.dt.float32
BF16 = mybir.dt.bfloat16
F16 = mybir.dt.float16
ALU = mybir.AluOpType
ACT = mybir.ActivationFunctionType
AX = mybir.AxisListType

P = 128
EPS = 1e-7
EPS2 = 1e-14
LN_TINY = 1e-18
LN_EPS = 1e-6
MAX_ARG = float(np.float32(1.0 - 1e-5))
AM = 0.5 * math.log((1 + MAX_ARG) / (1 - MAX_ARG))
QK_UP = 64.0
SERIES_BELOW = 0.25


def _beta(a, b):
    return math.exp(math.lgamma(a) + math.lgamma(b) - math.lgamma(a + b))


def after(eng, sem, count):
    if isinstance(count, int) and count <= 0:
        return
    eng.wait_ge(sem, count)


def build(nc, x, cond, w_q, b_q, w_k, b_k, w_v, b_v, w_o, b_o, w_f1, b_f1, w_f2, b_f2, w_ada, b_ada, out):
    B, S, D = x.shape
    FF = w_f1.shape[1]
    H = 16
    HD = D // H
    C = D // P
    FC = FF // P
    TB = P // S
    T = B // TB
    HALF = T // 2
    RATIO = _beta(HD / 2, 0.5) / _beta(D / 2, 0.5)
    G = H // 2
    VW = HD + 1
    NF = 3 * H + 3
    SCALE = 1.0 / math.sqrt(HD)
    assert TB == 2 and C == 2 and H == 16 and HD == 16

    with ExitStack() as ctx:
        def sb(name, shape, dt=F32):
            return ctx.enter_context(nc.sbuf_tensor(name, shape, dt))

        def ps(name, shape):
            return ctx.enter_context(nc.psum_tensor(name, shape, F32))

        def sem(name):
            return ctx.enter_context(nc.semaphore(name))

        mod_dram = nc.dram_tensor("mod_rows", (B, 3 * D), F32).ap()
        mod2_dram = nc.dram_tensor("mod2_rows", (T // 2, TB, 2, 2 * D), F32).ap()
        gate2_dram = nc.dram_tensor("gate2_rows", (T // 2, TB, 2, D), F32).ap()

        x_all = sb("x_all", [P, T, D])
        g_all = sb("g_all", [P, T, D])
        flat = g_all[:, :, :].rearrange("p t d -> p (t d)")
        at = [0]

        def scratch(n):
            at[0] += n
            return flat[:, at[0] - n:at[0]]

        w1 = scratch(C * FF).rearrange("p (c n) -> p c n", c=C)
        w1T = scratch(FC * D).rearrange("p (c n) -> p c n", c=FC)
        w2 = scratch(FC * D).rearrange("p (c n) -> p c n", c=FC)
        b1rep = scratch(FC * P).rearrange("p (c n) -> p c n", c=FC)
        wada = scratch(C * 6 * D).rearrange("p (c n) -> p c n", c=C)
        bada = scratch(6 * D)
        ada = scratch(6 * D)
        condr = scratch(D)
        condT = scratch(D).rearrange("p (c n) -> p c n", c=C)
        b1col = scratch(FC)
        b1row = scratch(P)[0:FC, :]

        wqkv = sb("wqkv", [P, C, 3 * D])
        wo = sb("wo", [P, C, D])
        wff = sb("wff", [P, C, 2 * D])
        w1b = sb("w1b", [P, C])
        bqkv = sb("bqkv", [P, 3 * D])
        bo = sb("bo", [P, D])
        b2 = sb("b2", [P, D])
        b12 = sb("b12", [P, D])
        bb = sb("bb", [P, 1])
        ident = sb("ident", [P, P])
        ident16 = sb("ident16", [P, P], F16)

        bn = sb("bn", [P, T, 6])
        arrays = sb("arrays", [P, 26, T])
        stats = sb("stats", [P, T, 4])

        mod = sb("mod", [P, 2, 2 * D])
        gate = sb("gate", [P, 2, D])
        lnx = sb("lnx", [P, D])
        t = sb("t", [P, D])
        tT = sb("tT", [P, 2, C, P])
        u = sb("u", [P, 2, 3 * D])
        usq = sb("usq", [P, 3 * D])
        ss_t = sb("ss_t", [P, 2])
        rt = sb("rt", [P, 2])
        ct = sb("ct", [P, 2])
        hs = sb("hs", [P, NF])
        lnh = sb("lnh", [P, NF])
        y0 = sb("y0", [P, NF])
        nw = sb("nw", [P, 4, NF])
        roots = sb("roots", [P, NF])
        rlim = sb("rlim", [P, 3])
        fac = sb("fac", [P, 3 * H])
        facv = sb("facv", [P, H, TB])
        own = sb("own", [P, TB])
        qk = sb("qk", [P, 2 * D])
        qk4 = sb("qk4", [P, 2, H, 4, HD], F16)
        v = sb("v", [P, 2, H, TB, VW])
        qkT = sb("qkT", [P, 2, G, P], F16)
        pT = sb("pT", [P, 2, G, S])
        rden = sb("rden", [S, H, TB])
        o = sb("o", [S, TB, H, HD])
        oT = sb("oT", [P, C, P])
        z = sb("z", [P, D])
        st = sb("st", [P, 4])
        junk = sb("junk", [P, 4, D], BF16)

        c_fac = sb("c_fac", [P, NF])
        c_lim = sb("c_lim", [P, 3])
        c_three = sb("c_three", [P, NF])
        c_mhalf = sb("c_mhalf", [P, 2])
        c_half = sb("c_half", [P, 2])
        c_one = sb("c_one", [P, 2])
        c_two = sb("c_two", [P, 2])
        c_eps2 = sb("c_eps2", [P, 2])
        c_tiny = sb("c_tiny", [P, 1])

        f1, ff = (pT[:, n, :, :].rearrange("p g n -> p (g n)").rearrange("p (j d) -> p j d", j=2) for n in range(2))
        fgs = [b.rearrange("p (j d) -> p j d", j=2) for b in (qk[:, :], u[:, 1, 0:2 * D])]
        xo = u[:, 0, 0:2 * D].rearrange("p (j d) -> p j d", j=2)
        yo = usq[:, 0:2 * D].rearrange("p (j d) -> p j d", j=2)
        xa = sb("xa", [P, 2, D])
        gates2 = (gate[:, :, :], bqkv[:, 0:2 * D].rearrange("p (j d) -> p j d", j=2))
        lnx2 = (lnx, t)
        t2 = qkT[:, :, :, :].rearrange("p a g n -> p (a g n)").bitcast(F32).rearrange(
            "p (k j d) -> p k j d", k=2, j=2)
        t2T = qk4[:, :, :, :, :].rearrange("p a h r d -> p (a h r d)").bitcast(F32).rearrange(
            "p (k j c n) -> p k j c n", k=2, j=2, c=C)
        ss2 = sb("ss2", [P, 2])
        rt2 = sb("rt2", [P, 2])
        ct2 = sb("ct2", [P, 2, 2])
        rh = sb("rh", [P, 2])
        rf = sb("rf", [P, 2])
        cf = sb("cf", [P, 2])
        parts = sb("parts", [P, 3, 2])
        den = sb("den", [P, 3, 2])
        qf = sb("qf", [P, 2])
        hh = sb("hh", [P, 3, 2])
        ch = sb("ch", [P, 2])
        ca = sb("ca", [P, 2])
        fst = sb("fst", [P, 2, 3, 2])
        fin = sb("fin", [P, 11, 2])
        na = sb("na", [P, 2])
        th = sb("th", [P, 2])
        al2 = sb("al2", [P, 2])
        be2 = sb("be2", [P, 2])
        junk2 = wqkv[:, :, :].rearrange("p c n -> p (c n)")[:, 0:4 * D].bitcast(BF16).rearrange(
            "p (a j d) -> p a j d", a=4, j=2)

        p_t = ps("p_t", [P, 512])
        p_o = ps("p_o", [P, 1024])
        p_oh = p_o[0:S, :].rearrange("p (c n) -> p c n", c=2)[:, :, 0:G * TB * VW].rearrange(
            "p c (g b n) -> p c g b n", b=TB, n=VW)
        p_oz = ps("p_oz", [P, 512])
        p_qkv = ps("p_qkv", [P, 1024])
        p_s = ps("p_s", [P, 1024])
        s_bank = [p_s[:, 0:512], p_s[:, 512:1024], p_o[:, 0:512], p_o[:, 512:1024]]
        p_qkT = p_s[:, :].bitcast(F16).rearrange("p (a g n) -> p a g n", a=2, g=G)

        cond_in = sem("cond_in"); wada_in = sem("wada_in"); bada_in = sem("bada_in")
        w1_in = sem("w1_in"); w2_in = sem("w2_in"); b1_in = sem("b1_in")
        wqkv_in = sem("wqkv_in"); rows_in = sem("rows_in")
        x_in = [sem(f"x_in{k}") for k in range(8)]
        ident_made = sem("ident_made"); ident16_made = sem("ident16_made"); consts_made = sem("consts_made")
        condT_psum = sem("condT_psum"); condT_made = sem("condT_made")
        ada_psum = sem("ada_psum"); ada_made = sem("ada_made"); ada_plus = sem("ada_plus")
        ada_stored = sem("ada_stored")
        w1T_psum = sem("w1T_psum"); w1T_made = sem("w1T_made"); b1rep_made = sem("b1rep_made")
        ffw_psum = sem("ffw_psum"); ffw_made = sem("ffw_made")
        zeros_set = sem("zeros_set")
        bn_done = sem("bn_done")
        vec_step = sem("vec_step"); vec_asks = sem("vec_asks"); act_answers = sem("act_answers")
        mod_in = [sem(f"mod_in{k}") for k in range(2)]
        gate_in = [sem(f"gate_in{k}") for k in range(2)]
        ln_half = sem("ln_half"); t_ready = sem("t_ready"); t_squared = sem("t_squared")
        rt_ready = sem("rt_ready"); ln_rows = sem("ln_rows"); ct_ready = sem("ct_ready")
        tT_psum = sem("tT_psum"); tT_ready = sem("tT_ready")
        qkv_psum = sem("qkv_psum"); u_ready = sem("u_ready"); u_squared = sem("u_squared")
        heads_summed = sem("heads_summed"); rows_summed = sem("rows_summed"); roots_ready = sem("roots_ready"); rlim_ready = sem("rlim_ready")
        ln_taken = sem("ln_taken"); y0_ready = sem("y0_ready"); newton = sem("newton"); fac_ready = sem("fac_ready"); facv_ready = sem("facv_ready"); own_made = sem("own_made")
        qk_ready = sem("qk_ready"); high_ready = sem("high_ready"); low_ready = sem("low_ready"); again_ready = sem("again_ready"); v_ready = sem("v_ready")
        qkT_psum = sem("qkT_psum"); qkT_ready = sem("qkT_ready")
        s_psum = sem("s_psum"); p_ready = sem("p_ready")
        o_psum = sem("o_psum"); rden_ready = sem("rden_ready"); o_ready = sem("o_ready")
        oT_psum = sem("oT_psum"); oT_ready = sem("oT_ready")
        z_psum = sem("z_psum"); z_ready = sem("z_ready"); zg_ready = sem("zg_ready")
        xg_summed = sem("xg_summed"); z_squared = sem("z_squared"); zg_squared = sem("zg_squared")
        stats_kept = sem("stats_kept")
        factors_made = sem("factors_made")
        mod2_in = sem("mod2_in")
        gate2_in = [sem(f"gate2_in{k}") for k in range(2)]
        xa_ready = sem("xa_ready"); x1_ready = sem("x1_ready"); ln2_half = sem("ln2_half")
        t2_ready = sem("t2_ready"); t2_squared = sem("t2_squared"); rt2_ready = sem("rt2_ready"); rh_ready = sem("rh_ready"); rf_ready = sem("rf_ready"); cf_ready = sem("cf_ready"); parts_ready = sem("parts_ready"); den_step = sem("den_step")
        ct2_ready = sem("ct2_ready"); t2T_psum = sem("t2T_psum"); t2T_ready = sem("t2T_ready")
        ff_psum = sem("ff_psum"); qf_ready = sem("qf_ready"); hh_half = sem("hh_half"); hh_scaled = sem("hh_scaled"); hh_ready = sem("hh_ready")
        ch_ready = sem("ch_ready"); ca_ready = sem("ca_ready")
        f1_ready = sem("f1_ready"); ff_ready = sem("ff_ready"); fg_ready = sem("fg_ready")
        ff_squared = sem("ff_squared"); fg_squared = sem("fg_squared"); xf_summed = sem("xf_summed")
        fin_step = sem("fin_step"); na_ready = sem("na_ready"); th_ready = sem("th_ready")
        al2_ready = sem("al2_ready"); be2_ready = sem("be2_ready"); xo_ready = sem("xo_ready"); yo_ready = sem("yo_ready")
        out_ready = sem("out_ready"); out_stored = sem("out_stored")

        (MEAN, VAR, XX, R1, OMX, ALPHA, BETA, MEAN1, R2, XX1, OMX1, W0, W1_, W2_, W3, W4, W5, W6, W7, W8,
         W9, W10, W11, W12, W13, W14) = range(26)

        def row(k):
            return arrays[:, k, :]

        x_t = x.rearrange("(t b) s d -> (b s) t d", b=TB)
        out_t = out.rearrange("(t b) s d -> (b s) t d", b=TB)

        def bcast(vec, n):
            return vec.rearrange("(a n) -> a n", a=1).broadcast_to([P, n])

        def mod_rows(i, lo, hi):
            return mod_dram[bass.ds(TB * i, TB), lo:hi].unsqueeze(1).broadcast_to([TB, S, hi - lo])

        def pair_rows(dram, i):
            rows = dram[bass.ds(i, 1), :, :, :].rearrange("a b j n -> (a b) (j n)")
            return rows.unsqueeze(1).broadcast_to([TB, S, rows.shape[-1]])

        L_A, L_B, L_C, L_D, L_E, L_H, L_L = 0, 1, 2, 3, 4, 5, 6
        FIRST = 8
        M_A, M_Q, M_B, M_C, M_O, M_S = 0, 1, 2, 3, 4, 5
        FIRST2 = 6
        FIN_STEPS = 11

        def run_slots(eng, slot, first, items, slots):
            for s in range(first):
                slot(s // 2, s % 2)
            with eng.Fori(first // 2, items // 2) as h:
                slot(h, 0)
                slot(h, 1)
            for s in range(items, slots):
                slot(s // 2, s % 2)

        def count(n):
            return min(n, T) if isinstance(n, int) else n

        def run_tiles(eng, slot):
            run_slots(eng, slot, FIRST, T, T + L_L)

        def run_pairs(eng, slot):
            run_slots(eng, slot, FIRST2, HALF, HALF + M_S)

        def on(h, off, lag, items=T):
            return not isinstance(h, int) or 0 <= 2 * h + off - lag < items

        def on2(h, off, lag):
            return on(h, off, lag, HALF)

        block = ctx.enter_context(nc.Block())

        @block.sync
        def _(sp):
            sp.dma_start(condr, cond[:, :]).then_inc(cond_in, 16)
            sp.dma_start(wada, w_ada.rearrange("(c p) n -> p c n", p=P)).then_inc(wada_in, 16)
            sp.dma_start(bada, bcast(b_ada, 6 * D)).then_inc(bada_in, 16)
            for k in range(8):
                n = T // 8
                sp.dma_start(x_all[:, n * k:n * k + n, :], x_t[:, n * k:n * k + n, :]).then_inc(x_in[k], 16)
            sp.wait_ge(ada_plus, 2)
            sp.dma_start(mod_dram[:, :], ada[:, 0:3 * D]).then_inc(ada_stored, 16)
            for b in range(TB):
                seqs = slice(b, B, TB)
                sp.dma_start(mod2_dram[:, b, :, :], ada[seqs, 3 * D:5 * D]).then_inc(ada_stored, 16)
                sp.dma_start(gate2_dram[:, b, :, :], ada[seqs, 5 * D:6 * D]).then_inc(ada_stored, 16)
            sp.wait_ge(ada_stored, 80)

            def slot(h, off):
                if on(h, off, L_A):
                    i, k = 2 * h + off, off % 2
                    after(sp, t_ready, i - 1)
                    sp.dma_start(mod[:, k, :], mod_rows(i, 0, 2 * D)).then_inc(mod_in[k], 16)
                if on(h, off, L_H):
                    i, k = 2 * h + off - L_H, (off - L_H) % 2
                    after(sp, zg_ready, i - 1)
                    sp.dma_start(gate[:, k, :], mod_rows(i, 2 * D, 3 * D)).then_inc(gate_in[k], 16)

            run_tiles(sp, slot)

            def slot2(h, off):
                if on2(h, off, M_A):
                    i = 2 * h + off - M_A
                    after(sp, t2_ready, 2 * i)
                    sp.dma_start(mod[:, :, :].rearrange("p j n -> p (j n)"), pair_rows(mod2_dram, i)).then_inc(mod2_in, 16)
                if on2(h, off, M_Q):
                    i, k = 2 * h + off - M_Q, (off - M_Q) % 2
                    after(sp, fg_ready, 2 * (i - 1))
                    sp.dma_start(gates2[k].rearrange("p j n -> p (j n)"), pair_rows(gate2_dram, i)).then_inc(gate2_in[k], 16)
                if on2(h, off, M_S):
                    i = 2 * h + off - M_S
                    sp.wait_ge(out_ready, 2 * i + 2)
                    sp.dma_start(out_t[:, bass.ds(2 * i, 2), :], x_all[:, bass.ds(2 * i, 2), :]).then_inc(out_stored, 16)

            sp.wait_ge(t_ready, T)
            sp.wait_ge(zg_ready, T)
            sp.wait_ge(u_ready, T)
            run_pairs(sp, slot2)
            sp.wait_ge(out_stored, 16 * HALF)

        @block.gpsimd
        def _(pool):
            pool.memset(ident[:, :], 0.0).then_inc(ident_made, 1)
            pool.wait_ge(ident_made, 1)
            pool.affine_select(out=ident[:, :], in_=ident[:, :], compare_op=ALU.not_equal, fill=1.0,
                               base=0, pattern=[[-1, P]], channel_multiplier=1).then_inc(ident_made, 1)
            pool.memset(c_fac[:, 0:2 * H], -0.5 * AM * QK_UP)
            pool.memset(c_fac[:, 2 * H:3 * H], -0.5 * AM / RATIO)
            pool.memset(c_fac[:, 3 * H:3 * H + 2], -0.5 * AM * RATIO * QK_UP)
            pool.memset(c_fac[:, 3 * H + 2:NF], -0.5 * AM)
            pool.memset(c_lim[:, 0:2], RATIO * QK_UP)
            pool.memset(c_lim[:, 2:3], 1.0)
            pool.memset(c_three[:, :], 3.0)
            pool.memset(c_mhalf[:, :], -0.5)
            pool.memset(c_half[:, :], 0.5)
            pool.memset(c_one[:, :], 1.0)
            pool.memset(c_two[:, :], 2.0)
            pool.memset(c_eps2[:, :], EPS2)
            pool.memset(c_tiny[:, :], LN_TINY).then_inc(consts_made, 1)
            pool.wait_ge(consts_made, 1)
            for n, (b, c, value) in enumerate(((0, 0, 1.0), (0, 1, 0.0), (1, 0, 0.0), (1, 1, 1.0))):
                after(pool, zeros_set, n)
                pool.memset(v[S * b:S * b + S, :, :, c, :], value).then_inc(zeros_set, 1)
            pool.dma_start(wo[:, :, :], w_o.rearrange("(c p) n -> p c n", p=P)).then_inc(rows_in, 16)
            pool.dma_start(bo[:, :], bcast(b_o, D)).then_inc(rows_in, 16)
            pool.dma_start(b2[:, :], bcast(b_f2, D)).then_inc(rows_in, 16)

            def token_root(i, k):
                pool.wait_ge(t_squared, i + 1)
                after(pool, ct_ready, i - 1)
                pool.tensor_tensor(rt[:, k:k + 1], ss_t[:, k:k + 1], c_mhalf[:, 0:1], ALU.pow).then_inc(rt_ready, 1)

            def head_roots(i):
                pool.wait_ge(y0_ready, i + 1)
                pool.wait_ge(rows_summed, i + 1)
                after(pool, roots_ready, i)
                pool.tensor_tensor(nw[:, 0, :], y0[:, :], y0[:, :], ALU.mult).then_inc(newton, 1)
                pool.wait_ge(newton, 4 * i + 1)
                pool.tensor_tensor(nw[:, 1, :], nw[:, 0, :], hs[:, :], ALU.mult).then_inc(newton, 1)
                pool.wait_ge(newton, 4 * i + 2)
                pool.tensor_tensor(nw[:, 2, :], nw[:, 1, :], c_three[:, :], ALU.subtract).then_inc(newton, 1)
                pool.wait_ge(newton, 4 * i + 3)
                pool.tensor_tensor(nw[:, 3, :], nw[:, 2, :], y0[:, :], ALU.mult).then_inc(newton, 1)
                pool.wait_ge(newton, 4 * i + 4)
                after(pool, fac_ready, i)
                pool.tensor_tensor(roots[:, :], nw[:, 3, :], c_fac[:, :], ALU.mult).then_inc(roots_ready, 1)

            def scale_v(i, k):
                pool.wait_ge(facv_ready, i + 1)
                after(pool, o_psum, i - 1)
                pool.tensor_tensor(v[:, k, :, :, 0:HD],
                                   u[:, k, 2 * D:3 * D].rearrange("p (h d) -> p h d", d=HD).unsqueeze(2).broadcast_to([P, H, TB, HD]),
                                   facv[:, :, :].unsqueeze(3).broadcast_to([P, H, TB, HD]), ALU.mult).then_inc(v_ready, 1)

            def low_parts(i):
                pool.wait_ge(high_ready, i + 1)
                pool.wait_ge(qk_ready, 2 * i + 2)
                after(pool, qkT_psum, i)
                low = bass.AP(qk4[:, :, :, :, :].tensor, 2 * HD, [[8 * H * HD, P], [4 * H * HD - HD, 2], [4 * HD, H], [1, HD]])
                pool.tensor_tensor(low, qk[:, :].rearrange("p (a h d) -> p a h d", a=2, d=HD), qk4[:, :, :, 0, :],
                                   ALU.subtract).then_inc(low_ready, 1)

            def keep_stats(i):
                pool.wait_ge(z_squared, i + 1)
                pool.wait_ge(zg_squared, i + 1)
                pool.wait_ge(xg_summed, i + 1)
                pool.tensor_copy(stats[:, bass.ds(i, 1), :].rearrange("p a n -> p (a n)"), st[:, :]).then_inc(stats_kept, 1)

            def slot(h, off):
                if on(h, off, L_E):
                    scale_v(2 * h + off - L_E, (off - L_E) % 2)
                    low_parts(2 * h + off - L_E)
                if on(h, off, L_C):
                    token_root(2 * h + off - L_C, (off - L_C) % 2)
                if on(h, off, L_D):
                    head_roots(2 * h + off - L_D)
                if on(h, off, L_L):
                    keep_stats(2 * h + off - L_L)

            run_tiles(pool, slot)

            def token_roots2(i, k):
                pool.wait_ge(t2_squared, 2 * i + 2)
                after(pool, ct2_ready, i)
                pool.tensor_tensor(rt2[:, :], ss2[:, :], c_mhalf[:, :], ALU.pow).then_inc(rt2_ready, 1)

            def inner_roots(i):
                pool.wait_ge(hh_ready, i + 1)
                after(pool, ch_ready, i)
                pool.tensor_tensor(rh[:, :], hh[:, 1, :], c_mhalf[:, :], ALU.pow).then_inc(rh_ready, 1)

            def output_roots(i, k):
                pool.wait_ge(ff_squared, 2 * i + 2)
                after(pool, cf_ready, i)
                pool.tensor_tensor(rf[:, :], fst[:, k, 0, :], c_mhalf[:, :], ALU.pow).then_inc(rf_ready, 1)

            def fin_op(i, k, a, b, f):
                pool.tensor_tensor(fin[:, k, :], a, b, f).then_inc(fin_step, 1)
                pool.wait_ge(fin_step, FIN_STEPS * i + (k + 1))

            def output_norms(i, k):
                after(pool, be2_ready, i)
                pool.wait_ge(fg_squared, 2 * i + 2)
                pool.wait_ge(cf_ready, i + 1)
                fin_op(i, 0, cf[:, :], cf[:, :], ALU.mult)
                fin_op(i, 1, fin[:, 0, :], fst[:, k, 1, :], ALU.mult)
                fin_op(i, 2, fin[:, 1, :], c_eps2[:, :], ALU.add)
                after(pool, th_ready, i)
                pool.tensor_tensor(na[:, :], fin[:, 2, :], c_half[:, :], ALU.pow).then_inc(na_ready, 1)
                fin_op(i, 3, fin[:, 2, :], c_mhalf[:, :], ALU.pow)

            def output_parts(i, k):
                pool.wait_ge(th_ready, i + 1)
                fin_op(i, 4, th[:, :], fin[:, 3, :], ALU.mult)
                fin_op(i, 5, fin[:, 4, :], cf[:, :], ALU.mult)
                kap = fin[:, 5, :]
                fin_op(i, 6, kap, kap, ALU.mult)
                fin_op(i, 7, fin[:, 6, :], fst[:, k, 1, :], ALU.mult)
                y2 = fin[:, 7, :]
                pool.wait_ge(xf_summed, 2 * i + 2)
                fin_op(i, 8, kap, fst[:, k, 2, :], ALU.mult)
                fin_op(i, 9, fin[:, 8, :], c_two[:, :], ALU.mult)
                fin_op(i, 10, fin[:, 9, :], c_one[:, :], ALU.add)
                pool.tensor_tensor(parts[:, 0, :], arrays[:, XX1, bass.ds(2 * i, 2)], y2, ALU.mult).then_inc(parts_ready, 1)
                pool.tensor_tensor(parts[:, 1, :], fin[:, 10, :], y2, ALU.add).then_inc(parts_ready, 1)
                pool.tensor_tensor(parts[:, 2, :], arrays[:, OMX1, bass.ds(2 * i, 2)], kap, ALU.mult).then_inc(parts_ready, 1)

            def add_x(i, j):
                n = 2 * i + j
                pool.wait_ge(yo_ready, n + 1)
                xt = x_all[:, bass.ds(n, 1), :].rearrange("p a d -> p (a d)")
                pool.tensor_tensor(xt, xt, yo[:, j, :], ALU.add).then_inc(out_ready, 1)

            def slot2(h, off):
                if on2(h, off, M_C):
                    output_roots(2 * h + off - M_C, (off - M_C) % 2)
                    output_norms(2 * h + off - M_C, (off - M_C) % 2)
                    output_parts(2 * h + off - M_C, (off - M_C) % 2)
                if on2(h, off, M_A):
                    token_roots2(2 * h + off - M_A, (off - M_A) % 2)
                if on2(h, off, M_O):
                    for j in range(2):
                        add_x(2 * h + off - M_O, j)
                if on2(h, off, M_Q):
                    inner_roots(2 * h + off - M_Q)

            pool.wait_ge(factors_made, 1)
            run_pairs(pool, slot2)

        @block.scalar
        def _(act):
            act.dma_start(w1, w_f1.rearrange("(c p) n -> p c n", p=P)).then_inc(w1_in, 16)
            act.dma_start(w2, w_f2.rearrange("(c p) n -> p c n", p=P)).then_inc(w2_in, 16)
            act.dma_start(b1row, b_f1.rearrange("(c n) -> c n", n=P)).then_inc(b1_in, 16)
            for k, (w, b) in enumerate(((w_q, b_q), (w_k, b_k), (w_v, b_v))):
                act.dma_start(wqkv[:, :, k * D:k * D + D], w.rearrange("(c p) n -> p c n", p=P)).then_inc(wqkv_in, 16)
                act.dma_start(bqkv[:, k * D:k * D + D], bcast(b, D)).then_inc(wqkv_in, 16)
            for k in range(FC // 2):
                act.wait_ge(w1T_psum, k + 1)
                act.activation(w1T[:, 2 * k:2 * k + 2, :].rearrange("p c n -> p (c n)"),
                               s_bank[2 + k % 2][:, :], ACT.Copy).then_inc(w1T_made, 1)

            def rsq():
                asked[0] += 1
                act.wait_ge(vec_asks, asked[0])
                act.activation(row(W1_), row(W0), ACT.Ln).then_inc(ln_rows, 1)
                rsqs[0] += 1
                act.wait_ge(ln_rows, rsqs[0])
                act.activation(row(W2_), row(W1_), ACT.Exp, scale=-0.5).then_inc(act_answers, 1)

            def elementwise(f, src, dst):
                asked[0] += 1
                act.wait_ge(vec_asks, asked[0])
                act.activation(row(dst), row(src), f).then_inc(act_answers, 1)

            asked, rsqs = [0], [0]
            act.wait_ge(consts_made, 1)
            act.preload_act_table_set("natural_log_exp_and_others")
            rsq()
            elementwise(ACT.Ln, W7, W8)
            rsq()

            def high_parts(i):
                act.wait_ge(qk_ready, 2 * i + 2)
                after(act, qkT_psum, i)
                after(act, low_ready, i)
                after(act, again_ready, 2 * i)
                act.activation(qk4[:, :, :, 0, :], qk[:, :].rearrange("p (a h d) -> p a h d", a=2, d=HD), ACT.Copy).then_inc(high_ready, 1)

            def evac_qkT(i):
                act.wait_ge(qkT_psum, i + 1)
                after(act, s_psum, i)
                act.activation(qkT[:, :, :, :].rearrange("p a g n -> p (a g n)"), p_s[:, :].bitcast(F16), ACT.Copy).then_inc(qkT_ready, 1)

            def evac_oT(i):
                act.wait_ge(oT_psum, i + 1)
                after(act, z_psum, i)
                act.activation(oT[:, :, :].rearrange("p c n -> p (c n)"), p_oz[:, 0:D], ACT.Copy).then_inc(oT_ready, 1)

            def evac_tT(i, k):
                act.wait_ge(tT_psum, i + 1)
                after(act, qkv_psum, i - 1)
                act.activation(tT[:, k, :, :].rearrange("p c n -> p (c n)"), p_t[:, 0:D], ACT.Copy).then_inc(tT_ready, 1)

            def square_u(i, k):
                act.wait_ge(u_ready, i + 1)
                after(act, heads_summed, i)
                act.activation(usq[:, :], u[:, k, :], ACT.Square).then_inc(u_squared, 1)

            def square_t(i, k):
                act.wait_ge(t_ready, i + 1)
                after(act, rt_ready, i - 1)
                after(act, t_squared, i)
                act.activation(junk[:, 0, :], t[:, :], ACT.Square, accum_out=ss_t[:, k:k + 1]).then_inc(t_squared, 1)

            def inverse_norms(i):
                act.wait_ge(rows_summed, i + 1)
                after(act, y0_ready, i)
                act.activation(lnh[:, :], hs[:, :], ACT.Ln, bias=c_tiny[:, 0:1]).then_inc(ln_taken, 1)
                act.wait_ge(ln_taken, i + 1)
                after(act, roots_ready, i)
                act.activation(y0[:, :], lnh[:, :], ACT.Exp, scale=-0.5).then_inc(y0_ready, 1)

            def square_z(i):
                act.wait_ge(z_ready, i + 1)
                after(act, stats_kept, i)
                after(act, z_squared, i)
                act.activation(junk[:, 1, :], z[:, :], ACT.Square, accum_out=st[:, 0:1]).then_inc(z_squared, 1)
                act.wait_ge(zg_ready, i + 1)
                after(act, zg_squared, i)
                act.activation(junk[:, 2, :], g_all[:, bass.ds(i, 1), :].rearrange("p a d -> p (a d)"),
                               ACT.Square, accum_out=st[:, 3:4]).then_inc(zg_squared, 1)

            def exp_scores(i):
                act.wait_ge(s_psum, i + 1)
                after(act, o_psum, i)
                act.activation(pT[:, :, :, :].rearrange("p e g n -> p (e g n)"), p_s[:, :],
                               ACT.Exp, scale=SCALE / (QK_UP * QK_UP)).then_inc(p_ready, 1)

            def slot(h, off):
                if on(h, off, L_H):
                    evac_qkT(2 * h + off - L_H)
                if on(h, off, L_B):
                    evac_tT(2 * h + off - L_B, (off - L_B) % 2)
                if on(h, off, L_D):
                    square_u(2 * h + off - L_D, (off - L_D) % 2)
                if on(h, off, L_L):
                    evac_oT(2 * h + off - L_L)
                if on(h, off, L_E):
                    high_parts(2 * h + off - L_E)
                if on(h, off, L_H):
                    exp_scores(2 * h + off - L_H)
                if on(h, off, L_D):
                    inverse_norms(2 * h + off - L_D)
                if on(h, off, L_A):
                    square_t(2 * h + off - L_A, (off - L_A) % 2)
                if on(h, off, L_L):
                    square_z(2 * h + off - L_L)

            run_tiles(act, slot)

            rsq()
            rsq()
            elementwise(ACT.Tanh, W7, W8)
            act.preload_act_table_set("natural_log_exp_and_others")
            rsq()
            elementwise(ACT.Ln, W7, W8)
            rsq()

            def scale_x(i, j):
                n = 2 * i + j
                after(act, x1_ready, n - 1)
                act.activation(xa[:, j, :], x_all[:, bass.ds(n, 1), :].rearrange("p a d -> p (a d)"), ACT.Copy,
                               scale=arrays[:, ALPHA, bass.ds(n, 1)]).then_inc(xa_ready, 1)

            def square_t2(i, j, k):
                n = 2 * i + j
                act.wait_ge(t2_ready, n + 1)
                after(act, rt2_ready, i)
                after(act, t2_squared, n - 1)
                act.activation(junk2[:, 0, j, :], t2[:, k, j, :], ACT.Square, accum_out=ss2[:, j:j + 1]).then_inc(t2_squared, 1)

            def evac_t2T(i, k):
                act.wait_ge(t2T_psum, i + 1)
                after(act, ff_psum, 2 * (i - 1))
                act.activation(t2T[:, k, :, :, :].rearrange("p j c n -> p (j c n)"), p_t[:, :], ACT.Copy).then_inc(t2T_ready, 1)

            def square_ff(i, j, k):
                n = 2 * i + j
                act.wait_ge(ff_ready, n + 1)
                after(act, parts_ready, 3 * (i - 1))
                after(act, ff_squared, n - 1)
                act.activation(junk2[:, 1, j, :], ff[:, j, :], ACT.Square, accum_out=fst[:, k, 0, j:j + 1]).then_inc(ff_squared, 1)

            def square_fg(i, j, k):
                n = 2 * i + j
                act.wait_ge(fg_ready, n + 1)
                after(act, fg_squared, n - 1)
                act.activation(junk2[:, 2, j, :], fgs[k][:, j, :], ACT.Square, accum_out=fst[:, k, 1, j:j + 1]).then_inc(fg_squared, 1)

            def tanh_norm(i):
                act.wait_ge(na_ready, i + 1)
                after(act, parts_ready, 3 * i)
                act.activation(th[:, :], na[:, :], ACT.Tanh).then_inc(th_ready, 1)

            def scale_x1(i, j):
                n = 2 * i + j
                act.wait_ge(al2_ready, i + 1)
                after(act, yo_ready, n - 1)
                act.activation(xo[:, j, :], g_all[:, bass.ds(n, 1), :].rearrange("p a d -> p (a d)"), ACT.Copy,
                               scale=al2[:, j:j + 1]).then_inc(xo_ready, 1)

            def slot2(h, off):
                if on2(h, off, M_A):
                    for j in range(2):
                        scale_x(2 * h + off - M_A, j)
                if on2(h, off, M_O):
                    for j in range(2):
                        scale_x1(2 * h + off - M_O, j)
                if on2(h, off, M_C):
                    tanh_norm(2 * h + off - M_C)
                if on2(h, off, M_A):
                    i, k = 2 * h + off - M_A, (off - M_A) % 2
                    evac_t2T(i, k)
                    for j in range(2):
                        square_t2(i, j, k)
                if on2(h, off, M_B):
                    for j in range(2):
                        square_ff(2 * h + off - M_B, j, (off - M_B) % 2)
                    for j in range(2):
                        square_fg(2 * h + off - M_B, j, (off - M_B) % 2)

            act.preload_act_table(ACT.Tanh)
            act.wait_ge(factors_made, 1)
            run_pairs(act, slot2)

        @block.tensor
        def _(pe):
            pe.wait_ge(ident_made, 2)
            pe.wait_ge(cond_in, 16)
            for c in range(C):
                pe.transpose(p_t[:, c * P:c * P + P], condr[:, c * P:c * P + P], ident[:, :])
            pe.wait_ge(b1_in, 16)
            pe.transpose(p_t[:, D:D + FC], b1row, ident[0:FC, 0:FC]).then_inc(condT_psum, 1)
            pe.wait_ge(w1_in, 16)
            for k in range(FC // 2):
                after(pe, w1T_made, k - 1)
                for m in range(4):
                    fc, c = 2 * k + m // 2, m % 2
                    mm = pe.transpose(s_bank[2 + k % 2][:, m * P:m * P + P], w1[:, c, fc * P:fc * P + P], ident[:, :])
                mm.then_inc(w1T_psum, 1)
            pe.wait_ge(wada_in, 16)
            pe.wait_ge(condT_made, 1)
            for n, bank in enumerate((p_qkv[:, 0:512], p_qkv[:, 512:1024], p_oz[:, :])):
                for c in range(C):
                    mm = pe.matmul(bank, condT[:, c, :], wada[:, c, n * 512:n * 512 + 512], start=c == 0, stop=c == C - 1)
            mm.then_inc(ada_psum, 1)
            pe.wait_ge(w1T_made, FC // 2)
            pe.wait_ge(w2_in, 16)
            pe.wait_ge(b1rep_made, 2)
            pe.wait_ge(ada_made, 3)

            def inner_sum(dst, lhs, rhs):
                for fc in range(FC):
                    mm = pe.matmul(dst, lhs(fc), rhs(fc), start=fc == 0, stop=fc == FC - 1)
                return mm

            for m in range(C):
                w1Tm = lambda fc: w1T[:, fc, m * P:m * P + P]
                inner_sum(p_s[:, m * 512:m * 512 + D], w1Tm, lambda fc: w2[:, fc, :])
                inner_sum(s_bank[2 + m][:, 0:D], w1Tm, lambda fc: w1T[:, fc, :])
                inner_sum(p_t[:, m:m + 1], w1Tm, lambda fc: b1col[:, fc:fc + 1])
            inner_sum(p_oz[:, 0:D], lambda fc: b1rep[:, fc, :], lambda fc: w2[:, fc, :])
            inner_sum(p_t[:, 2:3], lambda fc: b1rep[:, fc, :], lambda fc: b1col[:, fc:fc + 1]).then_inc(ffw_psum, 1)
            pe.wait_ge(ffw_made, 1)
            pe.wait_ge(wqkv_in, 96)
            pe.wait_ge(rows_in, 48)
            pe.wait_ge(zeros_set, 4)
            pe.wait_ge(ident16_made, 1)

            def transpose_t(i):
                pe.wait_ge(t_ready, i + 1)
                after(pe, tT_ready, i)
                for c in range(C):
                    mm = pe.transpose(p_t[:, c * P:c * P + P], t[:, c * P:c * P + P], ident[:, :])
                mm.then_inc(tT_psum, 1)

            def transpose_qk(i):
                pe.wait_ge(again_ready, 2 * i + 2)
                after(pe, p_ready, i)
                for a in range(2):
                    for g in range(G):
                        mm = pe.transpose(p_qkT[:, a, g, :], qk4[:, a, 2 * g:2 * g + 2, :, :].rearrange("p h r d -> p (h r d)"),
                                          ident16[:, :])
                mm.then_inc(qkT_psum, 1)

            def output_waits(i):
                pe.wait_ge(o_ready, 2 * i + 2)
                after(pe, z_ready, i)

            def transpose_o(i):
                for c in range(C):
                    for b in range(TB):
                        mm = pe.transpose(p_oz[:, c * P + b * S:c * P + b * S + S],
                                          o[:, b, c * G:c * G + G, :].rearrange("p h d -> p (h d)"), ident[0:S, 0:S])
                mm.then_inc(oT_psum, 1)

            def project_o(i):
                pe.wait_ge(oT_ready, i + 1)
                for c in range(C):
                    mm = pe.matmul(p_oz[:, 0:D], oT[:, c, :], wo[:, c, :], start=c == 0, stop=c == C - 1)
                mm.then_inc(z_psum, 1)

            def scores_wait(i):
                pe.wait_ge(qkT_ready, i + 1)

            def scores(i):
                for g in range(G):
                    for e in range(2):
                        rows = slice(64 * e, 64 * e + 64)
                        for b in range(TB):
                            tok = slice(S * b, S * b + S)
                            col = 512 * e + S * g
                            mm = pe.matmul(p_s[tok, col:col + S], qkT[rows, 1, g, tok], qkT[rows, 0, g, tok], start=True, stop=True,
                                           skip_group_check=True)
                mm.then_inc(s_psum, 1)

            def qkv(i, k, a):
                if a == 0:
                    pe.wait_ge(tT_ready, i + 1)
                    after(pe, u_ready, i)
                for c in range(C):
                    mm = pe.matmul(p_qkv[:, a * D:a * D + D], tT[:, k, c, :], wqkv[:, c, a * D:a * D + D], start=c == 0, stop=c == C - 1)
                return mm

            def attend(i, k):
                pe.wait_ge(p_ready, i + 1)
                pe.wait_ge(v_ready, i + 1)
                after(pe, o_ready, 2 * i)
                for n in range(H):
                    col = 512 * (n // G) + n % G * TB * VW
                    mm = pe.matmul(p_o[0:S, col:col + TB * VW], pT[:, n % 2, n // 2, :],
                                   v[:, k, n, :, :].rearrange("p b n -> p (b n)"), start=True, stop=True)
                mm.then_inc(o_psum, 1)

            def slot(h, off):
                if on(h, off, L_H):
                    transpose_qk(2 * h + off - L_H)
                if on(h, off, L_B):
                    transpose_t(2 * h + off - L_B)
                if on(h, off, L_C):
                    i, k = 2 * h + off - L_C, (off - L_C) % 2
                    qkv(i, k, 0)
                if on(h, off, L_L):
                    output_waits(2 * h + off - L_L)
                if on(h, off, L_C):
                    qkv(i, k, 1)
                if on(h, off, L_L):
                    transpose_o(2 * h + off - L_L)
                if on(h, off, L_H):
                    scores_wait(2 * h + off - L_H)
                if on(h, off, L_C):
                    qkv(i, k, 2).then_inc(qkv_psum, 1)
                if on(h, off, L_H):
                    scores(2 * h + off - L_H)
                if on(h, off, L_L):
                    project_o(2 * h + off - L_L)
                if on(h, off, L_H):
                    attend(2 * h + off - L_H, (off - L_H) % 2)

            run_tiles(pe, slot)

            def transpose_t2(i, k):
                pe.wait_ge(t2_ready, 2 * i + 2)
                after(pe, t2T_ready, i)
                for m in range(4):
                    mm = pe.transpose(p_t[:, m * P:m * P + P], t2[:, k, m // 2, (m % 2) * P:(m % 2) * P + P], ident[:, :])
                mm.then_inc(t2T_psum, 1)

            def inner(i, j, k):
                pe.wait_ge(t2T_ready, i + 1)
                after(pe, f1_ready, 2 * (i - 1))
                after(pe, hh_ready, i - 1)
                after(pe, qf_ready, 2 * (i - 1))
                bank = (p_qkv, p_s)[k]
                for c in range(C):
                    pe.matmul(bank[:, 512 * j:512 * j + 512], t2T[:, k, j, c, :], wff[:, c, :], start=c == 0, stop=c == C - 1)
                for c in range(C):
                    mm = pe.matmul(s_bank[2 + k][:, j:j + 1], t2T[:, k, j, c, :], w1b[:, c:c + 1], start=c == 0, stop=c == C - 1)
                mm.then_inc(ff_psum, 1)

            def slot2(h, off):
                if on2(h, off, M_A):
                    i, k = 2 * h + off - M_A, (off - M_A) % 2
                    transpose_t2(i, k)
                    for j in range(2):
                        inner(i, j, k)

            pe.wait_ge(factors_made, 1)
            run_pairs(pe, slot2)

        @block.vector
        def _(dve):
            dve.wait_ge(ident_made, 2)
            dve.tensor_copy(ident16[:, :], ident[:, :]).then_inc(ident16_made, 1)
            for b in range(TB):
                dve.memset(own[S * b:S * b + S, b:b + 1], 1.0).then_inc(own_made, 1)
                dve.memset(own[S * b:S * b + S, 1 - b:2 - b], 0.0).then_inc(own_made, 1)
            dve.wait_ge(condT_psum, 1)
            dve.tensor_copy(condT.rearrange("p c n -> p (c n)"), p_t[:, 0:D]).then_inc(condT_made, 1)
            dve.tensor_copy(b1col, p_t[:, D:D + FC]).then_inc(b1rep_made, 1)
            dve.wait_ge(b1rep_made, 1)
            dve.tensor_copy(b1rep, b1col.unsqueeze(2).broadcast_to([P, FC, P])).then_inc(b1rep_made, 1)
            dve.wait_ge(ada_psum, 1)
            dve.wait_ge(bada_in, 16)
            for n, bank in enumerate((p_qkv[:, 0:512], p_qkv[:, 512:1024], p_oz[:, :])):
                dve.tensor_tensor(ada[:, n * 512:n * 512 + 512], bank, bada[:, n * 512:n * 512 + 512], ALU.add).then_inc(ada_made, 1)
            dve.wait_ge(ada_made, 3)
            for n in (1, 4):
                dve.tensor_scalar(ada[:, n * D:n * D + D], ada[:, n * D:n * D + D], 1.0, None, ALU.add).then_inc(ada_plus, 1)
            n = T // 8
            for k in range(8):
                dve.wait_ge(x_in[k], 16)
                with dve.Fori(n * k // 4, (n * k + n) // 4) as i:
                    for m in range(4):
                        dve.bn_stats(bn[:, bass.ds(4 * i + m, 1), :].rearrange("p a n -> p (a n)"),
                                     x_all[:, bass.ds(4 * i + m, 1), :].rearrange("p a d -> p (a d)")).then_inc(bn_done, 1)
            dve.wait_ge(ffw_psum, 1)
            for m in range(C):
                dve.tensor_copy(wff[:, m, 0:D], p_s[:, m * 512:m * 512 + D])
                dve.tensor_copy(wff[:, m, D:2 * D], s_bank[2 + m][:, 0:D])
            dve.tensor_scalar(w1b[:, :], p_t[:, 0:C], 2.0, None, ALU.mult)
            dve.tensor_copy(b12[:, :], p_oz[:, 0:D])
            dve.tensor_copy(bb[:, :], p_t[:, 2:3]).then_inc(ffw_made, 1)

            steps, asks = [0], [0]

            def step(ins):
                ins.then_inc(vec_step, 1)
                steps[0] += 1
                dve.wait_ge(vec_step, steps[0])

            def tt(dst, a, b, f):
                step(dve.tensor_tensor(row(dst), row(a), row(b), f))

            def ts(dst, a, s1, f1_, s2=None, f2_=None):
                if f2_ is None:
                    step(dve.tensor_scalar(row(dst), row(a), s1, None, f1_))
                else:
                    step(dve.tensor_scalar(row(dst), row(a), s1, s2, f1_, f2_))

            def stt(dst, a, s1, b, f1_, f2_):
                step(dve.scalar_tensor_tensor(out=row(dst), in0=row(a), scalar=s1, in1=row(b), op0=f1_, op1=f2_))

            def ask():
                dve.drain().then_inc(vec_asks, 1)
                asks[0] += 1
                dve.wait_ge(act_answers, asks[0])

            def rsq(dst):
                ask()
                tt(W3, W2_, W2_, ALU.mult)
                stt(W3, W3, -0.5, W0, ALU.mult, ALU.mult)
                stt(dst, W3, 1.5, W2_, ALU.add, ALU.mult)

            def log_map_factor(dst, xx):
                ts(W0, xx, EPS2, ALU.max)
                rsq(W4)
                tt(W5, W0, W4, ALU.mult)
                ts(W5, W5, MAX_ARG, ALU.min)
                ts(W6, W5, -1.0, ALU.mult, 1.0, ALU.add)
                step(dve.reciprocal(row(W6), row(W6)))
                stt(W7, W5, 1.0, W6, ALU.add, ALU.mult)
                ask()
                stt(W8, W8, 0.5, W4, ALU.mult, ALU.mult)
                tt(W9, W5, W5, ALU.mult)
                ts(W10, W9, 1.0 / 15, ALU.mult)
                for m in (13, 11, 9, 7, 5, 3):
                    stt(W10, W10, 1.0 / m, W9, ALU.add, ALU.mult)
                ts(W10, W10, 1.0, ALU.add)
                tt(W10, W10, W5, ALU.mult)
                tt(W10, W10, W4, ALU.mult)
                ts(W11, W5, SERIES_BELOW, ALU.is_lt)
                tt(W10, W10, W8, ALU.subtract)
                tt(W10, W10, W11, ALU.mult)
                tt(dst, W8, W10, ALU.add)

            def norm_factor(dst, s, var):
                tt(W0, s, s, ALU.mult)
                tt(W0, W0, var, ALU.mult)
                ts(W0, W0, LN_EPS, ALU.add)
                rsq(W4)
                tt(dst, s, W4, ALU.mult)

            dve.wait_ge(bn_done, T)
            part = lambda k: bn[:, :, k]
            add = lambda dst, a, b, f: step(dve.tensor_tensor(row(dst), a, b, f))
            add(MEAN, part(1), part(4), ALU.add)
            ts(MEAN, MEAN, 0.5, ALU.mult)
            add(W0, part(1), part(4), ALU.subtract)
            add(W1_, part(2), part(5), ALU.add)
            tt(W0, W0, W0, ALU.mult)
            stt(W0, W0, D / 4.0, W1_, ALU.mult, ALU.add)
            ts(VAR, W0, 1.0 / D, ALU.mult)
            tt(W1_, MEAN, MEAN, ALU.mult)
            stt(XX, W1_, float(D), W0, ALU.mult, ALU.add)
            ts(OMX, XX, -1.0, ALU.mult, 1.0, ALU.add)
            log_map_factor(W12, XX)
            norm_factor(R1, W12, VAR)

            dve.wait_ge(wqkv_in, 96)
            dve.wait_ge(rows_in, 48)
            dve.wait_ge(zeros_set, 4)
            dve.wait_ge(own_made, 4)
            dve.wait_ge(ada_stored, 80)

            def tile_of(big, i):
                return big[:, bass.ds(i, 1), :].rearrange("p a d -> p (a d)")

            def modulate(i, k, half):
                dve.wait_ge(mod_in[k], 16 * half + 16)
                after(dve, t_ready, i)
                dve.scalar_tensor_tensor(out=lnx[:, :], in0=tile_of(x_all, i), scalar=arrays[:, MEAN, bass.ds(i, 1)],
                                         in1=mod[:, k, D:2 * D], op0=ALU.subtract, op1=ALU.mult).then_inc(ln_half, 1)

            def shift_t(i, k):
                dve.wait_ge(ln_half, i + 1)
                after(dve, tT_psum, i)
                after(dve, t_squared, i)
                dve.scalar_tensor_tensor(out=t[:, :], in0=lnx[:, :], scalar=arrays[:, R1, bass.ds(i, 1)],
                                         in1=mod[:, k, 0:D], op0=ALU.mult, op1=ALU.add).then_inc(t_ready, 1)

            def clip_t(i, k):
                dve.wait_ge(rt_ready, i + 1)
                after(dve, u_ready, i - 1)
                dve.tensor_scalar(ct[:, k:k + 1], rt[:, k:k + 1], AM, 1.0, ALU.mult, ALU.min).then_inc(ct_ready, 1)

            def project(i, k):
                dve.wait_ge(qkv_psum, i + 1)
                dve.wait_ge(ct_ready, i + 1)
                after(dve, qk_ready, 2 * i - 2)
                after(dve, v_ready, i - 1)
                after(dve, u_squared, i - 1)
                dve.scalar_tensor_tensor(out=u[:, k, :], in0=p_qkv[:, 0:3 * D], scalar=ct[:, k:k + 1],
                                         in1=bqkv[:, :], op0=ALU.mult, op1=ALU.add).then_inc(u_ready, 1)

            def sum_squares(i):
                dve.wait_ge(u_squared, i + 1)
                after(dve, roots_ready, i)
                dve.tensor_reduce(hs[:, 0:3 * H], usq[:, :].rearrange("p (a d) -> p a d", d=HD), AX.X, ALU.add).then_inc(heads_summed, 1)

            def sum_rows(i):
                dve.wait_ge(heads_summed, i + 1)
                dve.tensor_reduce(hs[:, 3 * H:NF], hs[:, 0:3 * H].rearrange("p (a h) -> p a h", h=H), AX.X, ALU.add).then_inc(rows_summed, 1)

            def softmax_sums(i):
                dve.wait_ge(o_psum, i + 1)
                after(dve, o_ready, 2 * i)
                for c in range(2):
                    dve.reciprocal(rden[:, c * G:c * G + G, :], p_oh[:, c, :, :, HD]).then_inc(rden_ready, 1)

            def normalise(i):
                dve.wait_ge(rden_ready, 2 * i + 2)
                after(dve, oT_psum, i)
                for b in range(TB):
                    dve.tensor_tensor(o[:, b, :, :].rearrange("p (c g) d -> p c g d", c=2), p_oh[:, :, :, b, 0:HD],
                                      rden[:, :, b].rearrange("p (c g) -> p c g", c=2).unsqueeze(3).broadcast_to([S, 2, G, HD]),
                                      ALU.mult).then_inc(o_ready, 1)

            def add_bo(i):
                dve.wait_ge(z_psum, i + 1)
                after(dve, z_squared, i)
                after(dve, zg_ready, i)
                dve.tensor_tensor(z[:, :], p_oz[:, 0:D], bo[:, :], ALU.add).then_inc(z_ready, 1)

            def gate_z(i, k, half):
                dve.wait_ge(z_ready, i + 1)
                dve.wait_ge(gate_in[k], 16 * half + 16)
                after(dve, stats_kept, i)
                dve.scalar_tensor_tensor(out=tile_of(g_all, i), in0=z[:, :], scalar=1.0, in1=gate[:, k, :],
                                         op0=ALU.mult, op1=ALU.mult, accum_out=st[:, 1:2]).then_inc(zg_ready, 1)

            def dot_x(i):
                dve.wait_ge(zg_ready, i + 1)
                after(dve, xg_summed, i)
                dve.scalar_tensor_tensor(out=junk[:, 3, :], in0=tile_of(x_all, i), scalar=1.0, in1=tile_of(g_all, i),
                                         op0=ALU.mult, op1=ALU.mult, accum_out=st[:, 2:3]).then_inc(xg_summed, 1)

            def limit(i):
                dve.wait_ge(roots_ready, i + 1)
                after(dve, fac_ready, i)
                dve.tensor_tensor(rlim[:, :], roots[:, 3 * H:NF], c_lim[:, :], ALU.min).then_inc(rlim_ready, 1)

            def factors(i):
                dve.wait_ge(rlim_ready, i + 1)
                after(dve, qk_ready, 2 * i)
                after(dve, facv_ready, i)
                dve.tensor_tensor(fac[:, :].rearrange("p (a h) -> p a h", a=3),
                                  roots[:, 0:3 * H].rearrange("p (a h) -> p a h", a=3),
                                  rlim[:, :].unsqueeze(2).broadcast_to([P, 3, H]), ALU.min).then_inc(fac_ready, 1)

            def factors_v(i):
                dve.wait_ge(fac_ready, i + 1)
                after(dve, v_ready, i)
                dve.tensor_tensor(facv[:, :, :], fac[:, 2 * H:3 * H].unsqueeze(2).broadcast_to([P, H, TB]),
                                  own[:, :].unsqueeze(1).broadcast_to([P, H, TB]), ALU.mult).then_inc(facv_ready, 1)

            def scale_qk(i, k):
                dve.wait_ge(fac_ready, i + 1)
                after(dve, low_ready, i)
                for a in range(2):
                    part = slice(a * D, a * D + D)
                    dve.tensor_tensor(qk[:, part].rearrange("p (h d) -> p h d", d=HD), u[:, k, part].rearrange("p (h d) -> p h d", d=HD),
                                      fac[:, a * H:a * H + H].unsqueeze(2).broadcast_to([P, H, HD]), ALU.mult).then_inc(qk_ready, 1)

            def repeat_parts(i):
                dve.wait_ge(high_ready, i + 1)
                dve.wait_ge(low_ready, i + 1)
                after(dve, qkT_psum, i)
                q4, k4 = (qk4[:, a, :, :, :].rearrange("p h (y z) d -> p h y z d", y=2) for a in range(2))
                dve.tensor_copy(q4[:, :, :, 1, :], q4[:, :, :, 0, :]).then_inc(again_ready, 1)
                dve.tensor_copy(k4[:, :, 1, :, :], k4[:, :, 0, :, :]).then_inc(again_ready, 1)

            def slot(h, off):
                if on(h, off, L_D):
                    project(2 * h + off - L_D, (off - L_D) % 2)
                if on(h, off, L_E):
                    limit(2 * h + off - L_E)
                if on(h, off, L_L):
                    softmax_sums(2 * h + off - L_L)
                if on(h, off, L_E):
                    factors(2 * h + off - L_E)
                if on(h, off, L_L):
                    normalise(2 * h + off - L_L)
                if on(h, off, L_E):
                    factors_v(2 * h + off - L_E)
                    scale_qk(2 * h + off - L_E, (off - L_E) % 2)
                if on(h, off, L_A):
                    modulate(2 * h + off - L_A, (off - L_A) % 2, h + (off - L_A) // 2)
                if on(h, off, L_D):
                    sum_squares(2 * h + off - L_D)
                if on(h, off, L_A):
                    shift_t(2 * h + off - L_A, (off - L_A) % 2)
                if on(h, off, L_D):
                    sum_rows(2 * h + off - L_D)
                if on(h, off, L_L):
                    add_bo(2 * h + off - L_L)
                if on(h, off, L_E):
                    repeat_parts(2 * h + off - L_E)
                if on(h, off, L_L):
                    gate_z(2 * h + off - L_L, (off - L_L) % 2, h + (off - L_L) // 2)
                if on(h, off, L_C):
                    clip_t(2 * h + off - L_C, (off - L_C) % 2)
                if on(h, off, L_L):
                    dot_x(2 * h + off - L_L)

            run_tiles(dve, slot)

            dve.wait_ge(stats_kept, T)
            sm = lambda k: stats[:, :, k]
            step(dve.tensor_scalar(row(W0), sm(0), EPS2, None, ALU.max))
            rsq(W4)
            ts(W4, W4, AM, ALU.mult, 1.0, ALU.min)
            tt(W5, W4, W4, ALU.mult)
            add(W0, row(W5), sm(3), ALU.mult)
            ts(W0, W0, EPS2, ALU.max)
            rsq(W6)
            tt(W7, W0, W6, ALU.mult)
            ask()
            tt(W8, W8, W6, ALU.mult)
            tt(W9, W8, W4, ALU.mult)
            tt(W10, W9, W9, ALU.mult)
            add(W10, row(W10), sm(3), ALU.mult)
            add(W11, row(W9), sm(2), ALU.mult)
            ts(W11, W11, 2.0, ALU.mult, 1.0, ALU.add)
            tt(W12, XX, W10, ALU.mult)
            tt(W12, W12, W11, ALU.add)
            ts(W12, W12, EPS, ALU.max)
            step(dve.reciprocal(row(W12), row(W12)))
            tt(W13, W11, W10, ALU.add)
            tt(ALPHA, W13, W12, ALU.mult)
            tt(W13, OMX, W9, ALU.mult)
            tt(BETA, W13, W12, ALU.mult)
            step(dve.tensor_scalar(row(W9), sm(1), 1.0 / D, None, ALU.mult))
            tt(W10, W9, W9, ALU.mult)
            step(dve.scalar_tensor_tensor(out=row(W10), in0=sm(3), scalar=1.0 / D, in1=row(W10), op0=ALU.mult, op1=ALU.subtract))
            tt(W11, W9, MEAN, ALU.mult)
            step(dve.scalar_tensor_tensor(out=row(W11), in0=sm(2), scalar=1.0 / D, in1=row(W11), op0=ALU.mult, op1=ALU.subtract))
            tt(W12, ALPHA, MEAN, ALU.mult)
            tt(W13, BETA, W9, ALU.mult)
            tt(MEAN1, W12, W13, ALU.add)
            tt(W12, ALPHA, ALPHA, ALU.mult)
            tt(W13, ALPHA, BETA, ALU.mult)
            tt(W14, BETA, BETA, ALU.mult)
            tt(W9, W12, VAR, ALU.mult)
            tt(W10, W14, W10, ALU.mult)
            tt(W9, W9, W10, ALU.add)
            tt(W11, W13, W11, ALU.mult)
            stt(W9, W11, 2.0, W9, ALU.mult, ALU.add)
            ts(VAR, W9, 0.0, ALU.max)
            tt(W9, W12, XX, ALU.mult)
            add(W10, row(W14), sm(3), ALU.mult)
            tt(W9, W9, W10, ALU.add)
            add(W10, row(W13), sm(2), ALU.mult)
            stt(W9, W10, 2.0, W9, ALU.mult, ALU.add)
            ts(XX1, W9, 0.0, ALU.max)
            ts(OMX1, XX1, -1.0, ALU.mult, 1.0, ALU.add)
            log_map_factor(W12, XX1)
            norm_factor(R2, W12, VAR)
            dve.drain().then_inc(factors_made, 1)

            def first_sum(i, j):
                n = 2 * i + j
                dve.wait_ge(xa_ready, n + 1)
                g = tile_of(g_all, n)
                dve.scalar_tensor_tensor(out=g, in0=g, scalar=arrays[:, BETA, bass.ds(n, 1)], in1=xa[:, j, :],
                                         op0=ALU.mult, op1=ALU.add).then_inc(x1_ready, 1)

            def scale_t2(i, j):
                n = 2 * i + j
                dve.wait_ge(mod2_in, 16 * i + 16)
                dve.wait_ge(x1_ready, n + 1)
                after(dve, t2_ready, n - 1)
                dve.scalar_tensor_tensor(out=lnx2[j][:, :], in0=tile_of(g_all, n), scalar=arrays[:, MEAN1, bass.ds(n, 1)],
                                         in1=mod[:, j, D:2 * D], op0=ALU.subtract, op1=ALU.mult).then_inc(ln2_half, 1)

            def shift_t2(i, j, k):
                n = 2 * i + j
                dve.wait_ge(ln2_half, n + 1)
                after(dve, t2T_psum, i - 1)
                after(dve, t2_squared, n - 3)
                after(dve, qf_ready, n - 3)
                dve.scalar_tensor_tensor(out=t2[:, k, j, :], in0=lnx2[j][:, :], scalar=arrays[:, R2, bass.ds(n, 1)],
                                         in1=mod[:, j, 0:D], op0=ALU.mult, op1=ALU.add).then_inc(t2_ready, 1)

            def inner_square(i, j, k):
                n = 2 * i + j
                dve.wait_ge(ff_psum, n + 1)
                after(dve, qf_ready, n - 1)
                after(dve, hh_half, n - 1)
                dve.scalar_tensor_tensor(out=junk2[:, 3, j, :], in0=(p_qkv, p_s)[k][:, 512 * j + D:512 * j + 2 * D], scalar=1.0,
                                         in1=t2[:, k, j, :], op0=ALU.mult, op1=ALU.mult,
                                         accum_out=qf[:, j:j + 1]).then_inc(qf_ready, 1)

            def clip_t2(i, k):
                dve.wait_ge(rt2_ready, i + 1)
                after(dve, ca_ready, i - 1)
                dve.tensor_scalar(ct2[:, k, :], rt2[:, :], AM, 1.0, ALU.mult, ALU.min).then_inc(ct2_ready, 1)

            def inner_norm_1(i, j, k):
                dve.wait_ge(ct2_ready, i + 1)
                dve.wait_ge(qf_ready, 2 * i + j + 1)
                after(dve, hh_scaled, i)
                dve.scalar_tensor_tensor(out=hh[:, 0, j:j + 1], in0=qf[:, j:j + 1], scalar=ct2[:, k, j:j + 1],
                                         in1=s_bank[2 + k][:, j:j + 1], op0=ALU.mult, op1=ALU.add).then_inc(hh_half, 1)

            def inner_norm_2(i, k):
                dve.wait_ge(hh_half, 2 * i + 2)
                after(dve, hh_ready, i)
                dve.tensor_tensor(hh[:, 2, :], hh[:, 0, :], ct2[:, k, :], ALU.mult).then_inc(hh_scaled, 1)

            def inner_norm_3(i):
                dve.wait_ge(hh_scaled, i + 1)
                after(dve, rh_ready, i)
                dve.tensor_scalar(hh[:, 1, :], hh[:, 2, :], bb[:, 0:1], None, ALU.add).then_inc(hh_ready, 1)

            def inner_factors(i):
                dve.wait_ge(rh_ready, i + 1)
                after(dve, ff_ready, 2 * i)
                after(dve, ca_ready, i)
                dve.tensor_scalar(ch[:, :], rh[:, :], AM, 1.0, ALU.mult, ALU.min).then_inc(ch_ready, 1)

            def inner_product(i, k):
                dve.wait_ge(ch_ready, i + 1)
                dve.tensor_tensor(ca[:, :], ch[:, :], ct2[:, k, :], ALU.mult).then_inc(ca_ready, 1)

            def mlp_half(i, j, k):
                n = 2 * i + j
                dve.wait_ge(ca_ready, i + 1)
                after(dve, ff_ready, n - 1)
                dve.scalar_tensor_tensor(out=f1[:, j, :], in0=(p_qkv, p_s)[k][:, 512 * j:512 * j + D], scalar=ca[:, j:j + 1],
                                         in1=b2[:, :], op0=ALU.mult, op1=ALU.add).then_inc(f1_ready, 1)

            def mlp_output(i, j):
                n = 2 * i + j
                dve.wait_ge(f1_ready, n + 1)
                after(dve, ff_squared, n - 1)
                after(dve, fg_ready, n - 1)
                dve.scalar_tensor_tensor(out=ff[:, j, :], in0=b12[:, :], scalar=ch[:, j:j + 1], in1=f1[:, j, :],
                                         op0=ALU.mult, op1=ALU.add).then_inc(ff_ready, 1)

            def gate_mlp(i, j, k, half):
                n = 2 * i + j
                dve.wait_ge(ff_ready, n + 1)
                dve.wait_ge(gate2_in[k], 16 * half + 16)
                after(dve, yo_ready, n - 3)
                after(dve, xf_summed, n - 3)
                after(dve, fg_squared, n - 3)
                dve.tensor_tensor(fgs[k][:, j, :], ff[:, j, :], gates2[k][:, j, :], ALU.mult).then_inc(fg_ready, 1)

            def dot_x1(i, j, k):
                n = 2 * i + j
                dve.wait_ge(fg_ready, n + 1)
                after(dve, xf_summed, n - 1)
                after(dve, parts_ready, 3 * (i - 1))
                dve.scalar_tensor_tensor(out=junk[:, j, :], in0=tile_of(g_all, n), scalar=1.0, in1=fgs[k][:, j, :],
                                         op0=ALU.mult, op1=ALU.mult, accum_out=fst[:, k, 2, j:j + 1]).then_inc(xf_summed, 1)

            def output_clip(i):
                dve.wait_ge(rf_ready, i + 1)
                after(dve, parts_ready, 3 * i)
                dve.tensor_scalar(cf[:, :], rf[:, :], AM, 1.0, ALU.mult, ALU.min).then_inc(cf_ready, 1)

            def sum_factors(i):
                dve.wait_ge(parts_ready, 3 * i + 3)
                dve.wait_ge(fin_step, FIN_STEPS * i + FIN_STEPS)
                after(dve, al2_ready, i)
                after(dve, be2_ready, i)
                dve.tensor_tensor(den[:, 0, :], parts[:, 0, :], fin[:, 10, :], ALU.add).then_inc(den_step, 1)

            def clip_den(i):
                dve.wait_ge(den_step, 3 * i + 1)
                dve.tensor_scalar(den[:, 1, :], den[:, 0, :], EPS, None, ALU.max).then_inc(den_step, 1)

            def invert_den(i):
                dve.wait_ge(den_step, 3 * i + 2)
                dve.reciprocal(den[:, 2, :], den[:, 1, :]).then_inc(den_step, 1)

            def finish_factors(i):
                dve.wait_ge(den_step, 3 * i + 3)
                after(dve, xo_ready, 2 * i)
                after(dve, yo_ready, 2 * i)
                dve.tensor_tensor(al2[:, :], parts[:, 1, :], den[:, 2, :], ALU.mult).then_inc(al2_ready, 1)
                dve.tensor_tensor(be2[:, :], parts[:, 2, :], den[:, 2, :], ALU.mult).then_inc(be2_ready, 1)

            def second_sum(i, j, k):
                n = 2 * i + j
                dve.wait_ge(be2_ready, i + 1)
                dve.wait_ge(xo_ready, n + 1)
                after(dve, out_ready, n - 1)
                dve.scalar_tensor_tensor(out=yo[:, j, :], in0=fgs[k][:, j, :], scalar=be2[:, j:j + 1], in1=xo[:, j, :],
                                         op0=ALU.mult, op1=ALU.add).then_inc(yo_ready, 1)

            def slot2(h, off):
                slots = 2 * h + off
                if on2(h, off, M_O):
                    sum_factors(slots - M_O)
                if on2(h, off, M_A):
                    first_sum(slots - M_A, 0)
                if on2(h, off, M_O):
                    clip_den(slots - M_O)
                if on2(h, off, M_A):
                    first_sum(slots - M_A, 1)
                if on2(h, off, M_O):
                    invert_den(slots - M_O)
                if on2(h, off, M_A):
                    scale_t2(slots - M_A, 0)
                if on2(h, off, M_O):
                    finish_factors(slots - M_O)
                if on2(h, off, M_A):
                    scale_t2(slots - M_A, 1)
                if on2(h, off, M_C):
                    output_clip(slots - M_C)
                if on2(h, off, M_A):
                    shift_t2(slots - M_A, 0, (off - M_A) % 2)
                    shift_t2(slots - M_A, 1, (off - M_A) % 2)
                if on2(h, off, M_B):
                    inner_factors(slots - M_B)
                if on2(h, off, M_O):
                    second_sum(slots - M_O, 0, (off - M_O) % 2)
                if on2(h, off, M_B):
                    inner_product(slots - M_B, (off - M_B) % 2)
                if on2(h, off, M_O):
                    second_sum(slots - M_O, 1, (off - M_O) % 2)
                if on2(h, off, M_B):
                    mlp_half(slots - M_B, 0, (off - M_B) % 2)
                    mlp_half(slots - M_B, 1, (off - M_B) % 2)
                    mlp_output(slots - M_B, 0)
                    mlp_output(slots - M_B, 1)
                if on2(h, off, M_Q):
                    clip_t2(slots - M_Q, (off - M_Q) % 2)
                    inner_square(slots - M_Q, 0, (off - M_Q) % 2)
                if on2(h, off, M_B):
                    gate_mlp(slots - M_B, 0, (off - M_B) % 2, h + (off - M_B) // 2)
                    gate_mlp(slots - M_B, 1, (off - M_B) % 2, h + (off - M_B) // 2)
                if on2(h, off, M_Q):
                    inner_square(slots - M_Q, 1, (off - M_Q) % 2)
                    inner_norm_1(slots - M_Q, 0, (off - M_Q) % 2)
                if on2(h, off, M_B):
                    dot_x1(slots - M_B, 0, (off - M_B) % 2)
                if on2(h, off, M_Q):
                    inner_norm_1(slots - M_Q, 1, (off - M_Q) % 2)
                    inner_norm_2(slots - M_Q, (off - M_Q) % 2)
                if on2(h, off, M_B):
                    dot_x1(slots - M_B, 1, (off - M_B) % 2)
                if on2(h, off, M_Q):
                    inner_norm_3(slots - M_Q)

            run_pairs(dve, slot2)


_WEIGHTS = ["w_q", "b_q", "w_k", "b_k", "w_v", "b_v", "w_o", "b_o", "w_f1", "b_f1", "w_f2", "b_f2", "w_ada", "b_ada"]
_INS = ["x", "cond_1024"] + ["L0_cond_" + n for n in _WEIGHTS]


def kernel(**inputs):
    import concourse.bacc as bacc
    from concourse.bass_utils import run_bass_kernel_spmd

    nc = bacc.Bacc("TRN2", target_bir_lowering=False, num_devices=1)
    arrays, args = {}, []
    for name in _INS:
        a = np.ascontiguousarray(inputs[name])
        arrays[f"in_{name}"] = a
        args.append(nc.dram_tensor(f"in_{name}", a.shape, mybir.dt.from_np(a.dtype), kind="ExternalInput").ap())
    out = nc.dram_tensor("out", inputs["x"].shape, F32, kind="ExternalOutput").ap()
    build(nc, *args, out)
    r = run_bass_kernel_spmd(nc, [arrays], core_ids=[0])
    return r.results[0]["out"]
```
